# Optimizing a Trainium2 kernel written in Bass

```python
import numpy as np
import jax
import jax.numpy as jnp

def _softmax(x, axis=-1):
    return jax.nn.softmax(x, axis=axis)

def _gelu(x):
    return jax.nn.gelu(x, approximate=True)

def _silu(x):
    return jax.nn.silu(x)

def _sigmoid(x):
    return jax.nn.sigmoid(x)

def _layernorm(x, axis=-1, eps=1e-05):
    m = jnp.mean(x, axis=axis, keepdims=True)
    v = jnp.var(x, axis=axis, keepdims=True)
    return (x - m) / jnp.sqrt(v + eps)

def _scatter_add(tgt, idx, src, axis=0):
    return tgt.at[idx].add(src)

def _segment_sum(src, seg, n):
    return jax.ops.segment_sum(src, seg, n)
kernel_name = 'mk_gnn_preln_d4_gnn_r64_727fd5'

def setup_inputs(seed: int=0):
    np.random.seed(seed)
    _w = jnp.asarray

    def _rec_inputs():
        import jax
        import jax.numpy as jnp
        _gk = jax.random.key(seed)
        x = -1.686e-05 + 1 * jax.random.normal(jax.random.fold_in(_gk, 1), (50000, 160), jnp.float32)
        src = jax.random.randint(jax.random.fold_in(_gk, 2), (25000,), 0, 50000, jnp.int32)
        dst = jnp.minimum((50000 * jax.random.uniform(jax.random.fold_in(_gk, 3), (25000,)) ** 2.0).astype(jnp.int32), 49999)
        _o = jnp.argsort(dst, stable=True)
        src = src[_o]
        dst = dst[_o]
        edge_attr_12 = jax.random.uniform(jax.random.fold_in(_gk, 12), (25000, 12), jnp.float32, 0.0, 1)
        edge_attr_16 = -0.000191324 + 0.999809 * jax.random.normal(jax.random.fold_in(_gk, 13), (25000, 16), jnp.float32)
        edge_attr_32 = 0.000196303 + 1.00016 * jax.random.normal(jax.random.fold_in(_gk, 14), (25000, 32), jnp.float32)
        edge_attr_4 = 0.000126197 + 0.999763 * jax.random.normal(jax.random.fold_in(_gk, 15), (25000, 4), jnp.float32)
        node_vec1 = -0.00915711 + 0.999674 * jax.random.normal(jax.random.fold_in(_gk, 17), (50000, 1), jnp.float32)
        return (x, src, dst, edge_attr_12, edge_attr_16, edge_attr_32, edge_attr_4, node_vec1)
    x, src, dst, edge_attr_12, edge_attr_16, edge_attr_32, edge_attr_4, node_vec1 = _rec_inputs()

    def _L0_gnn_setup():
        import jax, jax.numpy as jnp
        import numpy as np
        MUL0_N, MUL1_N = (64, 32)
        MUL0_E, MUL1_E = (8, 8)
        MUL0_H, MUL1_H = (64, 32)
        N_NODES, N_EDGES = (50000, 12500)
        D_NODE = MUL0_N + 3 * MUL1_N
        D_EDGE = MUL0_E + 3 * MUL1_E
        D_HID = MUL0_H + 3 * MUL1_H

        def _split(x, mul0, mul1):
            s = x[..., :mul0]
            v = x[..., mul0:].reshape(x.shape[0], mul1, 3)
            return (s, v)

        def fctp_messages(x, e, W1, W2, W3, W4):
            xs, xv = _split(x, MUL0_N, MUL1_N)
            es, ev = _split(e, MUL0_E, MUL1_E)
            inv_sqrt2 = 1.0 / np.sqrt(2.0)
            s1 = jnp.einsum('ea,eb,abc->ec', xs, es, W1) * (1.0 / np.sqrt(MUL0_N * MUL0_E))
            s2 = jnp.einsum('eai,ebi,abc->ec', xv, ev, W2) * (1.0 / (np.sqrt(3.0) * np.sqrt(MUL1_N * MUL1_E)))
            out_s = (s1 + s2) * inv_sqrt2
            v1 = jnp.einsum('ea,ebi,abc->eci', xs, ev, W3) * (1.0 / np.sqrt(MUL0_N * MUL1_E))
            v2 = jnp.einsum('eai,eb,abc->eci', xv, es, W4) * (1.0 / np.sqrt(MUL1_N * MUL0_E))
            out_v = (v1 + v2) * inv_sqrt2
            return jnp.concatenate([out_s, out_v.reshape(out_v.shape[0], -1)], axis=-1)
        key = jax.random.key(seed)
        ks = jax.random.split(key, 12)
        node_features = jax.random.normal(ks[0], (N_NODES, D_NODE), dtype=jnp.float32)
        edge_index = jax.random.randint(ks[1], (2, N_EDGES), 0, N_NODES, dtype=jnp.int64)
        edge_attr_tensor = jax.random.normal(ks[2], (N_EDGES, D_EDGE), dtype=jnp.float32)
        node_attr_scalar_raw = jax.random.normal(ks[3], (N_NODES, 1), dtype=jnp.float32)
        W1 = jax.random.normal(ks[4], (MUL0_N, MUL0_E, MUL0_H), dtype=jnp.float32)
        W2 = jax.random.normal(ks[5], (MUL1_N, MUL1_E, MUL0_H), dtype=jnp.float32)
        W3 = jax.random.normal(ks[6], (MUL0_N, MUL1_E, MUL1_H), dtype=jnp.float32)
        W4 = jax.random.normal(ks[7], (MUL1_N, MUL0_E, MUL1_H), dtype=jnp.float32)
        Wm = jax.random.normal(ks[8], (D_HID, D_HID), dtype=jnp.float32) / np.sqrt(D_HID)
        bm = jnp.zeros((D_HID,), dtype=jnp.float32)
        Wu = jax.random.normal(ks[9], (D_NODE + D_HID, D_NODE), dtype=jnp.float32) / np.sqrt(D_NODE + D_HID)
        bu = jnp.zeros((D_NODE,), dtype=jnp.float32)
        return {'node_features': node_features, 'edge_index': edge_index, 'edge_attr_tensor': edge_attr_tensor, 'node_attr_scalar_raw': node_attr_scalar_raw, 'W1': W1, 'W2': W2, 'W3': W3, 'W4': W4, 'Wm': Wm, 'bm': bm, 'Wu': Wu, 'bu': bu}
    _L0_gnn_all = _L0_gnn_setup()
    _L0_gnn_in = {k: v for k, v in _L0_gnn_all.items() if k in ('W1', 'W2', 'W3', 'W4', 'Wm', 'bm', 'Wu', 'bu')}
    del _L0_gnn_all

    def _L1_gnn_setup():
        import jax, jax.numpy as jnp
        import numpy as np
        N = 20000
        E = 5000
        MUL0 = 64
        MUL1 = 32
        FC_IN = 16
        FC_H = 64
        WNUM = 192
        key = jax.random.key(seed)
        ks = jax.random.split(key, 16)
        return {'x': jax.random.normal(ks[0], (N, MUL0 + 3 * MUL1), jnp.float32), 'node_attr': jnp.ones((N, 1), jnp.float32), 'edge_scalars': jax.random.normal(ks[1], (E, FC_IN), jnp.float32), 'edge_attr_sh': jax.random.normal(ks[2], (E, 4), jnp.float32), 'edge_src': jax.random.randint(ks[3], (E,), 0, N), 'edge_dst': jax.random.randint(ks[4], (E,), 0, N), 'Wfc1': jax.random.normal(ks[5], (FC_IN, FC_H), jnp.float32), 'Wfc2': jax.random.normal(ks[6], (FC_H, WNUM), jnp.float32), 'Wsc0': jax.random.normal(ks[7], (MUL0, MUL0), jnp.float32), 'Wsc1': jax.random.normal(ks[8], (MUL1, MUL1), jnp.float32), 'Wl1_0': jax.random.normal(ks[9], (MUL0, MUL0), jnp.float32), 'Wl1_1': jax.random.normal(ks[10], (MUL1, MUL1), jnp.float32), 'Wl2_s': jax.random.normal(ks[11], (MUL0 + MUL1, MUL0), jnp.float32), 'Wl2_v': jax.random.normal(ks[12], (MUL0 + MUL1, MUL1), jnp.float32), 'Wa': 0.1 * jax.random.normal(ks[13], (MUL0 + MUL1, 1), jnp.float32)}
    _L1_gnn_all = _L1_gnn_setup()
    _L1_gnn_in = {k: v for k, v in _L1_gnn_all.items() if k in ('Wfc1', 'Wfc2', 'Wsc0', 'Wsc1', 'Wl1_0', 'Wl1_1', 'Wl2_s', 'Wl2_v', 'Wa')}
    del _L1_gnn_all

    def _L2_gnn_setup():
        import jax, jax.numpy as jnp
        import numpy as np
        N = 50000
        E = 6250
        MUL0 = 64
        MUL1 = 32
        NEF = 12
        RN = 100
        NUM_NEIGHBORS = 8.0
        WNUM = MUL0 + MUL0 + MUL1 + MUL1

        def _split(x):
            return (x[:, :MUL0], x[:, MUL0:].reshape(-1, MUL1, 3))

        def _fctp_scalar_attr(x0, x1, z, Ws, Wv):
            s = x0 @ Ws * z / np.sqrt(Ws.shape[0])
            v = jnp.einsum('nuc,uw->nwc', x1, Wv) * z[:, :, None] / np.sqrt(Wv.shape[0])
            return (s, v)
        key = jax.random.key(seed)
        ks = jax.random.split(key, 16)
        return {'node_input': jax.random.normal(ks[0], (N, MUL0 + 3 * MUL1), jnp.float32), 'node_attr': jax.random.uniform(ks[1], (N, 1), dtype=jnp.float32), 'edge_src': jax.random.randint(ks[2], (E,), 0, N), 'edge_dst': jax.random.randint(ks[3], (E,), 0, N), 'edge_attr': jax.random.normal(ks[4], (E, 4), jnp.float32), 'edge_features': jax.random.uniform(ks[5], (E, NEF), dtype=jnp.float32), 'W_sc0': jax.random.normal(ks[6], (MUL0, MUL0), jnp.float32), 'W_sc1': jax.random.normal(ks[7], (MUL1, MUL1), jnp.float32), 'W_l1_0': jax.random.normal(ks[8], (MUL0, MUL0), jnp.float32), 'W_l1_1': jax.random.normal(ks[9], (MUL1, MUL1), jnp.float32), 'W_fc1': jax.random.normal(ks[10], (NEF, RN), jnp.float32), 'W_fc2': jax.random.normal(ks[11], (RN, WNUM), jnp.float32), 'W_l2_0': jax.random.normal(ks[12], (MUL0 + MUL1, MUL0), jnp.float32), 'W_l2_1': jax.random.normal(ks[13], (MUL0 + MUL1, MUL1), jnp.float32)}
    _L2_gnn_all = _L2_gnn_setup()
    _L2_gnn_in = {k: v for k, v in _L2_gnn_all.items() if k in ('W_sc0', 'W_sc1', 'W_l1_0', 'W_l1_1', 'W_fc1', 'W_fc2', 'W_l2_0', 'W_l2_1')}
    del _L2_gnn_all

    def _L3_gnn_setup():
        import jax, jax.numpy as jnp
        import numpy as np
        N = 20000
        E = 10000
        INV_SQRT3 = 0.5773502691896258
        INV8 = 0.125
        INV_SQRT32 = 0.17677669529663687
        INV64 = 0.015625
        INV32 = 0.03125
        INV_SQRT2048 = 0.022097086912079608
        key = jax.random.key(seed)
        ks = jax.random.split(key, 16)
        f32 = jnp.float32
        return {'node_features': jax.random.normal(ks[0], (N, 160), f32), 'edge_index': jax.random.randint(ks[1], (2, E), 0, N), 'edge_attr_tensor': jax.random.normal(ks[2], (E, 4), f32), 'node_attr_scalar_raw': jax.random.normal(ks[3], (N, 1), f32), 'Wm_ss': jax.random.normal(ks[4], (64, 64), f32), 'Wm_vv': jax.random.normal(ks[5], (32, 64), f32), 'Wm_sv': jax.random.normal(ks[6], (64, 32), f32), 'Wm_vs': jax.random.normal(ks[7], (32, 32), f32), 'Lm_s': jax.random.normal(ks[8], (64, 64), f32), 'Lm_v': jax.random.normal(ks[9], (32, 32), f32), 'Wu_ss': jax.random.normal(ks[10], (64, 64, 64), f32), 'Wu_vv': jax.random.normal(ks[11], (32, 32, 64), f32), 'Wu_sv': jax.random.normal(ks[12], (64, 32, 32), f32), 'Wu_vs': jax.random.normal(ks[13], (32, 64, 32), f32), 'Lu_s': jax.random.normal(ks[14], (64, 64), f32), 'Lu_v': jax.random.normal(ks[15], (32, 32), f32)}
    _L3_gnn_all = _L3_gnn_setup()
    _L3_gnn_in = {k: v for k, v in _L3_gnn_all.items() if k in ('Wm_ss', 'Wm_vv', 'Wm_sv', 'Wm_vs', 'Lm_s', 'Lm_v', 'Wu_ss', 'Wu_vv', 'Wu_sv', 'Wu_vs', 'Lu_s', 'Lu_v')}
    del _L3_gnn_all
    return {'x': x, 'src': src, 'dst': dst, 'edge_attr_12': edge_attr_12, 'edge_attr_16': edge_attr_16, 'edge_attr_32': edge_attr_32, 'edge_attr_4': edge_attr_4, 'node_vec1': node_vec1, 'L0_gnn_W1': _L0_gnn_in['W1'], 'L0_gnn_W2': _L0_gnn_in['W2'], 'L0_gnn_W3': _L0_gnn_in['W3'], 'L0_gnn_W4': _L0_gnn_in['W4'], 'L0_gnn_Wm': _L0_gnn_in['Wm'], 'L0_gnn_bm': _L0_gnn_in['bm'], 'L0_gnn_Wu': _L0_gnn_in['Wu'], 'L0_gnn_bu': _L0_gnn_in['bu'], 'L1_gnn_Wfc1': _L1_gnn_in['Wfc1'], 'L1_gnn_Wfc2': _L1_gnn_in['Wfc2'], 'L1_gnn_Wsc0': _L1_gnn_in['Wsc0'], 'L1_gnn_Wsc1': _L1_gnn_in['Wsc1'], 'L1_gnn_Wl1_0': _L1_gnn_in['Wl1_0'], 'L1_gnn_Wl1_1': _L1_gnn_in['Wl1_1'], 'L1_gnn_Wl2_s': _L1_gnn_in['Wl2_s'], 'L1_gnn_Wl2_v': _L1_gnn_in['Wl2_v'], 'L1_gnn_Wa': _L1_gnn_in['Wa'], 'L2_gnn_W_sc0': _L2_gnn_in['W_sc0'], 'L2_gnn_W_sc1': _L2_gnn_in['W_sc1'], 'L2_gnn_W_l1_0': _L2_gnn_in['W_l1_0'], 'L2_gnn_W_l1_1': _L2_gnn_in['W_l1_1'], 'L2_gnn_W_fc1': _L2_gnn_in['W_fc1'], 'L2_gnn_W_fc2': _L2_gnn_in['W_fc2'], 'L2_gnn_W_l2_0': _L2_gnn_in['W_l2_0'], 'L2_gnn_W_l2_1': _L2_gnn_in['W_l2_1'], 'L3_gnn_Wm_ss': _L3_gnn_in['Wm_ss'], 'L3_gnn_Wm_vv': _L3_gnn_in['Wm_vv'], 'L3_gnn_Wm_sv': _L3_gnn_in['Wm_sv'], 'L3_gnn_Wm_vs': _L3_gnn_in['Wm_vs'], 'L3_gnn_Lm_s': _L3_gnn_in['Lm_s'], 'L3_gnn_Lm_v': _L3_gnn_in['Lm_v'], 'L3_gnn_Wu_ss': _L3_gnn_in['Wu_ss'], 'L3_gnn_Wu_vv': _L3_gnn_in['Wu_vv'], 'L3_gnn_Wu_sv': _L3_gnn_in['Wu_sv'], 'L3_gnn_Wu_vs': _L3_gnn_in['Wu_vs'], 'L3_gnn_Lu_s': _L3_gnn_in['Lu_s'], 'L3_gnn_Lu_v': _L3_gnn_in['Lu_v']}

def reference(x, src, dst, edge_attr_12, edge_attr_16, edge_attr_32, edge_attr_4, node_vec1, L0_gnn_W1, L0_gnn_W2, L0_gnn_W3, L0_gnn_W4, L0_gnn_Wm, L0_gnn_bm, L0_gnn_Wu, L0_gnn_bu, L1_gnn_Wfc1, L1_gnn_Wfc2, L1_gnn_Wsc0, L1_gnn_Wsc1, L1_gnn_Wl1_0, L1_gnn_Wl1_1, L1_gnn_Wl2_s, L1_gnn_Wl2_v, L1_gnn_Wa, L2_gnn_W_sc0, L2_gnn_W_sc1, L2_gnn_W_l1_0, L2_gnn_W_l1_1, L2_gnn_W_fc1, L2_gnn_W_fc2, L2_gnn_W_l2_0, L2_gnn_W_l2_1, L3_gnn_Wm_ss, L3_gnn_Wm_vv, L3_gnn_Wm_sv, L3_gnn_Wm_vs, L3_gnn_Lm_s, L3_gnn_Lm_v, L3_gnn_Wu_ss, L3_gnn_Wu_vv, L3_gnn_Wu_sv, L3_gnn_Wu_vs, L3_gnn_Lu_s, L3_gnn_Lu_v):
    import jax
    import jax.numpy as jnp

    def _L0_gnn_ref(node_features, edge_index, edge_attr_tensor, node_attr_scalar_raw, W1, W2, W3, W4, Wm, bm, Wu, bu):
        import jax, jax.numpy as jnp
        import numpy as np
        MUL0_N, MUL1_N = (64, 32)
        MUL0_E, MUL1_E = (8, 8)
        MUL0_H, MUL1_H = (64, 32)
        N_NODES, N_EDGES = (50000, 12500)
        D_NODE = MUL0_N + 3 * MUL1_N
        D_EDGE = MUL0_E + 3 * MUL1_E
        D_HID = MUL0_H + 3 * MUL1_H

        def _split(x, mul0, mul1):
            s = x[..., :mul0]
            v = x[..., mul0:].reshape(x.shape[0], mul1, 3)
            return (s, v)

        def fctp_messages(x, e, W1, W2, W3, W4):
            xs, xv = _split(x, MUL0_N, MUL1_N)
            es, ev = _split(e, MUL0_E, MUL1_E)
            inv_sqrt2 = 1.0 / np.sqrt(2.0)
            s1 = jnp.einsum('ea,eb,abc->ec', xs, es, W1) * (1.0 / np.sqrt(MUL0_N * MUL0_E))
            s2 = jnp.einsum('eai,ebi,abc->ec', xv, ev, W2) * (1.0 / (np.sqrt(3.0) * np.sqrt(MUL1_N * MUL1_E)))
            out_s = (s1 + s2) * inv_sqrt2
            v1 = jnp.einsum('ea,ebi,abc->eci', xs, ev, W3) * (1.0 / np.sqrt(MUL0_N * MUL1_E))
            v2 = jnp.einsum('eai,eb,abc->eci', xv, es, W4) * (1.0 / np.sqrt(MUL1_N * MUL0_E))
            out_v = (v1 + v2) * inv_sqrt2
            return jnp.concatenate([out_s, out_v.reshape(out_v.shape[0], -1)], axis=-1)
        row, col = (edge_index[0], edge_index[1])
        tp = fctp_messages(node_features[col], edge_attr_tensor, W1, W2, W3, W4)
        messages = tp @ Wm + bm
        agg = jax.ops.segment_sum(messages, row, num_segments=N_NODES)
        upd = jnp.concatenate([node_features, agg], axis=-1) @ Wu + bu
        return node_features + upd

    def _L1_gnn_ref(x, node_attr, edge_scalars, edge_attr_sh, edge_src, edge_dst, Wfc1, Wfc2, Wsc0, Wsc1, Wl1_0, Wl1_1, Wl2_s, Wl2_v, Wa):
        import jax, jax.numpy as jnp
        import numpy as np
        N = 20000
        E = 5000
        MUL0 = 64
        MUL1 = 32
        FC_IN = 16
        FC_H = 64
        WNUM = 192
        n = x.shape[0]
        x0 = x[:, :MUL0]
        x1 = x[:, MUL0:].reshape(n, MUL1, 3)
        a = node_attr
        h = jax.nn.silu(edge_scalars @ (Wfc1 / jnp.sqrt(jnp.float32(FC_IN))))
        w = h @ (Wfc2 / jnp.sqrt(jnp.float32(FC_H)))
        w0 = w[:, :64]
        w1 = w[:, 64:128]
        w2 = w[:, 128:160]
        w3 = w[:, 160:192]
        inv8 = 1.0 / jnp.sqrt(jnp.float32(MUL0))
        inv32 = 1.0 / jnp.sqrt(jnp.float32(MUL1))
        sc = jnp.concatenate([x0 @ Wsc0 * a * inv8, (jnp.einsum('num,uv->nvm', x1, Wsc1) * a[..., None] * inv32).reshape(n, 3 * MUL1)], axis=1)
        f0 = x0 @ Wl1_0 * a * inv8
        f1 = jnp.einsum('num,uv->nvm', x1, Wl1_1) * a[..., None] * inv32
        e0 = f0[edge_src]
        e1 = f1[edge_src]
        sh0 = edge_attr_sh[:, :1]
        sh1 = edge_attr_sh[:, 1:4]
        mid0 = w0 * e0 * sh0
        mid1 = w3 * jnp.einsum('eum,em->eu', e1, sh1) / jnp.sqrt(3.0)
        mid2 = w1[:, :, None] * e0[:, :, None] * sh1[:, None, :]
        mid3 = w2[:, :, None] * e1 * sh0[:, :, None]
        cnt = jnp.clip(jax.ops.segment_sum(jnp.ones(edge_dst.shape, x.dtype), edge_dst, num_segments=n), 1.0)

        def smean(v):
            s = jax.ops.segment_sum(v, edge_dst, num_segments=n)
            return s / cnt.reshape((n,) + (1,) * (v.ndim - 1))
        n0, n1 = (smean(mid0), smean(mid1))
        n2, n3 = (smean(mid2), smean(mid3))
        scal = jnp.concatenate([n0, n1], axis=1)
        vec = jnp.concatenate([n2, n3], axis=1)
        inv96 = 1.0 / jnp.sqrt(jnp.float32(MUL0 + MUL1))
        alpha = scal @ Wa * a * inv96
        out_s = scal @ Wl2_s * a * inv96
        out_v = jnp.einsum('num,uv->nvm', vec, Wl2_v) * a[..., None] * inv96
        conv = jnp.concatenate([out_s, out_v.reshape(n, 3 * MUL1)], axis=1)
        return sc + alpha * conv

    def _L2_gnn_ref(node_input, node_attr, edge_src, edge_dst, edge_attr, edge_features, W_sc0, W_sc1, W_l1_0, W_l1_1, W_fc1, W_fc2, W_l2_0, W_l2_1):
        import jax, jax.numpy as jnp
        import numpy as np
        N = 50000
        E = 6250
        MUL0 = 64
        MUL1 = 32
        NEF = 12
        RN = 100
        NUM_NEIGHBORS = 8.0
        WNUM = MUL0 + MUL0 + MUL1 + MUL1

        def _split(x):
            return (x[:, :MUL0], x[:, MUL0:].reshape(-1, MUL1, 3))

        def _fctp_scalar_attr(x0, x1, z, Ws, Wv):
            s = x0 @ Ws * z / np.sqrt(Ws.shape[0])
            v = jnp.einsum('nuc,uw->nwc', x1, Wv) * z[:, :, None] / np.sqrt(Wv.shape[0])
            return (s, v)
        x0, x1 = _split(node_input)
        z = node_attr
        s0, s1 = _fctp_scalar_attr(x0, x1, z, W_sc0, W_sc1)
        h0, h1 = _fctp_scalar_attr(x0, x1, z, W_l1_0, W_l1_1)
        h = jax.nn.silu(edge_features @ W_fc1 / np.sqrt(NEF))
        w = h @ W_fc2 / np.sqrt(RN)
        w0 = w[:, :MUL0]
        w1 = w[:, MUL0:2 * MUL0]
        w2 = w[:, 2 * MUL0:2 * MUL0 + MUL1]
        w3 = w[:, 2 * MUL0 + MUL1:]
        e0 = h0[edge_src]
        e1 = h1[edge_src]
        y0 = edge_attr[:, :1]
        y1 = edge_attr[:, 1:]
        m0a = w0 * e0 * y0
        m0b = w3 * jnp.einsum('eui,ei->eu', e1, y1) / np.sqrt(3.0)
        m1a = (w1 * e0)[:, :, None] * y1[:, None, :]
        m1b = w2[:, :, None] * (e1 * y0[:, :, None])
        mid_s = jnp.concatenate([m0a, m0b], axis=1)
        mid_v = jnp.concatenate([m1a, m1b], axis=1)
        inv = 1.0 / np.sqrt(NUM_NEIGHBORS)
        ns = jax.ops.segment_sum(mid_s, edge_dst, num_segments=N) * inv
        nv = jax.ops.segment_sum(mid_v, edge_dst, num_segments=N) * inv
        o0, o1 = _fctp_scalar_attr(ns, nv, z, W_l2_0, W_l2_1)
        c_s, c_x = (np.sin(np.pi / 8), np.cos(np.pi / 8))
        out0 = c_s * s0 + c_x * o0
        out1 = c_s * s1 + c_x * o1
        return jnp.concatenate([out0, out1.reshape(N, -1)], axis=1)

    def _L3_gnn_ref(node_features, edge_index, edge_attr_tensor, node_attr_scalar_raw, Wm_ss, Wm_vv, Wm_sv, Wm_vs, Lm_s, Lm_v, Wu_ss, Wu_vv, Wu_sv, Wu_vs, Lu_s, Lu_v):
        import jax, jax.numpy as jnp
        import numpy as np
        N = 20000
        E = 10000
        INV_SQRT3 = 0.5773502691896258
        INV8 = 0.125
        INV_SQRT32 = 0.17677669529663687
        INV64 = 0.015625
        INV32 = 0.03125
        INV_SQRT2048 = 0.022097086912079608
        n = node_features.shape[0]
        e = edge_attr_tensor.shape[0]
        row, col = (edge_index[0], edge_index[1])
        r_vec = edge_attr_tensor[:, :3]
        dist = edge_attr_tensor[:, 3:4]
        xj = node_features[col]
        s = xj[:, :64]
        v = xj[:, 64:].reshape(e, 32, 3)
        m0 = s @ Wm_ss * dist * INV8 + jnp.einsum('eui,ei->eu', v, r_vec) @ Wm_vv * (INV_SQRT3 * INV_SQRT32)
        m1 = (s @ Wm_sv)[:, :, None] * r_vec[:, None, :] * INV8 + jnp.einsum('eui,uw->ewi', v, Wm_vs) * dist[:, :, None] * INV_SQRT32
        m0 = m0 + s @ Lm_s * INV8
        m1 = m1 + jnp.einsum('eui,uw->ewi', v, Lm_v) * INV_SQRT32
        msg = jnp.concatenate([m0, m1.reshape(e, 96)], axis=-1)
        agg = jax.ops.segment_sum(msg, row, num_segments=n)
        a0 = agg[:, :64]
        a1 = agg[:, 64:].reshape(n, 32, 3)
        xs = node_features[:, :64]
        xv = node_features[:, 64:].reshape(n, 32, 3)
        u0 = jnp.einsum('nu,nv,uvw->nw', xs, a0, Wu_ss) * INV64 + jnp.einsum('nui,nvi,uvw->nw', xv, a1, Wu_vv) * (INV_SQRT3 * INV32)
        u1 = jnp.einsum('nu,nvi,uvw->nwi', xs, a1, Wu_sv) * INV_SQRT2048 + jnp.einsum('nui,nv,uvw->nwi', xv, a0, Wu_vs) * INV_SQRT2048
        u0 = u0 + xs @ Lu_s * INV8
        u1 = u1 + jnp.einsum('nui,uw->nwi', xv, Lu_v) * INV_SQRT32
        upd = jnp.concatenate([u0, u1.reshape(n, 96)], axis=-1)
        return node_features + upd
    edge_index = jnp.stack([src, dst])
    h = jnp.maximum(_layernorm(x, axis=-1), 0.0)
    x = x + _L0_gnn_ref(h, edge_index, edge_attr_32, node_vec1, L0_gnn_W1, L0_gnn_W2, L0_gnn_W3, L0_gnn_W4, L0_gnn_Wm, L0_gnn_bm, L0_gnn_Wu, L0_gnn_bu)
    h = jnp.maximum(_layernorm(x, axis=-1), 0.0)
    x = x + _L1_gnn_ref(h, node_vec1, edge_attr_16, edge_attr_4, src, dst, L1_gnn_Wfc1, L1_gnn_Wfc2, L1_gnn_Wsc0, L1_gnn_Wsc1, L1_gnn_Wl1_0, L1_gnn_Wl1_1, L1_gnn_Wl2_s, L1_gnn_Wl2_v, L1_gnn_Wa)
    h = jnp.maximum(_layernorm(x, axis=-1), 0.0)
    x = x + _L2_gnn_ref(h, node_vec1, src, dst, edge_attr_4, edge_attr_12, L2_gnn_W_sc0, L2_gnn_W_sc1, L2_gnn_W_l1_0, L2_gnn_W_l1_1, L2_gnn_W_fc1, L2_gnn_W_fc2, L2_gnn_W_l2_0, L2_gnn_W_l2_1)
    h = jnp.maximum(_layernorm(x, axis=-1), 0.0)
    x = x + _L3_gnn_ref(h, edge_index, edge_attr_4, node_vec1, L3_gnn_Wm_ss, L3_gnn_Wm_vv, L3_gnn_Wm_sv, L3_gnn_Wm_vs, L3_gnn_Lm_s, L3_gnn_Lm_v, L3_gnn_Wu_ss, L3_gnn_Wu_vv, L3_gnn_Wu_sv, L3_gnn_Wu_vs, L3_gnn_Lu_s, L3_gnn_Lu_v)
    return x

_drawn_inputs = setup_inputs


def setup_inputs(seed=0):
    import zlib

    import numpy as np

    out = dict(_drawn_inputs(seed))
    spreads = {'L0_gnn_bm': (0.0, 0.1), 'L0_gnn_bu': (0.0, 0.1)}
    factors = {'edge_attr_12': 3.618,
     'L1_gnn_Wl1_1': 3.331,
     'L1_gnn_Wl2_s': 3.204,
     'L1_gnn_Wl2_v': 3.251,
     'L2_gnn_W_l1_1': 3.203}
    for name, (base, spread) in spreads.items():
        noise = np.random.default_rng([zlib.crc32(name.encode()), seed]).standard_normal(out[name].shape)
        drawn = base * np.exp(spread * noise) if base else spread * noise
        out[name] = jnp.asarray(drawn.astype(out[name].dtype))
    for name, factor in factors.items():
        out[name] = (out[name] * factor).astype(out[name].dtype)
    return out
```

```python
import numpy as np
import concourse.bass as bass
from concourse import mybir
from contextlib import ExitStack

F32, F32R, I32 = mybir.dt.float32, mybir.dt.float32r, mybir.dt.int32
ALU = mybir.AluOpType
ACT = mybir.ActivationFunctionType
AX = mybir.AxisListType
POOL, DVE = mybir.EngineType.Pool, mybir.EngineType.DVE

P = 128
T = 4
GR = T * P
S, V, D = 64, 32, 160
HALF = D // 2
AW = D + 2
EPS = 1e-5


class At:

    def __init__(self, g, rest, half, quarter):
        self.g, self.rest, self.half, self.quarter = g, rest, half, quarter
        self.b = rest % 2

    def back(self, n):
        r = self.rest - n
        return At(self.g - n, r % 4, self.half + (r // 2 - self.rest // 2), 
                  None if self.quarter is None else self.quarter + r // 4)

    def next(self):
        return self.back(-1)

    def has(self, n):
        return not isinstance(self.g, int) or self.g >= n

    def within(self, n, count):
        return not isinstance(self.g, int) or n <= self.g < n + count

    def first(self):
        return isinstance(self.g, int) and self.g == 0

    def last(self, count):
        return isinstance(self.g, int) and self.g == count - 1


def walk(eng, count, body, unroll=2, lag=0):
    head = -(-max(lag, 2) // unroll) * unroll
    turns = (count - 1 - head) // unroll
    for g in range(head):
        body(At(g, g % 4, g // 2, g // 4))
    with eng.Fori(head // unroll, head // unroll + turns) as j:
        for r in range(unroll):
            if unroll == 2:
                body(At(j * 2 + r, r, j, None))
            else:
                body(At(j * 4 + r, r, j * 2 + r // 2, j))
    for g in range(head + turns * unroll, count + lag):
        body(At(g, g % 4, g // 2, g // 4))


def apart(core, eng, at):
    if not isinstance(at.g, int):
        eng.sem_inc(core.passed[eng.engine], 1)


class Count:

    def __init__(self, sem, per):
        self.sem, self.per = sem, per

    def at(self, at, k=None):
        return at.g * self.per + (self.per if k is None else k)


class Moves:

    def __init__(self, sems, per=1):
        self.sems, self.per = sems, per

    def of(self, at):
        return self.sems[at.rest % len(self.sems)]

    def at(self, at, k=None):
        n = at.half if len(self.sems) == 2 else at.quarter
        return n * (16 * self.per) + 16 * (self.per if k is None else k)


class Core:

    def __init__(self, nc, ctx, d, n_nodes, n_edges):
        self.nc, self.ctx, self.d = nc, ctx, d
        self.node_groups, self.edge_groups = n_nodes // GR, n_edges // GR

        self.passed = {e: nc.alloc_semaphore(name=f"passed_{e.name}") for e in (POOL, DVE)}
        self.pass_sems = []

    def sem(self, name):
        self.pass_sems.append(self.nc.alloc_semaphore(name=name))
        return self.pass_sems[-1]

    def run(self, one_pass):
        one_pass(self)
        self.nc.clear_and_free_semaphores(self.pass_sems)
        self.nc.all_engine_barrier()
        self.pass_sems = []

    def count(self, name, per):
        return Count(self.sem(name), per)

    def moves(self, name, per=1):
        return Moves([self.sem(f"{name}_0"), self.sem(f"{name}_1")], per)


def sbuf(nc, ctx, name, shape, dt=F32):
    return ctx.enter_context(nc.sbuf_tensor(name, shape, dt))


def banks(nc, ctx, name, n):
    return [ctx.enter_context(nc.psum_tensor(f"{name}{i}", [P, 512], F32)) for i in range(n)]


def over(ap, n):
    p, m = ap.shape
    return ap.unsqueeze(2).broadcast_to([p, m, n])


PACKS = {
    "n0": {"lin": (97, 2 * D)},
    "e0": {"w1": (P, 4 * S), "w2": (96, 8 * S), "w4": (96, 8 * 96), "w3": (P, 2 * P),
           "wm_s": (HALF, 2 * P), "wm_v": (HALF, 2 * 97), "wu": (HALF, 2 * D),
           "gather": (P, 26 * P), "sum": (P, V)},
    "e1": {"fc1": (P, P), "fc2": (P, 192), "l1": (HALF, 2 * 3 * 96), "l2": (96, 4 * AW),
           "gather": (P, 6 * 96)},
    "n1": {"sc": (HALF, 2 * D), "sc2": (HALF, 2 * D)},
    "e2": {"fc1": (P, P), "fc2": (P, 192), "l1": (HALF, 2 * 3 * 96), "l2": (96, 4 * AW),
           "gather": (P, 6 * 96)},
    "n3": {"lin": (HALF, 2 * D)},
    "e3": {"y": (96, 2 * (2 * D + V)), "ss": (P, 32 * S), "vv": (P, 8 * S), "sv": (P, 8 * P),
           "vs": (P, 8 * P), "pick_s": (P, 32 * P), "pick_v": (P, 8 * P), "sum": (P, 8 * V),
           "out_s": (P, D), "out_v": (96, D)},
    "ident": {"eye": (P, P), "earlier": (P, P), "spare": (P, 1)},
}


def offsets(name):
    at, out = 0, {}
    for k, (_, w) in PACKS[name].items():
        out[k] = at
        at += w
    return out, at


def pack(name, **parts):
    off, width = offsets(name)
    out = np.zeros((P, width), np.float32)
    for k, (rows, w) in PACKS[name].items():
        out[:rows, off[k]:off[k] + w] = np.asarray(parts[k]).reshape(rows, w)
    return out


def feature_scales(part, width):
    return [(part, 0, S, 0, width, 1 / 8), (part, S, HALF, 0, width, 1 / np.sqrt(32.0)),
            (part, 0, HALF, width, 2 * width, 1 / np.sqrt(32.0))]


def load_pack(core, ctx, name, scales, halves):
    nc = core.nc
    off, width = offsets(name)
    W = sbuf(nc, ctx, f"{name}_w", [P, width])
    part = lambda k: W[:PACKS[name][k][0], off[k]:off[k] + PACKS[name][k][1]]
    hi, lo = {}, {}
    for k, both in halves.items():
        shape = list(PACKS[name][k])
        hi[k] = sbuf(nc, ctx, f"{name}_{k}_hi", shape, F32R)
        if both:
            lo[k] = sbuf(nc, ctx, f"{name}_{k}_lo", shape, F32R)
    loaded, scaled, rounded = (core.sem(f"{name}_{x}") for x in ("w_loaded", "w_scaled", "w_rounded"))
    with nc.Block() as block:
        @block.sync
        def _(sp):
            sp.dma_start(W[:, :], core.d[f"pack_{name}"]).then_inc(loaded, 16)

        @block.vector
        def _(dve):
            dve.wait_ge(loaded, 16)
            for k, r0, r1, c0, c1, c in scales:
                o = W[r0:r1, off[k] + c0:off[k] + c1]
                dve.tensor_scalar(o, o, float(c), None, ALU.mult).then_inc(scaled, 1)
            if scales:
                dve.wait_ge(scaled, len(scales))
            n = 0
            for k in hi:
                dve.tensor_copy(hi[k][:, :], part(k)).then_inc(rounded, 1)
                n += 1
            for k in lo:
                dve.wait_ge(rounded, n)
                dve.tensor_tensor(lo[k][:, :], part(k), hi[k][:, :].bitcast(F32),
                                  ALU.subtract).then_inc(rounded, 1)
    return W, {k: part(k) for k in PACKS[name]}, hi, lo


def index_pass(core):
    nc, d, n = core.nc, core.d, core.edge_groups
    with ExitStack() as ctx:
        same = [sbuf(nc, ctx, f"ix_same{x}", [P, T, P]) for x in range(2)]
        rank = [sbuf(nc, ctx, f"ix_rank{x}", [P, T]) for x in range(2)]
        move = [sbuf(nc, ctx, f"ix_move{x}", [P, T]) for x in range(2)]
        row_of = sbuf(nc, ctx, "ix_row", [P, 2, T])
        loaded = core.moves("ix_loaded", 2)
        step = core.count("ix_step", 16)
        ready = core.sem("ix_ready")
        rows2 = [sbuf(nc, ctx, f"ix_rows{b}", [P, 2, GR], I32) for b in range(2)]
        ends = ("src", "dst")
        with nc.Block() as block:
            @block.sync
            def _(sp):
                for e in ends:
                    sp.dma_start(core.cols[e][:, :], d[f"{e}_cols"]).then_inc(ready, 16)
                sp.dma_start(core.ident[:, :], d["pack_ident"]).then_inc(ready, 16)

                def body(at):
                    if at.has(2):
                        sp.wait_ge(step.sem, step.at(at.back(2)))
                    for x, e in enumerate(ends):
                        sp.dma_start(rows2[at.b][:, x, :],
                                     d[f"{e}_rows"][:, bass.ds(at.g * GR, GR)].broadcast_to([P, GR])
                                     ).then_inc(loaded.of(at), 16)
                walk(sp, n, body)

            @block.vector
            def _(dve):
                dve.wait_ge(ready, 48)

                def body(at):
                    dve.wait_ge(loaded.of(at), loaded.at(at))
                    k = 0

                    def then(ins):
                        nonlocal k
                        ins.then_inc(step.sem, 1)
                        k += 1

                    cols = [core.cols[e][:, bass.ds(at.g * T, T)] for e in ends]
                    for x in range(2):
                        then(dve.tensor_tensor(same[x][:, :, :],
                                               rows2[at.b][:, x, :].rearrange("p (t q) -> p t q", t=T),
                                               over(cols[x], P), ALU.is_equal))
                    dve.wait_ge(step.sem, step.at(at, k))
                    for x in range(2):
                        then(dve.tensor_tensor(same[x][:, :, :], same[x][:, :, :],
                                               core.earlier.unsqueeze(1).broadcast_to([P, T, P]), ALU.mult))
                    dve.wait_ge(step.sem, step.at(at, k))
                    for x in range(2):
                        then(dve.tensor_reduce(rank[x][:, :], same[x][:, :, :], AX.X, ALU.max))
                    for x in range(2):
                        then(dve.tensor_copy(move[x][:, :], cols[x]))
                    dve.wait_ge(step.sem, step.at(at, k))
                    for x in range(2):
                        then(dve.tensor_scalar(row_of[:, x, :], move[x][:, :], -1.0, core.spare,
                                               ALU.mult, ALU.add))
                    dve.wait_ge(step.sem, step.at(at, k))
                    for x in range(2):
                        then(dve.tensor_tensor(rank[x][:, :], rank[x][:, :], row_of[:, x, :], ALU.mult))
                    dve.wait_ge(step.sem, step.at(at, k))
                    for x in range(2):
                        then(dve.tensor_tensor(move[x][:, :], move[x][:, :], rank[x][:, :], ALU.add))
                    dve.wait_ge(step.sem, step.at(at, k))
                    for x, e in enumerate(ends):
                        then(dve.tensor_copy(core.target[e][:, bass.ds(at.g * T, T)], move[x][:, :]))
                    assert k == step.per
                walk(dve, n, body)


def plain_node_pass(core, name, src, dst, with_agg):
    nc, d, n = core.nc, core.d, core.node_groups
    kb = PACKS[name]["lin"][0]
    with ExitStack() as ctx:
        W, w, _, _ = load_pack(core, ctx, name, feature_scales("lin", D) if name == "n3" else [], {})
        X = [sbuf(nc, ctx, f"{name}_x{b}", [P, T * D]) for b in range(2)]
        H = [sbuf(nc, ctx, f"{name}_h{b}", [P, T * D]) for b in range(2)]
        Y = [sbuf(nc, ctx, f"{name}_y{b}", [P, T * D]) for b in range(2)]
        HT = [sbuf(nc, ctx, f"{name}_ht{b}", [P, 2, GR]) for b in range(2)]
        st = [sbuf(nc, ctx, f"{name}_st{b}", [P, T, 6]) for b in range(2)]
        mv = [sbuf(nc, ctx, f"{name}_mv{b}", [P, T, 2]) for b in range(2)]
        sd = [sbuf(nc, ctx, f"{name}_sd{b}", [P, T]) for b in range(2)]
        rs = [sbuf(nc, ctx, f"{name}_rs{b}", [P, T]) for b in range(2)]
        nm = [sbuf(nc, ctx, f"{name}_nm{b}", [P, T]) for b in range(2)]
        eps = sbuf(nc, ctx, f"{name}_eps", [P, 1])
        zero = sbuf(nc, ctx, f"{name}_zero", [P, T * AW])
        TP = banks(nc, ctx, f"{name}_tp", 4)
        LP = banks(nc, ctx, f"{name}_lp", 4)
        x_in = core.moves(f"{name}_x_in")
        h_out = core.moves(f"{name}_h_out")
        y_out = core.moves(f"{name}_y_out")
        zeroed = core.moves(f"{name}_zeroed")
        stats = core.count(f"{name}_stats", T)
        means = core.count(f"{name}_means", T)
        std = core.count(f"{name}_std", 1)
        inv = core.count(f"{name}_inv", 2)
        h_ready = core.count(f"{name}_h_ready", T)
        turned = core.count(f"{name}_turned", 2)
        ht_ready = core.count(f"{name}_ht_ready", 2)
        mixed = core.count(f"{name}_mixed", 2)
        y_ready = core.count(f"{name}_y_ready", 2)
        const = core.sem(f"{name}_const")
        fold = core.sem(f"{name}_fold")
        rows = lambda a, at: a[bass.ds(at.g * GR, GR), :].rearrange("(p t) c -> p (t c)", t=T)
        with nc.Block() as block:
            nconst = 4 + 2 * (kb > HALF)

            @block.sync
            def _(sp):
                def body(at):
                    if at.has(2):
                        sp.wait_ge(y_ready.sem, y_ready.at(at.back(2)))
                    sp.dma_start(X[at.b][:, :], rows(d[src], at)).then_inc(x_in.of(at), 16)
                    if not at.first():
                        p = at.back(1)
                        sp.wait_ge(y_ready.sem, y_ready.at(p))
                        sp.dma_start(rows(d[dst], p), Y[p.b][:, :]).then_inc(y_out.of(p), 16)
                    if at.last(n):
                        sp.wait_ge(y_ready.sem, y_ready.at(at))
                        sp.dma_start(rows(d[dst], at), Y[at.b][:, :]).then_inc(y_out.of(at), 16)
                        for q in (at, at.back(1)):
                            sp.wait_ge(y_out.of(q), y_out.at(q))
                walk(sp, n, body)

            @block.vector
            def _(dve):
                dve.memset(eps[:, :], EPS).then_inc(const, 1)
                dve.memset(zero[:, :], 0.0).then_inc(const, 1)
                for b in range(2):
                    dve.memset(HT[b][64:128, :, :], 0.0).then_inc(const, 1)
                if kb > HALF:
                    dve.wait_ge(const, 4)
                    for b in range(2):
                        dve.memset(HT[b][96:97, 1, :], 1.0).then_inc(const, 1)
                for h in range(2):
                    dve.tensor_tensor(w["lin"][0:HALF, h * D + h * HALF:h * D + (h + 1) * HALF],
                                      w["lin"][0:HALF, h * D + h * HALF:h * D + (h + 1) * HALF],
                                      core.eye[0:HALF, 0:HALF], ALU.add).then_inc(fold, 1)

                def front(at):
                    dve.wait_ge(x_in.of(at), x_in.at(at))
                    if at.has(2):
                        dve.wait_ge(h_ready.sem, h_ready.at(at.back(2)))
                    for t in range(T):
                        dve.bn_stats(st[at.b][:, t, :], X[at.b][:, t * D:(t + 1) * D]).then_inc(stats.sem, 1)
                    for t in range(T):
                        dve.wait_ge(stats.sem, stats.at(at, t + 1))
                        apart(core, dve, at)
                        dve.bn_aggr(mv[at.b][:, t, :], st[at.b][:, t, :]).then_inc(means.sem, 1)
                    dve.wait_ge(std.sem, std.at(at))
                    dve.reciprocal(rs[at.b][:, :], sd[at.b][:, :]).then_inc(inv.sem, 1)
                    dve.wait_ge(inv.sem, inv.at(at, 1))
                    dve.scalar_tensor_tensor(nm[at.b][:, :], mv[at.b][:, :, 0], -1.0, rs[at.b][:, :],
                                             ALU.mult, ALU.mult).then_inc(inv.sem, 1)

                def back(at):
                    if at.has(2):
                        dve.wait_ge(y_out.of(at.back(2)), y_out.at(at.back(2)))
                    for h in range(2):
                        dve.wait_ge(mixed.sem, mixed.at(at, h + 1))
                        dve.tensor_tensor(Y[at.b][:, h * 2 * D:(h + 1) * 2 * D], LP[2 * at.b + h][:, 0:2 * D],
                                          X[at.b][:, h * 2 * D:(h + 1) * 2 * D], ALU.add).then_inc(y_ready.sem, 1)

                def body(at):
                    front(at)
                    if not at.first():
                        back(at.back(1))
                    if at.last(n):
                        back(at)
                walk(dve, n, body)

            @block.scalar
            def _(act):
                act.wait_ge(const, nconst)

                def front(at):
                    act.wait_ge(means.sem, means.at(at))
                    act.activation(sd[at.b][:, :], mv[at.b][:, :, 1], ACT.Sqrt, bias=eps[:, 0:1]
                                   ).then_inc(std.sem, 1)
                    act.wait_ge(inv.sem, inv.at(at))
                    if at.has(2):
                        act.wait_ge(h_out.of(at.back(2)), h_out.at(at.back(2)))
                    if at.has(2):
                        act.wait_ge(turned.sem, turned.at(at.back(2)))
                    for t in range(T):
                        act.activation(H[at.b][:, t * D:(t + 1) * D], X[at.b][:, t * D:(t + 1) * D], ACT.Relu,
                                       bias=nm[at.b][:, t:t + 1], scale=rs[at.b][:, t:t + 1]
                                       ).then_inc(h_ready.sem, 1)
                    act.wait_ge(h_ready.sem, h_ready.at(at))
                    act.dma_start(rows(d["H"], at), H[at.b][:, :]).then_inc(h_out.of(at), 16)
                    if with_agg:
                        act.dma_start(rows(d["AGG"], at), zero[:, :]).then_inc(zeroed.of(at), 16)

                def copies(at):
                    if at.has(2):
                        act.wait_ge(mixed.sem, mixed.at(at.back(2)))
                    for h in range(2):
                        act.wait_ge(turned.sem, turned.at(at, h + 1))
                        act.activation(HT[at.b][0:HALF, h, :], TP[2 * at.b + h][0:HALF, :], ACT.Copy
                                       ).then_inc(ht_ready.sem, 1)

                def body(at):
                    front(at)
                    if not at.first():
                        copies(at.back(1))
                    if at.last(n):
                        copies(at)
                        for q in (at, at.back(1)):
                            act.wait_ge(h_out.of(q), h_out.at(q))
                            if with_agg:
                                act.wait_ge(zeroed.of(q), zeroed.at(q))
                walk(act, n, body)

            @block.tensor
            def _(pe):
                pe.wait_ge(fold, 2)
                pe.wait_ge(const, nconst)

                def turn(at):
                    pe.wait_ge(h_ready.sem, h_ready.at(at))
                    if at.has(2):
                        pe.wait_ge(ht_ready.sem, ht_ready.at(at.back(2)))
                    for h in range(2):
                        for t in range(T):
                            ins = pe.transpose(TP[2 * at.b + h][0:HALF, t * P:(t + 1) * P],
                                               H[at.b][:, t * D + h * HALF:t * D + (h + 1) * HALF], core.eye)
                        ins.then_inc(turned.sem, 1)

                def mix(at):
                    if at.has(2):
                        pe.wait_ge(y_ready.sem, y_ready.at(at.back(2)))
                    pe.wait_ge(ht_ready.sem, ht_ready.at(at))
                    for t in range(T):
                        o = LP[2 * at.b + t // 2][:, (t % 2) * D:(t % 2 + 1) * D]
                        pe.matmul(o, HT[at.b][0:HALF, 0, t * P:(t + 1) * P], w["lin"][0:HALF, 0:D],
                                  start=True, stop=False)
                        ins = pe.matmul(o, HT[at.b][0:kb, 1, t * P:(t + 1) * P], w["lin"][:, D:2 * D],
                                        start=False, stop=True)
                        if t % 2:
                            ins.then_inc(mixed.sem, 1)

                def body(at):
                    turn(at)
                    if not at.first():
                        mix(at.back(1))
                    if at.last(n):
                        mix(at)
                walk(pe, n, body)


class Gather:

    def __init__(self, core, ctx, name, table, end, width=D):
        self.core, self.table, self.end = core, table, end
        self.rows = [sbuf(core.nc, ctx, f"{name}_g{b}", [P, T, width]) for b in range(2)]
        self.index = [sbuf(core.nc, ctx, f"{name}_gi{b}", [P, T], I32) for b in range(2)]
        self.indexed = core.count(f"{name}_gather_index", 1)
        self.here = core.moves(f"{name}_gathered", T)

    def pool(self, pool, at):
        if at.has(2):
            pool.wait_ge(self.here.of(at.back(2)), self.here.at(at.back(2)))
        apart(self.core, pool, at)
        pool.tensor_copy(self.index[at.b][:, :], self.core.cols[self.end][:, bass.ds(at.g * T, T)]
                         ).then_inc(self.indexed.sem, 1)
        pool.wait_ge(self.indexed.sem, self.indexed.at(at))
        apart(self.core, pool, at)
        for t in range(T):
            pool.indirect_dma_start(self.rows[at.b][:, t, :], None, self.core.d[self.table],
                                    bass.IndirectOffsetOnAxis(ap=self.index[at.b][:, t:t + 1], axis=0)
                                    ).then_inc(self.here.of(at), 16)


class Scatter:

    def __init__(self, core, ctx, name, table, end, width, bank):
        nc = core.nc
        self.core, self.table, self.end, self.width, self.bank = core, table, end, width, bank
        self.U = [sbuf(nc, ctx, f"{name}_u{b}", [P, T, width]) for b in range(2)]
        self.out = [sbuf(nc, ctx, f"{name}_so{b}", [P, T, width]) for b in range(2)]
        self.same = [sbuf(nc, ctx, f"{name}_sm{b}", [P, T, P]) for b in range(2)]
        self.near = [sbuf(nc, ctx, f"{name}_sr{b}", [P, GR], I32) for b in range(2)]
        self.index = [sbuf(nc, ctx, f"{name}_si{b}", [P, T], I32) for b in range(2)]
        self.near_in = core.moves(f"{name}_targets_in")
        self.same_ready = core.count(f"{name}_same_ready", 1)
        self.u_ready = core.count(f"{name}_u_ready", 2)
        self.merged = core.count(f"{name}_merged", 2)
        self.out_ready = core.count(f"{name}_out_ready", 2)
        self.indexed = core.count(f"{name}_scatter_index", 1)
        self.added = core.moves(f"{name}_added", T)

    def sp(self, sp, at):
        if at.has(2):
            sp.wait_ge(self.same_ready.sem, self.same_ready.at(at.back(2)))
        sp.dma_start(self.near[at.b][:, :], self.core.d[f"{self.end}_rows"][:, bass.ds(at.g * GR, GR)]
                     .broadcast_to([P, GR])).then_inc(self.near_in.of(at), 16)

    def dve(self, dve, at):
        dve.wait_ge(self.near_in.of(at), self.near_in.at(at))
        if at.has(2):
            dve.wait_ge(self.merged.sem, self.merged.at(at.back(2)))
        dve.tensor_tensor(self.same[at.b][:, :, :], self.near[at.b][:, :].rearrange("p (t q) -> p t q", t=T),
                          over(self.core.cols[self.end][:, bass.ds(at.g * T, T)], P), ALU.is_equal
                          ).then_inc(self.same_ready.sem, 1)

    def pe(self, pe, at):
        pe.wait_ge(self.same_ready.sem, self.same_ready.at(at))
        pe.wait_ge(self.u_ready.sem, self.u_ready.at(at))
        for t in range(T):
            ins = pe.matmul(self.bank[t // 2][:, (t % 2) * self.width:(t % 2 + 1) * self.width],
                            self.same[at.b][:, t, :], self.U[at.b][:, t, :], start=True, stop=True)
            if t % 2:
                ins.then_inc(self.merged.sem, 1)

    def act(self, act, at):
        if at.has(2):
            act.wait_ge(self.added.of(at.back(2)), self.added.at(at.back(2)))
        for h in range(2):
            act.wait_ge(self.merged.sem, self.merged.at(at, h + 1))
            act.activation(self.out[at.b][:, 2 * h:2 * h + 2, :].rearrange("p t c -> p (t c)"),
                           self.bank[h][:, 0:2 * self.width], ACT.Copy).then_inc(self.out_ready.sem, 1)

    def pool(self, pool, at):
        if at.has(2):
            pool.wait_ge(self.added.of(at.back(2)), self.added.at(at.back(2)))
        apart(self.core, pool, at)
        pool.tensor_copy(self.index[at.b][:, :], self.core.target[self.end][:, bass.ds(at.g * T, T)]
                         ).then_inc(self.indexed.sem, 1)
        pool.wait_ge(self.indexed.sem, self.indexed.at(at))
        pool.wait_ge(self.out_ready.sem, self.out_ready.at(at))
        if at.has(1):
            pool.wait_ge(self.added.of(at.back(1)), self.added.at(at.back(1)))
        apart(self.core, pool, at)
        for t in range(T):
            if t:
                pool.wait_ge(self.added.of(at), self.added.at(at, t))
                apart(self.core, pool, at)
            pool.indirect_dma_start(self.core.d[self.table],
                                    bass.IndirectOffsetOnAxis(ap=self.index[at.b][:, t:t + 1], axis=0),
                                    self.out[at.b][:, t, :], None, compute_op=ALU.add
                                    ).then_inc(self.added.of(at), 16)


class Plan:

    def __init__(self, core, ctx, name, counts, ring, tiles, lag):
        self.counts, self.ring, self.lag = counts, ring, lag
        self.F = [sbuf(core.nc, ctx, f"{name}_f{i}", [P, GR]) for i in range(tiles)]
        self.first = [sum(counts[:s]) for s in range(len(counts))]
        self.ns, self.nm = len(counts), sum(counts)
        self.filled = core.count(f"{name}_filled", self.ns)
        self.multiplied = core.count(f"{name}_multiplied", self.nm)
        self.contracted = core.count(f"{name}_contracted", self.nm)

    def bank(self, s):
        return self.ring[s % len(self.ring)]

    def tile(self, m):
        return self.F[m % len(self.F)]

    def bank_read(self, s):
        last = s - len(self.ring)
        if last >= 0:
            return self.first[last] + self.counts[last]
        last = max(x for x in range(self.ns) if x % len(self.ring) == s)
        return self.first[last] + self.counts[last] - self.nm

    def tile_read(self, m):
        last = m - len(self.F)
        if last >= 0:
            return last + 1
        return max(x for x in range(self.nm) if x % len(self.F) == m) + 1 - self.nm


def edges0(core):
    nc, d, n, name = core.nc, core.d, core.edge_groups, "e0"
    r2 = 1 / np.sqrt(2.0)
    with ExitStack() as ctx:
        W, w, hi, lo = load_pack(core, ctx, name,
                                 [("w1", 0, P, 0, 4 * S, r2 / np.sqrt(512)),
                                  ("w2", 0, 96, 0, 8 * S, r2 / (np.sqrt(3.0) * 16)),
                                  ("w4", 0, 96, 0, 8 * 96, r2 / 16), ("w3", 0, P, 0, 2 * P, r2 / np.sqrt(512))],
                                 {"w3": True, "gather": False})
        EA = [sbuf(nc, ctx, f"e0_ea{b}", [64, GR]) for b in range(2)]
        EH = [sbuf(nc, ctx, f"e0_eh{b}", [P, GR], F32R) for b in range(2)]
        XX = [sbuf(nc, ctx, f"e0_xx{b}", [P, T, 224]) for b in range(2)]
        XS = [sbuf(nc, ctx, f"e0_xs{b}", [P, GR]) for b in range(2)]
        XH = [sbuf(nc, ctx, f"e0_xh{b}", [P, GR], F32R) for b in range(2)]
        XV = [sbuf(nc, ctx, f"e0_xv{b}", [96, GR]) for b in range(2)]
        T3 = [sbuf(nc, ctx, f"e0_t3{b}", [P, 2, GR]) for b in range(2)]
        US = [sbuf(nc, ctx, f"e0_us{b}", [P, GR]) for b in range(2)]
        UV = [sbuf(nc, ctx, f"e0_uv{b}", [97, GR]) for b in range(2)]
        fold_s = sbuf(nc, ctx, "e0_fold_s", [P, D])
        fold_v = sbuf(nc, ctx, "e0_fold_v", [97, D])
        front = banks(nc, ctx, "e0_front", 2)
        ring = banks(nc, ctx, "e0_ring", 4)
        AS, AV = banks(nc, ctx, "e0_acc", 2)

        ga = Gather(core, ctx, name, "H", "dst")
        sc = Scatter(core, ctx, name, "X1", "src", D, front)
        ea_in = core.moves("e0_ea_in", 2)
        spread = core.count("e0_spread", 2)
        turned = core.count("e0_turned", 2)
        x_ready = core.count("e0_x_ready", 3)
        ea_hi = core.count("e0_ea_hi", 1)
        rest = core.count("e0_rest", 2)
        t3_done = core.count("e0_t3_done", 2)
        t3_ready = core.count("e0_t3_ready", 2)
        sums = core.count("e0_sums", 2)
        mixed = core.count("e0_mixed", 2)
        folded, fold_ready, const = (core.sem(f"e0_{x}") for x in ("folded", "fold_ready", "const"))

        sources = []
        for c in range(4):
            sources.append((P, c, (XS,), w["w1"][:, c * S:(c + 1) * S], AS, 64 * (c % 2), c < 2))
        for c in range(8):
            sources.append((96, 4 + c, (XV,), w["w2"][:, c * S:(c + 1) * S], AS, 64 * (c % 2), False))
        for c in range(8):
            sources.append((96, 12 + c, (XV,), w["w4"][:, c * 96:(c + 1) * 96], AV, 0, c == 0))
        for i in range(3):
            for q in range(2):
                sources.append((P, 20 + 2 * i + q, (T3, q), w["sum"], AV, 32 * i, False))
        pr = Plan(core, ctx, name, [1] * len(sources), ring, 4, 3)

        with nc.Block() as block:
            @block.gpsimd
            def _(pool):
                def body(at):
                    if at.first():
                        ga.pool(pool, at)
                    if not at.last(n):
                        if at.has(1):
                            pool.wait_ge(spread.sem, spread.at(at.back(1)))
                        apart(core, pool, at)
                        ga.pool(pool, at.next())
                    if not at.first():
                        sc.pool(pool, at.back(1))
                    if at.last(n):
                        sc.pool(pool, at)
                        for q in (at, at.back(1)):
                            pool.wait_ge(sc.added.of(q), sc.added.at(q))
                            apart(core, pool, q)
                walk(pool, n, body)

            @block.sync
            def _(sp):
                def body(at):
                    if at.has(2):
                        sp.wait_ge(rest.sem, rest.at(at.back(2)))
                    for h in range(2):
                        sp.dma_start(EA[at.b][32 * h:32 * h + 32, :], d["ea32"][:, bass.ds(at.g * GR, GR)]
                                     ).then_inc(ea_in.of(at), 16)
                    sc.sp(sp, at)
                walk(sp, n, body)

            @block.scalar
            def _(act):
                act.wait_ge(folded, 2)
                act.activation(fold_s[:, :], front[0][:, 0:D], ACT.Copy).then_inc(fold_ready, 1)
                act.activation(fold_v[:, :], front[1][0:97, 0:D], ACT.Copy).then_inc(fold_ready, 1)
                act.wait_ge(const, 4)

                def start(at):
                    act.wait_ge(ga.here.of(at), ga.here.at(at))
                    act.activation(XX[at.b][:, :, 0:P].rearrange("p t (r a) -> p t r a", r=2),
                                   ga.rows[at.b][:, :, 0:S].unsqueeze(2).broadcast_to([P, T, 2, S]), ACT.Copy
                                   ).then_inc(spread.sem, 1)
                    act.activation(XX[at.b][:, :, P:224].rearrange("p t (i a) -> p t i a", i=3),
                                   ga.rows[at.b][:, :, S:D].rearrange("p t (a i) -> p t i a", i=3), ACT.Copy
                                   ).then_inc(spread.sem, 1)
                    act.wait_ge(ea_in.of(at), ea_in.at(at))
                    act.activation(EH[at.b][0:64, :], EA[at.b][:, :], ACT.Copy).then_inc(ea_hi.sem, 1)
                    act.wait_ge(turned.sem, turned.at(at, 1))
                    act.activation(XS[at.b][:, :], front[0][:, :], ACT.Copy).then_inc(x_ready.sem, 1)
                    act.activation(XH[at.b][:, :], front[0][:, :], ACT.Copy).then_inc(x_ready.sem, 1)
                    act.wait_ge(turned.sem, turned.at(at, 2))
                    act.activation(XV[at.b][:, :], front[1][0:96, :], ACT.Copy).then_inc(x_ready.sem, 1)
                    for q in range(2):
                        act.wait_ge(t3_done.sem, t3_done.at(at, q + 1))
                        act.activation(T3[at.b][:, q, :], front[q][:, :], ACT.Copy).then_inc(t3_ready.sem, 1)

                def finish(at):
                    act.wait_ge(pr.contracted.sem, pr.contracted.at(at))
                    act.activation(US[at.b][:, :], AS[:, :], ACT.Copy).then_inc(sums.sem, 1)
                    act.activation(UV[at.b][0:96, :], AV[0:96, :], ACT.Copy).then_inc(sums.sem, 1)
                    for h in range(2):
                        act.wait_ge(mixed.sem, mixed.at(at, h + 1))
                        act.activation(sc.U[at.b][:, 2 * h:2 * h + 2, :].rearrange("p t c -> p (t c)"),
                                       front[h][:, 0:2 * D], ACT.Copy).then_inc(sc.u_ready.sem, 1)
                    sc.act(act, at)

                def body(at):
                    if at.first():
                        start(at)
                    else:
                        finish(at.back(1))
                    if not at.last(n):
                        start(at.next())
                    else:
                        finish(at)
                walk(act, n, body)

            @block.vector
            def _(dve):
                for b in range(2):
                    dve.memset(EH[b][64:128, :].bitcast(F32), 0.0).then_inc(const, 1)
                    dve.memset(UV[b][96:97, :], 1.0).then_inc(const, 1)

                def split(at):
                    dve.wait_ge(ea_hi.sem, ea_hi.at(at))
                    dve.tensor_tensor(EH[at.b][32:64, :], EA[at.b][32:64, :], EH[at.b][32:64, :].bitcast(F32),
                                      ALU.subtract).then_inc(rest.sem, 1)
                    dve.wait_ge(x_ready.sem, x_ready.at(at, 2))
                    dve.tensor_tensor(XH[at.b][64:128, :], XS[at.b][64:128, :], XH[at.b][64:128, :].bitcast(F32),
                                      ALU.subtract).then_inc(rest.sem, 1)

                def body(at):
                    if at.first():
                        split(at)
                        dve.wait_ge(x_ready.sem, x_ready.at(at, 3))
                    dve.wait_ge(x_ready.sem, x_ready.at(at))
                    dve.wait_ge(t3_ready.sem, t3_ready.at(at))
                    for s, (r, _, other, _, _, _, _) in enumerate(sources):
                        dve.wait_ge(pr.filled.sem, pr.filled.at(at, s + 1))
                        k = pr.tile_read(s)
                        if k > 0 or at.has(1):
                            dve.wait_ge(pr.contracted.sem, pr.contracted.at(at, k))
                        x = other[0][at.b][0:r, :] if len(other) == 1 else other[0][at.b][0:r, other[1], :]
                        dve.tensor_tensor(pr.tile(s)[0:r, :], pr.bank(s)[0:r, :], x, ALU.mult
                                          ).then_inc(pr.multiplied.sem, 1)
                        if s == 0:
                            sc.dve(dve, at)
                        if s == 17 and not at.last(n):
                            split(at.next())
                walk(dve, n, body)

            @block.tensor
            def _(pe):
                for k, (part, m) in enumerate((("wm_s", P), ("wm_v", 97))):
                    for h in range(2):
                        ins = pe.matmul(front[k][0:m, 0:D], w[part][:, h * m:(h + 1) * m],
                                        w["wu"][:, h * D:(h + 1) * D], start=h == 0, stop=h == 1)
                    ins.then_inc(folded, 1)
                pe.wait_ge(fold_ready, 2)
                pe.wait_ge(const, 4)

                def turn(at):
                    pe.wait_ge(spread.sem, spread.at(at))
                    for k, (lo_, hi_) in enumerate(((0, P), (P, 224))):
                        for t in range(T):
                            ins = pe.transpose(front[k][0:hi_ - lo_, t * P:(t + 1) * P],
                                               XX[at.b][:, t, lo_:hi_], core.eye)
                        ins.then_inc(turned.sem, 1)

                def t3(at):
                    pe.wait_ge(x_ready.sem, x_ready.at(at))
                    pe.wait_ge(rest.sem, rest.at(at))
                    for q in range(2):
                        pe.matmul(front[q][:, :], hi["w3"][:, q * P:(q + 1) * P], XH[at.b][:, :],
                                  start=True, stop=False)
                        pe.matmul(front[q][:, :], lo["w3"][:, q * P:(q + 1) * P], XH[at.b][:, :],
                                  start=False, stop=True).then_inc(t3_done.sem, 1)

                def mix(at, after):
                    pe.wait_ge(t3_ready.sem, t3_ready.at(after))
                    pe.wait_ge(sums.sem, sums.at(at))
                    for t in range(T):
                        o = front[t // 2][:, (t % 2) * D:(t % 2 + 1) * D]
                        pe.matmul(o, US[at.b][:, t * P:(t + 1) * P], fold_s[:, :], start=True, stop=False)
                        ins = pe.matmul(o, UV[at.b][:, t * P:(t + 1) * P], fold_v[:, :], start=False, stop=True)
                        if t % 2:
                            ins.then_inc(mixed.sem, 1)

                def body(at):
                    if at.first():
                        turn(at)
                        t3(at)
                    for s in range(pr.ns + pr.lag):
                        if s < pr.ns:
                            _, sel, _, lhs, _, _, _ = sources[s]
                            k = pr.bank_read(s)
                            if k > 0 or at.has(1):
                                pe.wait_ge(pr.multiplied.sem, pr.multiplied.at(at, k))
                            m = lhs.shape[0]
                            pe.matmul(pr.bank(s)[0:m, :], hi["gather"][:, sel * P:sel * P + m], EH[at.b][:, :],
                                      start=True, stop=True).then_inc(pr.filled.sem, 1)
                        m = s - pr.lag
                        if m == 0 and at.has(1):
                            pe.wait_ge(sums.sem, sums.at(at.back(1)))
                        if m >= 0:
                            r, _, _, lhs, acc, r0, start = sources[m]
                            pe.wait_ge(pr.multiplied.sem, pr.multiplied.at(at, m + 1))
                            pe.matmul(acc[r0:r0 + lhs.shape[1], :], lhs, pr.tile(m)[0:r, :], start=start,
                                      stop=True, skip_group_check=True).then_inc(pr.contracted.sem, 1)
                        if s == 3 and not at.first():
                            mix(at.back(1), at)
                        if s == 9 and not at.first():
                            sc.pe(pe, at.back(1))
                        if s == 14 and not at.last(n):
                            if at.first():
                                pe.wait_ge(t3_ready.sem, t3_ready.at(at))
                            else:
                                pe.wait_ge(sc.out_ready.sem, sc.out_ready.at(at.back(1)))
                            turn(at.next())
                        if s == 20 and not at.last(n):
                            t3(at.next())
                    if at.last(n):
                        if at.has(1):
                            pe.wait_ge(sc.out_ready.sem, sc.out_ready.at(at.back(1)))
                        mix(at, at)
                        sc.pe(pe, at)
                walk(pe, n, body)
def edges_conv(core, name, table, hidden_in, c1, out_table, norm):
    nc, d, n = core.nc, core.d, core.edge_groups
    width = AW if norm else D
    n_out = D + 1 if norm else D
    k96, l2 = 1 / np.sqrt(96), PACKS[name]["l2"][1]
    c_l2 = 1.0 if norm else float(np.cos(np.pi / 8) / (np.sqrt(8.0) * np.sqrt(96.0)))
    with ExitStack() as ctx:
        W, w, hi, _ = load_pack(core, ctx, name,
                                feature_scales("l1", 288) + [
                                    ("fc2", 0, P, 0, 192, 1 / 8 if norm else 1 / 10),
                                    ("l2", 0, 64, 0, AW, c_l2), ("l2", 64, 96, 0, AW, c_l2 / np.sqrt(3.0)),
                                    ("l2", 0, 96, AW, 4 * AW, c_l2)],
                                {"gather": False})
        AT = [sbuf(nc, ctx, f"{name}_at{b}", [P, GR]) for b in range(2)]
        AH = [sbuf(nc, ctx, f"{name}_ah{b}", [P, GR], F32R) for b in range(2)]
        XT = [sbuf(nc, ctx, f"{name}_xt{b}", [HALF, 2, GR]) for b in range(2)]
        HN = [sbuf(nc, ctx, f"{name}_hn{b}", [P, T, D]) for b in range(2)] if norm else None
        HS = [sbuf(nc, ctx, f"{name}_hs{b}", [P, GR]) for b in range(2)]
        WW = [sbuf(nc, ctx, f"{name}_ww{b}", [96, 2, GR]) for b in range(2)]
        PQ = [sbuf(nc, ctx, f"{name}_pq{i}", [96, 2, GR]) for i in range(2)]
        SV = [sbuf(nc, ctx, f"{name}_sv{b}", [96, 6, GR]) for b in range(2)]
        front = banks(nc, ctx, f"{name}_front", 2)
        mlp, = banks(nc, ctx, f"{name}_mlp", 1)
        EB = banks(nc, ctx, f"{name}_eb", 2)
        GB = banks(nc, ctx, f"{name}_gb", 2)

        ga = Gather(core, ctx, name, table, "src")
        gz = Gather(core, ctx, name + "z", "Z", "src" if norm else "dst", 1)
        sc = Scatter(core, ctx, name, out_table, "dst", width, front)
        at_in = core.moves(f"{name}_at_in", 3)
        at_hi = core.count(f"{name}_at_hi", 1)
        at_lo = core.count(f"{name}_at_lo", 1)
        turned = core.count(f"{name}_turned", 2)
        x_ready = core.count(f"{name}_x_ready", 2)
        gated = core.count(f"{name}_gated", 3)
        gate_out = core.count(f"{name}_gate_out", 3)
        filled = core.count(f"{name}_filled", 9)
        made = core.count(f"{name}_made", 12)
        mixed = core.count(f"{name}_mixed", 2)
        const = core.sem(f"{name}_const")
        if norm:
            st = [sbuf(nc, ctx, f"{name}_st{b}", [P, T, 6]) for b in range(2)]
            mv = [sbuf(nc, ctx, f"{name}_mv{b}", [P, T, 2]) for b in range(2)]
            sd = [sbuf(nc, ctx, f"{name}_sd{b}", [P, T]) for b in range(2)]
            rs = [sbuf(nc, ctx, f"{name}_rs{b}", [P, T]) for b in range(2)]
            eps = sbuf(nc, ctx, f"{name}_eps", [P, 1])
            stats = core.count(f"{name}_stats", T)
            means = core.count(f"{name}_means", T)
            std = core.count(f"{name}_std", 1)
            inv = core.count(f"{name}_inv", 1)
            centred = core.count(f"{name}_centred", T)
            h_ready = core.count(f"{name}_h_ready", T)

        with nc.Block() as block:
            @block.gpsimd
            def _(pool):
                def body(at):
                    if at.first():
                        ga.pool(pool, at)
                        gz.pool(pool, at)
                    if not at.last(n):
                        if norm:
                            if at.has(1):
                                pool.wait_ge(h_ready.sem, h_ready.at(at.back(1)))
                            apart(core, pool, at)
                        else:
                            if at.has(1):
                                pool.wait_ge(turned.sem, turned.at(at.back(1)))
                            apart(core, pool, at)
                        ga.pool(pool, at.next())
                        if not norm:
                            if at.has(1):
                                pool.wait_ge(sc.u_ready.sem, sc.u_ready.at(at.back(1)))
                            apart(core, pool, at)
                        gz.pool(pool, at.next())
                    if not at.first():
                        sc.pool(pool, at.back(1))
                    if at.last(n):
                        sc.pool(pool, at)
                        for q in (at, at.back(1)):
                            pool.wait_ge(sc.added.of(q), sc.added.at(q))
                            apart(core, pool, q)
                walk(pool, n, body)

            @block.sync
            def _(sp):
                sp.wait_ge(const, 2)

                def body(at):
                    if at.has(2):
                        sp.wait_ge(at_lo.sem, at_lo.at(at.back(2)))
                    if at.has(2):
                        sp.wait_ge(gated.sem, gated.at(at.back(2), 1))
                    cols = bass.ds(at.g * GR, GR)
                    k = d[hidden_in].shape[0]
                    sp.dma_start(AT[at.b][0:k, :], d[hidden_in][:, cols]).then_inc(at_in.of(at), 16)
                    for r0 in (32, 64):
                        sp.dma_start(AT[at.b][r0:r0 + 4, :], d["ea4"][:, cols]).then_inc(at_in.of(at), 16)
                    sc.sp(sp, at)
                walk(sp, n, body)

            @block.scalar
            def _(act):
                act.wait_ge(const, 5 if norm else 2)

                def root(at):
                    if norm:
                        act.wait_ge(means.sem, means.at(at))
                        act.activation(sd[at.b][:, :], mv[at.b][:, :, 1], ACT.Sqrt, bias=eps[:, 0:1]
                                       ).then_inc(std.sem, 1)

                def start(at):
                    act.wait_ge(at_in.of(at), at_in.at(at))
                    act.activation(AH[at.b][:, :], AT[at.b][:, :], ACT.Copy).then_inc(at_hi.sem, 1)
                    act.wait_ge(gated.sem, gated.at(at, 1))
                    act.activation(HS[at.b][:, :], mlp[:, :], ACT.Silu, scale=float(c1)).then_inc(gate_out.sem, 1)
                    act.wait_ge(gated.sem, gated.at(at, 2))
                    act.activation(WW[at.b][:, 0, :], mlp[0:96, :], ACT.Copy).then_inc(gate_out.sem, 1)
                    for h in range(2):
                        act.wait_ge(turned.sem, turned.at(at, h + 1))
                        act.activation(XT[at.b][:, h, :], front[h][0:HALF, :], ACT.Copy).then_inc(x_ready.sem, 1)
                    act.wait_ge(gated.sem, gated.at(at, 3))
                    act.activation(WW[at.b][:, 1, :], mlp[0:96, :], ACT.Copy).then_inc(gate_out.sem, 1)

                def finish(at):
                    for h in range(2):
                        act.wait_ge(mixed.sem, mixed.at(at, h + 1))
                        if norm:
                            act.activation(sc.U[at.b][:, 2 * h:2 * h + 2, 0:n_out],
                                           front[h][:, 0:2 * n_out].rearrange("p (t c) -> p t c", t=2), ACT.Copy
                                           ).then_inc(sc.u_ready.sem, 1)
                        else:
                            for t in (2 * h, 2 * h + 1):
                                act.wait_ge(gz.here.of(at), gz.here.at(at))
                                ins = act.activation(sc.U[at.b][:, t, :], front[h][:, (t % 2) * D:(t % 2 + 1) * D],
                                                     ACT.Copy, scale=gz.rows[at.b][:, t, 0:1])
                            ins.then_inc(sc.u_ready.sem, 1)
                    sc.act(act, at)

                def body(at):
                    if at.first():
                        root(at)
                        start(at)
                    if not at.last(n):
                        root(at.next())
                    if not at.first():
                        finish(at.back(1))
                    if not at.last(n):
                        start(at.next())
                    else:
                        finish(at)
                walk(act, n, body)

            @block.vector
            def _(dve):
                for b in range(2):
                    dve.memset(AT[b][:, :], 0.0).then_inc(const, 1)
                if norm:
                    dve.memset(eps[:, :], EPS).then_inc(const, 1)
                    for b in range(2):
                        dve.memset(sc.U[b][:, :, D + 1:AW], 1.0).then_inc(const, 1)

                def statistics(at):
                    if norm:
                        dve.wait_ge(ga.here.of(at), ga.here.at(at))
                        if at.has(2):
                            dve.wait_ge(std.sem, std.at(at.back(2)))
                        for t in range(T):
                            dve.bn_stats(st[at.b][:, t, :], ga.rows[at.b][:, t, :]).then_inc(stats.sem, 1)
                        for t in range(T):
                            dve.wait_ge(stats.sem, stats.at(at, t + 1))
                            apart(core, dve, at)
                            dve.bn_aggr(mv[at.b][:, t, :], st[at.b][:, t, :]).then_inc(means.sem, 1)

                def prepare(at):
                    if norm:
                        dve.wait_ge(std.sem, std.at(at))
                        dve.reciprocal(rs[at.b][:, :], sd[at.b][:, :]).then_inc(inv.sem, 1)
                        dve.wait_ge(inv.sem, inv.at(at))
                        if at.has(2):
                            dve.wait_ge(turned.sem, turned.at(at.back(2)))
                        for t in range(T):
                            dve.tensor_scalar(HN[at.b][:, t, :], ga.rows[at.b][:, t, :], mv[at.b][:, t, 0:1],
                                              rs[at.b][:, t:t + 1], ALU.subtract, ALU.mult
                                              ).then_inc(centred.sem, 1)
                        dve.wait_ge(gz.here.of(at), gz.here.at(at))
                        for t in range(T):
                            dve.wait_ge(centred.sem, centred.at(at, t + 1))
                            dve.tensor_scalar(HN[at.b][:, t, :], HN[at.b][:, t, :], 0.0, gz.rows[at.b][:, t, :],
                                              ALU.max, ALU.mult).then_inc(h_ready.sem, 1)
                    dve.wait_ge(at_hi.sem, at_hi.at(at))
                    dve.tensor_tensor(AH[at.b][64:96, :], AT[at.b][64:96, :], AH[at.b][64:96, :].bitcast(F32),
                                      ALU.subtract).then_inc(at_lo.sem, 1)

                def products(at):
                    dve.wait_ge(gate_out.sem, gate_out.at(at))
                    if at.has(2):
                        dve.wait_ge(mixed.sem, mixed.at(at.back(2)))
                    for m in range(3):
                        t = PQ[m % 2]
                        for q in range(2):
                            dve.wait_ge(filled.sem, filled.at(at, 3 * m + 2 + q))
                            if m < 2 and at.has(1):
                                dve.wait_ge(made.sem, made.at(at.back(1), 12 - 4 * m))
                            if m == 2:
                                dve.wait_ge(made.sem, made.at(at, 4))
                            dve.tensor_tensor(t[:, q, :], WW[at.b][:, q, :], GB[q][0:96, :], ALU.mult
                                              ).then_inc(made.sem, 1)
                        for q in range(2):
                            dve.wait_ge(made.sem, made.at(at, 4 * m + 1 + q))
                            dve.wait_ge(filled.sem, filled.at(at, 3 * m + 1))
                            dve.tensor_tensor(SV[at.b][:, 3 * q + m, :], t[:, q, :], EB[m % 2][0:96, :], ALU.mult
                                              ).then_inc(made.sem, 1)

                def body(at):
                    if at.first():
                        statistics(at)
                        prepare(at)
                    sc.dve(dve, at)
                    if not at.last(n):
                        statistics(at.next())
                    products(at)
                    if not at.last(n):
                        prepare(at.next())
                walk(dve, n, body)

            @block.tensor
            def _(pe):
                pe.wait_ge(const, 2)

                def turn(at):
                    if norm:
                        pe.wait_ge(h_ready.sem, h_ready.at(at))
                    else:
                        pe.wait_ge(ga.here.of(at), ga.here.at(at))
                    src = HN[at.b] if norm else ga.rows[at.b]
                    for h in range(2):
                        for t in range(T):
                            ins = pe.transpose(front[h][0:HALF, t * P:(t + 1) * P],
                                               src[:, t, h * HALF:(h + 1) * HALF], core.eye)
                        ins.then_inc(turned.sem, 1)

                def gates(at, k):
                    if k == 0:
                        pe.wait_ge(at_in.of(at), at_in.at(at))
                        if at.has(1):
                            pe.wait_ge(gate_out.sem, gate_out.at(at.back(1)))
                        pe.matmul(mlp[:, :], w["fc1"], AT[at.b][:, :], start=True, stop=True
                                  ).then_inc(gated.sem, 1)
                    else:
                        pe.wait_ge(gate_out.sem, gate_out.at(at, k))
                        pe.matmul(mlp[0:96, :], w["fc2"][:, (k - 1) * 96:k * 96], HS[at.b][:, :],
                                  start=True, stop=True).then_inc(gated.sem, 1)

                def fill(at, m):
                    if m == 2:
                        pe.wait_ge(made.sem, made.at(at, 4))
                    elif at.has(1):
                        pe.wait_ge(made.sem, made.at(at.back(1), 12 - 4 * m))
                    for h in range(2):
                        ins = pe.matmul(EB[m % 2][0:96, :], w["l1"][:, h * 288 + m * 96:h * 288 + (m + 1) * 96],
                                        XT[at.b][:, h, :], start=h == 0, stop=h == 1)
                    ins.then_inc(filled.sem, 1)
                    for q in range(2):
                        k = 4 * (m - 1) + 1 + q
                        if k > 0 or at.has(1):
                            pe.wait_ge(made.sem, made.at(at, k))
                        k = 3 * q + m
                        pe.matmul(GB[q][0:96, :], hi["gather"][:, k * 96:(k + 1) * 96], AH[at.b][:, :],
                                  start=True, stop=True).then_inc(filled.sem, 1)

                def mix(at):
                    pe.wait_ge(made.sem, made.at(at))
                    for t in range(T):
                        for k in range(6):
                            part = 1 + k if k < 3 else 0
                            ins = pe.matmul(front[t // 2][:, (t % 2) * n_out:(t % 2 + 1) * n_out],
                                            SV[at.b][:, k, t * P:(t + 1) * P],
                                            w["l2"][:, part * AW:part * AW + n_out], start=k == 0, stop=k == 5)
                        if t % 2:
                            ins.then_inc(mixed.sem, 1)

                def body(at):
                    if at.first():
                        turn(at)
                        for k in range(3):
                            gates(at, k)
                    pe.wait_ge(at_lo.sem, at_lo.at(at))
                    pe.wait_ge(x_ready.sem, x_ready.at(at))
                    fill(at, 0)
                    if not at.last(n):
                        gates(at.next(), 0)
                    if not at.first():
                        mix(at.back(1))
                    fill(at, 1)
                    if not at.first():
                        sc.pe(pe, at.back(1))
                    fill(at, 2)
                    if not at.last(n):
                        gates(at.next(), 1)
                        if not at.first():
                            if at.has(1):
                                pe.wait_ge(sc.out_ready.sem, sc.out_ready.at(at.back(1)))
                        else:
                            pe.wait_ge(x_ready.sem, x_ready.at(at))
                        turn(at.next())
                        gates(at.next(), 2)
                    else:
                        if at.has(1):
                            pe.wait_ge(sc.out_ready.sem, sc.out_ready.at(at.back(1)))
                        mix(at)
                        sc.pe(pe, at)
                walk(pe, n, body)


def edges1(core):
    edges_conv(core, "e1", "X1", "ea16", 1 / 4, "AGG", True)


def edges2(core):
    edges_conv(core, "e2", "H", "ea12", 1 / np.sqrt(12.0), "X3", False)


def nodes1(core):
    nc, d, n, name = core.nc, core.d, core.node_groups, "n1"
    with ExitStack() as ctx:
        sin8 = float(np.sin(np.pi / 8))
        W, w, _, _ = load_pack(core, ctx, name, feature_scales("sc", D) +
                               [(p, a, b, c, e, v * sin8) for p, a, b, c, e, v in feature_scales("sc2", D)], {})
        two = lambda tag, shape: [sbuf(nc, ctx, f"n1_{tag}{b}", shape) for b in range(2)]
        X, A, Z = two("x", [P, T * D]), two("a", [P, T * AW]), two("z", [P, T])
        X2, Y, ZH = two("x2", [P, T * D]), two("y", [P, T * D]), two("zh", [P, T * D])
        cf = two("cf", [P, 5, T])
        tmp = two("tmp", [P, T * D])
        eps = sbuf(nc, ctx, "n1_eps", [P, 1])
        x_in, y_out, h_out = core.moves("n1_x_in", 3), core.moves("n1_y_out"), core.moves("n1_h_out")
        const = core.sem("n1_const")
        coef = core.count("n1_coef", 5)
        scaled = core.count("n1_scaled", T)
        summed = core.count("n1_summed", T)
        y_ready = core.count("n1_y_ready", T)
        zh_ready = core.count("n1_zh_ready", T)

        class Half:

            def __init__(self, tag):
                self.H = two(tag + "h", [P, T * D])
                self.HT = two(tag + "ht", [HALF, 2, GR])
                self.st, self.mv = two(tag + "st", [P, T, 6]), two(tag + "mv", [P, T, 2])
                self.sd, self.rs, self.nm = (two(tag + k, [P, T]) for k in ("sd", "rs", "nm"))
                self.TP, self.LP = banks(nc, ctx, f"n1_{tag}tp", 2), banks(nc, ctx, f"n1_{tag}lp", 2)
                count = lambda what, per: core.count(f"n1_{tag}_{what}", per)
                self.stats, self.means, self.std = count("stats", T), count("means", T), count("std", 1)
                self.inv, self.h_ready, self.turned = count("inv", 2), count("h_ready", T), count("turned", 2)
                self.ht_ready, self.mixed = count("ht_ready", 2), count("mixed", 2)

            def statistics(self, dve, at, x):
                if at.has(2):
                    dve.wait_ge(self.std.sem, self.std.at(at.back(2)))
                for t in range(T):
                    dve.bn_stats(self.st[at.b][:, t, :], x[at.b][:, t * D:(t + 1) * D]).then_inc(self.stats.sem, 1)
                for t in range(T):
                    dve.wait_ge(self.stats.sem, self.stats.at(at, t + 1))
                    apart(core, dve, at)
                    dve.bn_aggr(self.mv[at.b][:, t, :], self.st[at.b][:, t, :]).then_inc(self.means.sem, 1)

            def factors(self, dve, at):
                dve.wait_ge(self.std.sem, self.std.at(at))
                dve.reciprocal(self.rs[at.b][:, :], self.sd[at.b][:, :]).then_inc(self.inv.sem, 1)
                dve.wait_ge(self.inv.sem, self.inv.at(at, 1))
                dve.scalar_tensor_tensor(self.nm[at.b][:, :], self.mv[at.b][:, :, 0], -1.0, self.rs[at.b][:, :],
                                         ALU.mult, ALU.mult).then_inc(self.inv.sem, 1)

            def root(self, act, at):
                act.wait_ge(self.means.sem, self.means.at(at))
                act.activation(self.sd[at.b][:, :], self.mv[at.b][:, :, 1], ACT.Sqrt, bias=eps[:, 0:1]
                               ).then_inc(self.std.sem, 1)

            def relu(self, act, at, x):
                act.wait_ge(self.inv.sem, self.inv.at(at))
                if at.has(2):
                    act.wait_ge(self.turned.sem, self.turned.at(at.back(2)))
                for t in range(T):
                    act.activation(self.H[at.b][:, t * D:(t + 1) * D], x[at.b][:, t * D:(t + 1) * D], ACT.Relu,
                                   bias=self.nm[at.b][:, t:t + 1], scale=self.rs[at.b][:, t:t + 1]
                                   ).then_inc(self.h_ready.sem, 1)

            def copies(self, act, at):
                if at.has(2):
                    act.wait_ge(self.mixed.sem, self.mixed.at(at.back(2)))
                for h in range(2):
                    act.wait_ge(self.turned.sem, self.turned.at(at, h + 1))
                    act.activation(self.HT[at.b][:, h, :], self.TP[h][0:HALF, :], ACT.Copy
                                   ).then_inc(self.ht_ready.sem, 1)

            def turn(self, pe, at):
                if at.has(1):
                    pe.wait_ge(self.ht_ready.sem, self.ht_ready.at(at.back(1)))
                pe.wait_ge(self.h_ready.sem, self.h_ready.at(at))
                for h in range(2):
                    for t in range(T):
                        ins = pe.transpose(self.TP[h][0:HALF, t * P:(t + 1) * P],
                                           self.H[at.b][:, t * D + h * HALF:t * D + (h + 1) * HALF], core.eye)
                    ins.then_inc(self.turned.sem, 1)

            def mix(self, pe, at, lin, read):
                if at.has(1):
                    pe.wait_ge(read.sem, read.at(at.back(1)))
                pe.wait_ge(self.ht_ready.sem, self.ht_ready.at(at))
                for t in range(T):
                    for h in range(2):
                        ins = pe.matmul(self.LP[t // 2][:, (t % 2) * D:(t % 2 + 1) * D],
                                        self.HT[at.b][:, h, t * P:(t + 1) * P], lin[:, h * D:(h + 1) * D],
                                        start=h == 0, stop=h == 1)
                    if t % 2:
                        ins.then_inc(self.mixed.sem, 1)

        a, b = Half("a"), Half("b")
        rows = lambda x, at: x[bass.ds(at.g * GR, GR), :].rearrange("(p t) c -> p (t c)", t=T)

        def both(eng, step_a, step_b):
            def body(at):
                for k in range(len(step_a)):
                    step_a[k](at)
                    if not at.first():
                        step_b[k](at.back(1))
                if at.last(n):
                    for k in range(len(step_b)):
                        step_b[k](at)
            walk(eng, n, body)

        with nc.Block() as block:
            @block.sync
            def _(sp):
                def load(at):
                    if at.has(2):
                        sp.wait_ge(y_ready.sem, y_ready.at(at.back(2)))
                    if at.has(2):
                        sp.wait_ge(zh_ready.sem, zh_ready.at(at.back(2)))
                    sp.dma_start(X[at.b][:, :], rows(d["X1"], at)).then_inc(x_in.of(at), 16)
                    sp.dma_start(A[at.b][:, :], rows(d["AGG"], at)).then_inc(x_in.of(at), 16)
                    sp.dma_start(Z[at.b][:, :], rows(d["Z"], at)).then_inc(x_in.of(at), 16)

                def store(at):
                    sp.wait_ge(y_ready.sem, y_ready.at(at))
                    sp.dma_start(rows(d["X3"], at), Y[at.b][:, :]).then_inc(y_out.of(at), 16)
                    if at.last(n):
                        for q in (at, at.back(1)):
                            sp.wait_ge(y_out.of(q), y_out.at(q))
                both(sp, [load], [store])

            @block.gpsimd
            def _(pool):
                def none(at):
                    pass

                def zh(at):
                    pool.wait_ge(b.h_ready.sem, b.h_ready.at(at))
                    if at.has(2):
                        pool.wait_ge(h_out.of(at.back(2)), h_out.at(at.back(2)))
                    apart(core, pool, at)
                    for t in range(T):
                        pool.tensor_scalar(ZH[at.b][:, t * D:(t + 1) * D], b.H[at.b][:, t * D:(t + 1) * D],
                                           Z[at.b][:, t:t + 1], None, ALU.mult).then_inc(zh_ready.sem, 1)
                    pool.wait_ge(zh_ready.sem, zh_ready.at(at))
                    apart(core, pool, at)
                    pool.dma_start(rows(d["H"], at), ZH[at.b][:, :]).then_inc(h_out.of(at), 16)
                    if at.last(n):
                        for q in (at, at.back(1)):
                            pool.wait_ge(h_out.of(q), h_out.at(q))
                            apart(core, pool, q)
                both(pool, [none], [zh])

            @block.scalar
            def _(act):
                act.wait_ge(const, 1)

                def relu_a(at):
                    a.relu(act, at, X)

                def relu_b(at):
                    if at.has(2):
                        act.wait_ge(zh_ready.sem, zh_ready.at(at.back(2)))
                    b.relu(act, at, X2)
                both(act, [lambda at: a.root(act, at), relu_a, lambda at: a.copies(act, at)],
                     [lambda at: b.root(act, at), relu_b, lambda at: b.copies(act, at)])

            @block.vector
            def _(dve):
                dve.memset(eps[:, :], EPS).then_inc(const, 1)
                col = lambda x, at, c: x[at.b][:, :].rearrange("p (t c) -> p t c", t=T)[:, :, c]

                def front_a(at):
                    dve.wait_ge(x_in.of(at), x_in.at(at))
                    a.statistics(dve, at, X)
                    f = cf[at.b]
                    dve.tensor_scalar(f[:, 0, :], col(A, at, D + 1), 1.0, None, ALU.max).then_inc(coef.sem, 1)
                    dve.wait_ge(coef.sem, coef.at(at, 1))
                    dve.reciprocal(f[:, 1, :], f[:, 0, :]).then_inc(coef.sem, 1)
                    dve.wait_ge(coef.sem, coef.at(at, 2))
                    dve.tensor_tensor(f[:, 2, :], f[:, 1, :], Z[at.b][:, :], ALU.mult).then_inc(coef.sem, 1)
                    dve.wait_ge(coef.sem, coef.at(at, 3))
                    dve.scalar_tensor_tensor(f[:, 3, :], f[:, 2, :], 1 / 96, f[:, 2, :], ALU.mult, ALU.mult
                                             ).then_inc(coef.sem, 1)
                    dve.wait_ge(coef.sem, coef.at(at, 4))
                    dve.tensor_tensor(f[:, 4, :], f[:, 3, :], col(A, at, D), ALU.mult).then_inc(coef.sem, 1)

                def front_b(at):
                    dve.wait_ge(summed.sem, summed.at(at))
                    b.statistics(dve, at, X2)

                def sum_a(at):
                    dve.wait_ge(coef.sem, coef.at(at))
                    for t in range(T):
                        dve.scalar_tensor_tensor(tmp[at.b][:, t * D:(t + 1) * D], A[at.b][:, t * AW:t * AW + D],
                                                 cf[at.b][:, 4, t:t + 1], X[at.b][:, t * D:(t + 1) * D],
                                                 ALU.mult, ALU.add).then_inc(scaled.sem, 1)
                    for t in range(T):
                        dve.wait_ge(a.mixed.sem, a.mixed.at(at, t // 2 + 1))
                        dve.wait_ge(scaled.sem, scaled.at(at, t + 1))
                        dve.scalar_tensor_tensor(X2[at.b][:, t * D:(t + 1) * D],
                                                 a.LP[t // 2][:, (t % 2) * D:(t % 2 + 1) * D],
                                                 Z[at.b][:, t:t + 1], tmp[at.b][:, t * D:(t + 1) * D],
                                                 ALU.mult, ALU.add).then_inc(summed.sem, 1)

                def sum_b(at):
                    if at.has(2):
                        dve.wait_ge(y_out.of(at.back(2)), y_out.at(at.back(2)))
                    for t in range(T):
                        dve.wait_ge(b.mixed.sem, b.mixed.at(at, t // 2 + 1))
                        dve.scalar_tensor_tensor(Y[at.b][:, t * D:(t + 1) * D],
                                                 b.LP[t // 2][:, (t % 2) * D:(t % 2 + 1) * D],
                                                 Z[at.b][:, t:t + 1], X2[at.b][:, t * D:(t + 1) * D],
                                                 ALU.mult, ALU.add).then_inc(y_ready.sem, 1)

                both(dve, [front_a, lambda at: a.factors(dve, at), sum_a],
                     [front_b, lambda at: b.factors(dve, at), sum_b])

            @block.tensor
            def _(pe):
                both(pe, [lambda at: a.turn(pe, at), lambda at: a.mix(pe, at, w["sc"], summed)],
                     [lambda at: b.turn(pe, at), lambda at: b.mix(pe, at, w["sc2"], y_ready)])


def edges3(core):
    nc, d, n, name = core.nc, core.d, core.edge_groups, "e3"
    YW = 2 * D + V
    with ExitStack() as ctx:
        yc = [("y", 0, 64, 0, YW, 1 / 8), ("y", 64, 96, 0, YW, 1 / np.sqrt(32.0)),
              ("y", 0, 64, YW, 2 * YW, 1 / np.sqrt(32.0)), ("y", 64, 96, YW, 2 * YW, 1 / np.sqrt(96.0))]
        W, w, hi, lo = load_pack(core, ctx, name, yc + [
            ("ss", 0, P, 0, 32 * S, 1 / 64), ("vv", 0, P, 0, 8 * S, 1 / (np.sqrt(3.0) * 32)),
            ("sv", 0, P, 0, 8 * P, 1 / np.sqrt(2048.0)), ("vs", 0, P, 0, 8 * P, 1 / np.sqrt(2048.0))],
            {"sv": True, "vs": True, "pick_s": False, "pick_v": False})
        two = lambda tag, shape, dt=F32: [sbuf(nc, ctx, f"e3_{tag}{b}", shape, dt) for b in range(2)]
        one = lambda tag, shape, dt=F32: sbuf(nc, ctx, f"e3_{tag}", shape, dt)
        ED = two("ed", [P, T * 4])
        RV = one("rv", [P, T, 96])
        GD = one("gd", [P, T, 96])
        XD = one("xd", [96, 2, GR])
        A = one("a", [P, T, D])
        AR = one("ar", [P, T, 96])
        XA = one("xa", [P, T, 4 * P])
        XX = one("xx", [P, T, 4 * P])
        A0, XS = two("a0", [P, GR]), one("xs", [P, GR])
        A1, XV = two("a1", [P, 3, GR]), two("xv", [P, 3, GR])
        A0H, XSH = two("a0h", [P, GR], F32R), two("xsh", [P, GR], F32R)
        XVH = two("xvh", [P, 3, GR], F32R)
        US, UV = one("us", [P, GR]), one("uv", [96, GR])
        front = banks(nc, ctx, "e3_front", 3)
        ring = banks(nc, ctx, "e3_ring", 3)
        AS, AV = banks(nc, ctx, "e3_acc", 2)

        gs, gd = Gather(core, ctx, "e3s", "H", "src"), Gather(core, ctx, "e3d", "H", "dst")
        sc = Scatter(core, ctx, name, "OUT", "src", D, [front[2], front[0]])
        ed_in = core.moves("e3_ed_in")
        vr = core.count("e3_vr", T)
        gd_ready = core.count("e3_gd_ready", 2)
        turned_d = core.count("e3_turned_d", 2)
        xd_ready = core.count("e3_xd_ready", 2)
        y_done = core.count("e3_y_done", T)
        a_scaled = core.count("e3_a_scaled", T)
        a_added = core.count("e3_a_added", 2 * T)
        a_ready = core.count("e3_a_ready", 1)
        spread = core.count("e3_spread", 8)
        turned = core.count("e3_turned", 8)
        out = core.count("e3_turned_out", 8)
        high = core.count("e3_high", 5)
        rest = core.count("e3_rest", 5)
        sums = core.count("e3_sums", 2)
        mixed = core.count("e3_mixed", 2)
        const = core.sem("e3_const")

        picked, applied = [], []
        for c in range(32):
            picked.append((("pick_s", c, XSH, None),
                           [(A0, None, w["ss"][:, c * S:(c + 1) * S], AS, 64 * (c % 2), c < 2)]))
        for c in range(8):
            for i in range(3):
                picked.append((("pick_v", c, XVH, i),
                               [(A1, i, w["vv"][:, c * S:(c + 1) * S], AS, 64 * ((c + i) % 2), False)]))
        for c in range(8):
            for part, rhs, other in (("sv", XSH, A1), ("vs", A0H, XV)):
                applied.append(((part, c, rhs, None),
                                [(other, i, w["sum"][:, c * V:(c + 1) * V], AV, 32 * i,
                                  c == 0 and part == "sv") for i in range(3)]))
        sources = []
        for c in range(8):
            sources += picked[7 * c:7 * c + 3] + [applied[2 * c]] + picked[7 * c + 3:7 * c + 7] + [applied[2 * c + 1]]
        part_of = lambda x, at, i: x[at.b][:, :] if i is None else x[at.b][:, i, :]
        pr = Plan(core, ctx, name, [len(x[1]) for x in sources], ring, 4, 2)

        with nc.Block() as block:
            @block.gpsimd
            def _(pool):
                def v_r(at):
                    pool.wait_ge(gd.here.of(at), gd.here.at(at))
                    pool.wait_ge(ed_in.of(at), ed_in.at(at))
                    if at.has(1):
                        pool.wait_ge(gd_ready.sem, gd_ready.at(at.back(1)))
                    apart(core, pool, at)
                    for t in range(T):
                        pool.tensor_tensor(RV[:, t, :].rearrange("p (u i) -> p u i", i=3),
                                           gd.rows[at.b][:, t, S:D].rearrange("p (u i) -> p u i", i=3),
                                           ED[at.b][:, 4 * t:4 * t + 3].unsqueeze(1).broadcast_to([P, V, 3]),
                                           ALU.mult).then_inc(vr.sem, 1)

                def body(at):
                    if at.first():
                        gd.pool(pool, at)
                        gs.pool(pool, at)
                        v_r(at)
                    if not at.last(n):
                        if at.has(1):
                            pool.wait_ge(turned_d.sem, turned_d.at(at.back(1)))
                        apart(core, pool, at)
                        gd.pool(pool, at.next())
                        if at.has(1):
                            pool.wait_ge(spread.sem, spread.at(at.back(1)))
                        apart(core, pool, at)
                        gs.pool(pool, at.next())
                        v_r(at.next())
                    if not at.first():
                        sc.pool(pool, at.back(1))
                    if at.last(n):
                        sc.pool(pool, at)
                        for q in (at, at.back(1)):
                            pool.wait_ge(sc.added.of(q), sc.added.at(q))
                            apart(core, pool, q)
                walk(pool, n, body)

            @block.sync
            def _(sp):
                def body(at):
                    if at.has(2):
                        sp.wait_ge(a_ready.sem, a_ready.at(at.back(2)))
                    sp.dma_start(ED[at.b][:, :], d["ea4_cols"][:, bass.ds(at.g * (4 * T), 4 * T)]
                                 ).then_inc(ed_in.of(at), 16)
                    sc.sp(sp, at)
                walk(sp, n, body)

            @block.scalar
            def _(act):
                act.wait_ge(const, 2)

                def spread_out(at, src, x, k0):
                    act.activation(x[:, :, 0:P].rearrange("p t (r a) -> p t r a", r=2),
                                   src[:, :, 0:S].unsqueeze(2).broadcast_to([P, T, 2, S]), ACT.Copy
                                   ).then_inc(spread.sem, 1)
                    for i in range(3):
                        v = src[:, :, S:D].rearrange("p t (u i) -> p t u i", i=3)[:, :, :, i]
                        act.activation(x[:, :, (1 + i) * P:(2 + i) * P].rearrange("p t (r u) -> p t r u", r=4),
                                       v.unsqueeze(2).broadcast_to([P, T, 4, V]), ACT.Copy
                                       ).then_inc(spread.sem, 1)

                def start(at):
                    act.wait_ge(gd.here.of(at), gd.here.at(at))
                    if at.has(1):
                        act.wait_ge(turned_d.sem, turned_d.at(at.back(1)))
                    act.activation(GD[:, :, 0:S], gd.rows[at.b][:, :, 96:D], ACT.Copy).then_inc(gd_ready.sem, 1)
                    act.wait_ge(gs.here.of(at), gs.here.at(at))
                    spread_out(at, gs.rows[at.b], XX, 0)
                    for h in range(2):
                        act.wait_ge(turned_d.sem, turned_d.at(at, h + 1))
                        act.activation(XD[:, h, :], front[(4 + h) % 3][0:96, :], ACT.Copy).then_inc(xd_ready.sem, 1)
                    for t in range(T):
                        act.wait_ge(y_done.sem, y_done.at(at, t + 1))
                        act.activation(A[:, t, :], front[t % 3][:, D:2 * D], ACT.Copy,
                                       scale=ED[at.b][:, 4 * t + 3:4 * t + 4]).then_inc(a_scaled.sem, 1)
                    targets = [XS[:, :]] + [XV[at.b][:, i, :] for i in range(3)] + \
                              [A0[at.b][:, :]] + [A1[at.b][:, i, :] for i in range(3)]
                    for k in range(8):
                        if k == 4:
                            act.wait_ge(a_ready.sem, a_ready.at(at))
                            spread_out(at, A, XA, 4)
                        act.wait_ge(turned.sem, turned.at(at, k + 1))
                        act.activation(targets[k], front[(10 + k) % 3][:, :], ACT.Copy).then_inc(out.sem, 1)
                        if k < 5:
                            h = (XSH[at.b][:, :], XVH[at.b][0:64, 0, :], XVH[at.b][0:64, 1, :],
                                 XVH[at.b][0:64, 2, :], A0H[at.b][:, :])[k]
                            act.wait_ge(out.sem, out.at(at, k + 1))
                            act.activation(h, targets[k][0:h.shape[0], :], ACT.Copy).then_inc(high.sem, 1)

                def finish(at):
                    act.wait_ge(pr.contracted.sem, pr.contracted.at(at))
                    act.activation(US[:, :], AS[:, :], ACT.Copy).then_inc(sums.sem, 1)
                    act.activation(UV[:, :], AV[0:96, :], ACT.Copy).then_inc(sums.sem, 1)
                    for h in range(2):
                        act.wait_ge(mixed.sem, mixed.at(at, h + 1))
                        act.activation(sc.U[at.b][:, 2 * h:2 * h + 2, :].rearrange("p t c -> p (t c)"),
                                       front[h][:, 0:2 * D], ACT.Copy).then_inc(sc.u_ready.sem, 1)
                    sc.act(act, at)

                def body(at):
                    if at.first():
                        start(at)
                    else:
                        finish(at.back(1))
                    if not at.last(n):
                        start(at.next())
                    else:
                        finish(at)
                walk(act, n, body)

            @block.vector
            def _(dve):
                for b in range(2):
                    dve.memset(XVH[b][64:128, :, :].bitcast(F32), 0.0).then_inc(const, 1)

                def dot(at):
                    dve.wait_ge(vr.sem, vr.at(at))
                    if at.has(1):
                        dve.wait_ge(turned_d.sem, turned_d.at(at.back(1)))
                    dve.tensor_reduce(GD[:, :, S:96], RV[:, :, :].rearrange("p t (u i) -> p t u i", i=3),
                                      AX.X, ALU.add).then_inc(gd_ready.sem, 1)

                def message(at, tiles):
                    for t in tiles:
                        dve.wait_ge(a_scaled.sem, a_scaled.at(at, t + 1))
                        dve.tensor_tensor(A[:, t, :], front[t % 3][:, 0:D], A[:, t, :], ALU.add
                                          ).then_inc(a_added.sem, 1)
                        dve.tensor_tensor(AR[:, t, :].rearrange("p (w i) -> p w i", i=3),
                                          over(front[t % 3][:, 2 * D:YW], 3),
                                          ED[at.b][:, 4 * t:4 * t + 3].unsqueeze(1).broadcast_to([P, V, 3]),
                                          ALU.mult).then_inc(a_added.sem, 1)
                    if T - 1 not in tiles:
                        return
                    dve.wait_ge(a_added.sem, a_added.at(at))
                    dve.tensor_tensor(A[:, :, S:D], A[:, :, S:D], AR[:, :, :], ALU.add).then_inc(a_ready.sem, 1)

                def remainders(at, ks):
                    pairs = [(XSH[at.b][64:128, :], XS[64:128, :])] + \
                            [(XVH[at.b][32:64, i, :], XV[at.b][32:64, i, :]) for i in range(3)] + \
                            [(A0H[at.b][64:128, :], A0[at.b][64:128, :])]
                    for k in ks:
                        dve.wait_ge(high.sem, high.at(at, k + 1))
                        dve.tensor_tensor(pairs[k][0], pairs[k][1], pairs[k][0].bitcast(F32), ALU.subtract
                                          ).then_inc(rest.sem, 1)

                def body(at):
                    if at.first():
                        dot(at)
                        message(at, range(T))
                        remainders(at, range(5))
                    dve.wait_ge(out.sem, out.at(at))
                    for s, (_, products) in enumerate(sources):
                        dve.wait_ge(pr.filled.sem, pr.filled.at(at, s + 1))
                        for j, (other, i, _, _, _, _) in enumerate(products):
                            m = pr.first[s] + j
                            k = pr.tile_read(m)
                            if k > 0 or at.has(1):
                                dve.wait_ge(pr.contracted.sem, pr.contracted.at(at, k))
                            dve.tensor_tensor(pr.tile(m)[:, :], pr.bank(s)[:, :], part_of(other, at, i), ALU.mult
                                              ).then_inc(pr.multiplied.sem, 1)
                        if s == 1:
                            sc.dve(dve, at)
                        if not at.last(n):
                            if s == 18:
                                dot(at.next())
                            if s == 30:
                                message(at.next(), (0, 1, 2))
                            if s == 34:
                                message(at.next(), (3,))
                            if s == 46:
                                remainders(at.next(), range(4))
                            if s == 64:
                                remainders(at.next(), range(4, 5))
                walk(dve, n, body)

            @block.tensor
            def _(pe):
                pe.wait_ge(const, 2)

                def turn_d(at):
                    if at.has(2):
                        pe.wait_ge(sc.out_ready.sem, sc.out_ready.at(at.back(2)))
                    if at.has(1):
                        pe.wait_ge(out.sem, out.at(at.back(1)))
                    pe.wait_ge(gd_ready.sem, gd_ready.at(at))
                    pe.wait_ge(gd.here.of(at), gd.here.at(at))
                    for h in range(2):
                        for t in range(T):
                            src = gd.rows[at.b][:, t, 0:96] if h == 0 else GD[:, t, :]
                            ins = pe.transpose(front[(4 + h) % 3][0:96, t * P:(t + 1) * P], src, core.eye)
                        ins.then_inc(turned_d.sem, 1)

                def message(at, tiles):
                    pe.wait_ge(xd_ready.sem, xd_ready.at(at))
                    for t in tiles:
                        if t == 3:
                            pe.wait_ge(a_added.sem, a_added.at(at, 2))
                        for h in range(2):
                            ins = pe.matmul(front[t % 3][:, 0:YW], XD[:, h, t * P:(t + 1) * P],
                                            w["y"][:, h * YW:(h + 1) * YW], start=h == 0, stop=h == 1)
                        ins.then_inc(y_done.sem, 1)

                def turn(at, ks):
                    for k in ks:
                        if k < 3:
                            pe.wait_ge(a_added.sem, a_added.at(at, 2 * (k + 2)))
                        else:
                            pe.wait_ge(out.sem, out.at(at, k - 2))
                        pe.wait_ge(spread.sem, spread.at(at, k + 1))
                        x = XX if k < 4 else XA
                        for t in range(T):
                            ins = pe.transpose(front[(10 + k) % 3][:, t * P:(t + 1) * P],
                                               x[:, t, (k % 4) * P:(k % 4 + 1) * P], core.eye)
                        ins.then_inc(turned.sem, 1)

                def mix(at, after):
                    pe.wait_ge(out.sem, out.at(after))
                    pe.wait_ge(sums.sem, sums.at(at))
                    for t in range(T):
                        o = front[t // 2][:, (t % 2) * D:(t % 2 + 1) * D]
                        pe.matmul(o, US[:, t * P:(t + 1) * P], w["out_s"], start=True, stop=False)
                        ins = pe.matmul(o, UV[:, t * P:(t + 1) * P], w["out_v"], start=False, stop=True)
                        if t % 2:
                            ins.then_inc(mixed.sem, 1)

                def body(at):
                    if at.first():
                        turn_d(at)
                        message(at, range(T))
                        turn(at, range(8))
                    pe.wait_ge(out.sem, out.at(at))
                    pe.wait_ge(rest.sem, rest.at(at))
                    for s in range(pr.ns + pr.lag):
                        if s < pr.ns:
                            part, c, rhs, i = sources[s][0]
                            k = pr.bank_read(s)
                            if k > 0 or at.has(1):
                                pe.wait_ge(pr.multiplied.sem, pr.multiplied.at(at, k))
                            x = part_of(rhs, at, i)
                            ins = pe.matmul(pr.bank(s)[:, :], hi[part][:, c * P:(c + 1) * P], x,
                                            start=True, stop=part not in lo)
                            if part in lo:
                                ins = pe.matmul(pr.bank(s)[:, :], lo[part][:, c * P:(c + 1) * P], x,
                                                start=False, stop=True)
                            ins.then_inc(pr.filled.sem, 1)
                        if s == pr.lag and at.has(1):
                            pe.wait_ge(sums.sem, sums.at(at.back(1)))
                        if s >= pr.lag:
                            for j, (_, _, lhs, acc, r0, start) in enumerate(sources[s - pr.lag][1]):
                                m = pr.first[s - pr.lag] + j
                                pe.wait_ge(pr.multiplied.sem, pr.multiplied.at(at, m + 1))
                                pe.matmul(acc[r0:r0 + lhs.shape[1], :], lhs, pr.tile(m)[:, :], start=start,
                                          stop=True, skip_group_check=True).then_inc(pr.contracted.sem, 1)
                        if s == 6 and not at.first():
                            mix(at.back(1), at)
                        if s == 12 and not at.first():
                            sc.pe(pe, at.back(1))
                        if not at.last(n):
                            if s == 20:
                                if at.has(1):
                                    pe.wait_ge(sc.out_ready.sem, sc.out_ready.at(at.back(1)))
                                turn_d(at.next())
                            if s == 30:
                                message(at.next(), (0, 1, 2))
                            if s == 33:
                                message(at.next(), (3,))
                            if s == 40:
                                turn(at.next(), range(4))
                            if s == 52:
                                turn(at.next(), range(4, 8))
                    if at.last(n):
                        if at.has(1):
                            pe.wait_ge(sc.out_ready.sem, sc.out_ready.at(at.back(1)))
                        mix(at, at)
                        sc.pe(pe, at)
                walk(pe, n, body)


def build_program(nc, d, n_nodes, n_edges, passes):
    with ExitStack() as ctx:
        core = Core(nc, ctx, d, n_nodes, n_edges)
        tiles = n_edges // P
        for name, dt, width in (("X1", F32, D), ("AGG", F32, AW), ("H", F32, D), ("X3", F32, D)):
            if name not in d:
                d[name] = nc.dram_tensor(f"table_{name}", [n_nodes, width], dt, kind="Internal").ap()
        core.cols = {e: sbuf(nc, ctx, f"cols_{e}", [P, tiles], I32) for e in ("src", "dst")}
        core.target = {e: sbuf(nc, ctx, f"target_{e}", [P, tiles], I32) for e in ("src", "dst")}
        off, width = offsets("ident")
        core.ident = sbuf(nc, ctx, "ident", [P, width])
        core.eye = core.ident[:, off["eye"]:off["eye"] + P]
        core.earlier = core.ident[:, off["earlier"]:off["earlier"] + P]
        core.spare = core.ident[:, off["spare"]:off["spare"] + 1]
        for one_pass in [index_pass] + passes:
            core.run(one_pass)


def pass_list():
    return [
        lambda c: plain_node_pass(c, "n0", "X", "X1", True),
        edges0,
        edges1,
        nodes1,
        edges2,
        lambda c: plain_node_pass(c, "n3", "X3", "OUT", False),
        edges3,
    ]


def halves(a):
    m = a.shape[1]
    return a.reshape(2, HALF, m).transpose(1, 0, 2).reshape(HALF, 2 * m)


def block_diagonal(ws, wv):
    out = np.zeros((D, D), np.float32)
    out[:S, :S] = ws
    for i in range(3):
        out[S + i::3, S + i::3] = wv
    return out


def pack_conv(name, fc1, fc2, l1_s, l1_v, l2_s, l2_v, alpha):
    first = np.zeros((P, P), np.float32)
    first[:fc1.shape[0], :fc1.shape[1]] = fc1
    w = fc2.reshape(fc2.shape[0], 192)
    second = np.zeros((P, 2, 96), np.float32)
    second[:w.shape[0], 0, :S], second[:w.shape[0], 0, S:] = w[:, 64:128], w[:, 128:160]
    second[:w.shape[0], 1, :S], second[:w.shape[0], 1, S:] = w[:, 0:64], w[:, 160:192]
    l1 = np.zeros((D, 3, 96), np.float32)
    for m in range(3):
        l1[:S, m, :S] = l1_s
        l1[S + m::3, m, S:] = l1_v
    l2 = np.zeros((96, 4, AW), np.float32)
    l2[:, 0, :S] = l2_s
    if alpha is not None:
        l2[:, 0, D] = alpha[:, 0]
    for m in range(3):
        l2[:, 1 + m, S + m:D:3] = l2_v
    g = np.zeros((P, 6, 96), np.float32)
    for r0 in (32, 64):
        for m in range(3):
            g[r0 + 1 + m, m, :S] = 1
            g[r0, m, S:] = 1
            g[r0 + 1 + m, 3 + m, S:] = 1
        g[r0, 3, :S] = 1
    return pack(name, fc1=first, fc2=second, l1=halves(l1.reshape(D, 288)), l2=l2, gather=g)


def host_arrays(i, n_nodes, n_edges):
    n, e = i["x"].shape[0], i["src"].shape[0]
    tiles = n_edges // P

    def rows(a, count):
        out = np.zeros((count,) + a.shape[1:], a.dtype)
        out[:a.shape[0]] = a
        return out

    d = {"X": rows(i["x"], n_nodes), "Z": rows(i["node_vec1"], n_nodes)}
    for end in ("src", "dst"):
        idx = np.full(n_edges, n_nodes - 1, np.int32)
        idx[:e] = i[end]
        d[f"{end}_rows"] = idx.reshape(1, -1)
        d[f"{end}_cols"] = np.ascontiguousarray(idx.reshape(tiles, P).T)
    across = lambda a: np.ascontiguousarray(rows(a, n_edges).T)
    d["ea32"] = across(i["edge_attr_32"])
    d["ea16"] = across(i["edge_attr_16"])
    d["ea12"] = across(i["edge_attr_12"])
    d["ea4"] = across(i["edge_attr_4"])
    d["ea4_cols"] = np.ascontiguousarray(rows(i["edge_attr_4"], n_edges).reshape(tiles, P, 4).transpose(1, 0, 2)
                                         .reshape(P, tiles * 4))

    q = np.arange(P)
    d["pack_ident"] = pack("ident", eye=np.eye(P), earlier=(q[None, :] < q[:, None]),
                           spare=(n + q)[:, None])

    g = lambda k: i["L0_gnn_" + k]
    W1, W2, W3, W4 = (g(f"W{k}") for k in (1, 2, 3, 4))
    w4 = np.zeros((3, V, 8, 3, V), np.float32)
    for k in range(3):
        w4[k, :, :, k, :] = W4
    wmT = g("Wm").T
    wm_v = np.concatenate([wmT[:, S:].reshape(D, V, 3).transpose(0, 2, 1).reshape(D, 96), g("bm")[:, None]], 1)
    sel = np.zeros((P, 26, P), np.float32)
    for r0 in (0, 32):
        for c in range(4):
            for j in range(2):
                sel[r0 + 2 * c + j, c, j * S:(j + 1) * S] = 1
        for b in range(8):
            for k in range(3):
                sel[r0 + 8 + 3 * b + k, 4 + b, k * V:(k + 1) * V] = 1
            sel[r0 + b, 12 + b, :96] = 1
        for k in range(3):
            for h in range(2):
                for b in range(4):
                    sel[r0 + 8 + 3 * (4 * h + b) + k, 20 + 2 * k + h, b * V:(b + 1) * V] = 1
    d["pack_e0"] = pack(
        "e0", w1=W1.reshape(S, 4, 2, S).transpose(2, 0, 1, 3), w2=np.tile(W2.reshape(V, 8 * S), (3, 1)),
        w4=w4, w3=np.tile(W3.reshape(S, 8 * V), (2, 1)), wm_s=halves(np.tile(wmT[:, :S], (1, 2))),
        wm_v=halves(wm_v), wu=halves(g("Wu")[D:]), gather=sel, sum=np.tile(np.eye(V), (4, 1)))
    lin = np.zeros((97, 2 * D), np.float32)
    lin[:HALF] = halves(g("Wu")[:D])
    lin[96, D:] = g("bu")
    d["pack_n0"] = pack("n0", lin=lin)

    g = lambda k: i["L1_gnn_" + k]
    d["pack_e1"] = pack_conv("e1", g("Wfc1"), g("Wfc2"), g("Wl1_0"), g("Wl1_1"), g("Wl2_s"), g("Wl2_v"), g("Wa"))
    h = lambda k: i["L2_gnn_" + k]
    d["pack_e2"] = pack_conv("e2", h("W_fc1"), h("W_fc2"), h("W_l1_0"), h("W_l1_1"), h("W_l2_0"), h("W_l2_1"), None)
    d["pack_n1"] = pack("n1", sc=halves(block_diagonal(g("Wsc0"), g("Wsc1"))),
                        sc2=halves(block_diagonal(h("W_sc0"), h("W_sc1"))))

    g = lambda k: i["L3_gnn_" + k]
    d["pack_n3"] = pack("n3", lin=halves(block_diagonal(g("Lu_s"), g("Lu_v"))))
    y = np.zeros((192, 2 * D + V), np.float32)
    y[:D, 0:D] = block_diagonal(g("Lm_s"), g("Lm_v"))
    y[:D, D:2 * D] = block_diagonal(g("Wm_ss"), g("Wm_vs"))
    y[:S, 2 * D:] = g("Wm_sv")
    y[D:, 0:S] = g("Wm_vv")
    pick_s = np.zeros((P, 32, 2, S), np.float32)
    for c in range(32):
        for j in range(2):
            for r0 in (0, 64):
                pick_s[r0 + 2 * c + j, c, j, :] = 1
    pick_v = np.zeros((P, 8, 4, V), np.float32)
    total = np.zeros((P, 8, V), np.float32)
    for c in range(8):
        for j in range(4):
            for r0 in (0, 32):
                pick_v[r0 + 4 * c + j, c, j, :] = 1
            total[j * V:(j + 1) * V, c, 4 * c + j] = 1
    out_v = np.zeros((3, V, D), np.float32)
    for k in range(3):
        out_v[k, np.arange(V), S + 3 * np.arange(V) + k] = 1
    d["pack_e3"] = pack(
        "e3", y=y.reshape(2, 96, 2 * D + V).transpose(1, 0, 2), ss=g("Wu_ss").reshape(32, 2, S, S).transpose(1, 2, 0, 3),
        vv=g("Wu_vv").reshape(8, 4, V, S).transpose(1, 2, 0, 3),
        sv=np.tile(g("Wu_sv").reshape(S, V, 8, 4).transpose(0, 2, 3, 1).reshape(S, 8 * P), (2, 1)),
        vs=np.tile(g("Wu_vs").reshape(V, S, 8, 4).transpose(1, 2, 3, 0).reshape(S, 8 * P), (2, 1)),
        pick_s=pick_s, pick_v=pick_v, sum=total,
        out_s=np.tile(np.eye(S, D), (2, 1)), out_v=out_v)
    return d


def kernel(**inputs):
    import concourse.bacc as bacc
    from concourse.bass_utils import run_bass_kernel_spmd

    inputs = {k: np.asarray(v) for k, v in inputs.items()}
    n, e = inputs["x"].shape[0], inputs["src"].shape[0]
    n_nodes, n_edges = -(-(n + P) // GR) * GR, -(-e // GR) * GR
    arrays = host_arrays(inputs, n_nodes, n_edges)
    nc = bacc.Bacc("TRN2", target_bir_lowering=False, num_devices=1)
    d = {k: nc.dram_tensor(f"in_{k}", a.shape, mybir.dt.from_np(a.dtype), kind="ExternalInput").ap()
         for k, a in arrays.items()}
    d["OUT"] = nc.dram_tensor("out_x", [n_nodes, D], F32, kind="ExternalOutput").ap()
    build_program(nc, d, n_nodes, n_edges, pass_list())
    result = run_bass_kernel_spmd(nc, [{f"in_{k}": a for k, a in arrays.items()}], core_ids=[0])
    return result.results[0]["out_x"][:n]
```

```python
import numpy as np
import concourse.bass as bass
from concourse import mybir
from contextlib import ExitStack

F32, F32R, I32 = mybir.dt.float32, mybir.dt.float32r, mybir.dt.int32
ALU = mybir.AluOpType
ACT = mybir.ActivationFunctionType
AX = mybir.AxisListType
POOL, DVE = mybir.EngineType.Pool, mybir.EngineType.DVE

P = 128
T = 4
GR = T * P
S, V, D = 64, 32, 160
HALF = D // 2
AW = D + 2
EPS = 1e-5


class At:

    def __init__(self, g, rest, half, quarter):
        self.g, self.rest, self.half, self.quarter = g, rest, half, quarter
        self.b = rest % 2

    @staticmethod
    def of(g):
        return At(g, g % 4, g // 2, g // 4)

    def back(self, n):
        r = self.rest - n
        return At(self.g - n, r % 4, self.half + (r // 2 - self.rest // 2), 
                  None if self.quarter is None else self.quarter + r // 4)

    def next(self):
        return self.back(-1)

    def has(self, n):
        return not isinstance(self.g, int) or self.g >= n

    def within(self, n, count):
        return not isinstance(self.g, int) or n <= self.g < n + count

    def first(self):
        return isinstance(self.g, int) and self.g == 0

    def last(self, count):
        return isinstance(self.g, int) and self.g == count - 1


def walk(eng, count, body, unroll=2, lag=0):
    head = -(-(lag + 2) // unroll) * unroll
    turns = (count - 1 - head) // unroll
    for g in range(head):
        body(At.of(g))
    with eng.Fori(head // unroll, head // unroll + turns) as j:
        for r in range(unroll):
            if unroll == 2:
                body(At(j * 2 + r, r, j, None))
            else:
                body(At(j * 4 + r, r, j * 2 + r // 2, j))
    for g in range(head + turns * unroll, count + lag):
        body(At.of(g))


def apart(core, eng, at):
    if not isinstance(at.g, int):
        eng.sem_inc(core.passed[eng.engine], 1)


class Count:

    def __init__(self, sem, per):
        self.sem, self.per = sem, per

    def at(self, at, k=None):
        return at.g * self.per + (self.per if k is None else k)


class Moves:

    def __init__(self, sems, per=1):
        self.sems, self.per = sems, per

    def of(self, at):
        return self.sems[at.rest % len(self.sems)]

    def at(self, at, k=None):
        n = at.half if len(self.sems) == 2 else at.quarter
        return n * (16 * self.per) + 16 * (self.per if k is None else k)


class Core:

    def __init__(self, nc, ctx, d, n_nodes, n_edges):
        self.nc, self.ctx, self.d = nc, ctx, d
        self.nodes = n_nodes
        self.node_groups, self.edge_groups = n_nodes // GR, n_edges // GR

        self.passed = {e: nc.alloc_semaphore(name=f"passed_{e.name}") for e in (POOL, DVE)}
        self.pass_sems = []

    def sem(self, name):
        self.pass_sems.append(self.nc.alloc_semaphore(name=name))
        return self.pass_sems[-1]

    def run(self, one_pass):
        one_pass(self)
        self.nc.clear_and_free_semaphores(self.pass_sems)
        self.nc.all_engine_barrier()
        self.pass_sems = []

    def count(self, name, per):
        return Count(self.sem(name), per)

    def moves(self, name, per=1, buffers=2):
        return Moves([self.sem(f"{name}_{b}") for b in range(buffers)], per)


def sbuf(nc, ctx, name, shape, dt=F32):
    return ctx.enter_context(nc.sbuf_tensor(name, shape, dt))


def banks(nc, ctx, name, n):
    return [ctx.enter_context(nc.psum_tensor(f"{name}{i}", [P, 512], F32)) for i in range(n)]


def over(ap, n):
    p, m = ap.shape
    return ap.unsqueeze(2).broadcast_to([p, m, n])


PACKS = {
    "n0": {"lin": (97, 2 * D)},
    "e0": {"w1": (P, 4 * S), "w2": (96, 8 * S), "w4": (96, 8 * 96), "w3": (P, 2 * P),
           "wm_s": (HALF, 2 * P), "wm_v": (HALF, 2 * 97), "wu": (HALF, 2 * D),
           "gather": (P, 26 * P), "sum": (P, V)},
    "e1": {"fc1": (P, P), "fc2": (P, 192), "l1": (HALF, 2 * 3 * 96), "l2": (96, 4 * AW),
           "gather": (P, 6 * 96)},
    "n1": {"sc": (HALF, 2 * D), "sc2": (HALF, 2 * D)},
    "e2": {"fc1": (P, P), "fc2": (P, 192), "l1": (HALF, 2 * 3 * 96), "l2": (96, 4 * AW),
           "gather": (P, 6 * 96)},
    "n3": {"lin": (HALF, 2 * D)},
    "e3": {"y": (96, 2 * (2 * D + V)), "ss": (P, 32 * S), "vv": (P, 8 * S), "sv": (P, 8 * P),
           "vs": (P, 8 * P), "pick_s": (P, 32 * P), "pick_v": (P, 8 * P), "sum": (P, 8 * V),
           "out_s": (P, D), "out_v": (96, D)},
    "ident": {"eye": (P, P), "earlier": (P, P), "spare": (P, 1)},
}


def offsets(name):
    at, out = 0, {}
    for k, (_, w) in PACKS[name].items():
        out[k] = at
        at += w
    return out, at


def pack(name, **parts):
    off, width = offsets(name)
    out = np.zeros((P, width), np.float32)
    for k, (rows, w) in PACKS[name].items():
        out[:rows, off[k]:off[k] + w] = np.asarray(parts[k]).reshape(rows, w)
    return out


def feature_scales(part, width):
    return [(part, 0, S, 0, width, 1 / 8), (part, S, HALF, 0, width, 1 / np.sqrt(32.0)),
            (part, 0, HALF, width, 2 * width, 1 / np.sqrt(32.0))]


def load_pack(core, ctx, name, scales, halves):
    nc = core.nc
    off, width = offsets(name)
    W = sbuf(nc, ctx, f"{name}_w", [P, width])
    part = lambda k: W[:PACKS[name][k][0], off[k]:off[k] + PACKS[name][k][1]]
    hi, lo = {}, {}
    for k, both in halves.items():
        shape = list(PACKS[name][k])
        hi[k] = sbuf(nc, ctx, f"{name}_{k}_hi", shape, F32R)
        if both:
            lo[k] = sbuf(nc, ctx, f"{name}_{k}_lo", shape, F32R)
    loaded, scaled, rounded = (core.sem(f"{name}_{x}") for x in ("w_loaded", "w_scaled", "w_rounded"))
    with nc.Block() as block:
        @block.sync
        def _(sp):
            sp.dma_start(W[:, :], core.d[f"pack_{name}"]).then_inc(loaded, 16)

        @block.vector
        def _(dve):
            dve.wait_ge(loaded, 16)
            for k, r0, r1, c0, c1, c in scales:
                o = W[r0:r1, off[k] + c0:off[k] + c1]
                dve.tensor_scalar(o, o, float(c), None, ALU.mult).then_inc(scaled, 1)
            if scales:
                dve.wait_ge(scaled, len(scales))
            n = 0
            for k in hi:
                dve.tensor_copy(hi[k][:, :], part(k)).then_inc(rounded, 1)
                n += 1
            for k in lo:
                dve.wait_ge(rounded, n)
                dve.tensor_tensor(lo[k][:, :], part(k), hi[k][:, :].bitcast(F32),
                                  ALU.subtract).then_inc(rounded, 1)
    return W, {k: part(k) for k in PACKS[name]}, hi, lo


def index_pass(core):
    nc, d, n = core.nc, core.d, core.edge_groups
    with ExitStack() as ctx:
        same = [sbuf(nc, ctx, f"ix_same{x}", [P, T, P]) for x in range(2)]
        rank = [sbuf(nc, ctx, f"ix_rank{x}", [P, T]) for x in range(2)]
        move = [sbuf(nc, ctx, f"ix_move{x}", [P, T]) for x in range(2)]
        row_of = sbuf(nc, ctx, "ix_row", [P, 2, T])
        loaded = core.moves("ix_loaded", 2)
        step = core.count("ix_step", 16)
        ready = core.sem("ix_ready")
        rows2 = [sbuf(nc, ctx, f"ix_rows{b}", [P, 2, GR], I32) for b in range(2)]
        ends = ("src", "dst")
        with nc.Block() as block:
            @block.sync
            def _(sp):
                for e in ends:
                    sp.dma_start(core.cols[e][:, :], d[f"{e}_cols"]).then_inc(ready, 16)
                sp.dma_start(core.ident[:, :], d["pack_ident"]).then_inc(ready, 16)

                def body(at):
                    if at.has(2):
                        sp.wait_ge(step.sem, step.at(at.back(2)))
                    for x, e in enumerate(ends):
                        sp.dma_start(rows2[at.b][:, x, :],
                                     d[f"{e}_rows"][:, bass.ds(at.g * GR, GR)].broadcast_to([P, GR])
                                     ).then_inc(loaded.of(at), 16)
                walk(sp, n, body)

            @block.vector
            def _(dve):
                dve.wait_ge(ready, 48)

                def body(at):
                    dve.wait_ge(loaded.of(at), loaded.at(at))
                    k = 0

                    def then(ins):
                        nonlocal k
                        ins.then_inc(step.sem, 1)
                        k += 1

                    cols = [core.cols[e][:, bass.ds(at.g * T, T)] for e in ends]
                    for x in range(2):
                        then(dve.tensor_tensor(same[x][:, :, :],
                                               rows2[at.b][:, x, :].rearrange("p (t q) -> p t q", t=T),
                                               over(cols[x], P), ALU.is_equal))
                    dve.wait_ge(step.sem, step.at(at, k))
                    for x in range(2):
                        then(dve.tensor_tensor(same[x][:, :, :], same[x][:, :, :],
                                               core.earlier.unsqueeze(1).broadcast_to([P, T, P]), ALU.mult))
                    dve.wait_ge(step.sem, step.at(at, k))
                    for x in range(2):
                        then(dve.tensor_reduce(rank[x][:, :], same[x][:, :, :], AX.X, ALU.max))
                    for x in range(2):
                        then(dve.tensor_copy(move[x][:, :], cols[x]))
                    dve.wait_ge(step.sem, step.at(at, k))
                    for x in range(2):
                        then(dve.tensor_scalar(row_of[:, x, :], move[x][:, :], -1.0, core.spare,
                                               ALU.mult, ALU.add))
                    dve.wait_ge(step.sem, step.at(at, k))
                    for x in range(2):
                        then(dve.tensor_tensor(rank[x][:, :], rank[x][:, :], row_of[:, x, :], ALU.mult))
                    dve.wait_ge(step.sem, step.at(at, k))
                    for x in range(2):
                        then(dve.tensor_tensor(move[x][:, :], move[x][:, :], rank[x][:, :], ALU.add))
                    dve.wait_ge(step.sem, step.at(at, k))
                    for x, e in enumerate(ends):
                        then(dve.tensor_copy(core.target[e][:, bass.ds(at.g * T, T)], move[x][:, :]))
                    assert k == step.per
                walk(dve, n, body)


class Norm:

    def __init__(self, core, ctx, name, tiles, eps, kb=HALF):
        nc = core.nc
        self.core, self.tiles, self.eps, self.kb = core, tiles, eps, kb
        self.pairs = tiles // 2
        self.chunks = tiles // 4
        two = lambda what, shape: [sbuf(nc, ctx, f"{name}_{what}{b}", shape) for b in range(2)]
        self.H = two("h", [P, tiles * D])
        self.HT = two("ht", [max(kb, HALF) if kb == HALF else P, self.chunks, 2, GR])
        self.st, self.mv = two("st", [P, tiles, 6]), two("mv", [P, tiles, 2])
        self.sd, self.rs, self.nm = two("sd", [P, tiles]), two("rs", [P, tiles]), two("nm", [P, tiles])
        self.TP = banks(nc, ctx, f"{name}_tp", 2 * self.chunks)
        self.LP = banks(nc, ctx, f"{name}_lp", self.pairs)
        self.stats = core.count(f"{name}_stats", tiles)
        self.means = core.count(f"{name}_means", tiles)
        self.std = core.count(f"{name}_std", 1)
        self.inv = core.count(f"{name}_inv", 2)
        self.h_ready = core.count(f"{name}_h_ready", tiles)
        self.turned = core.count(f"{name}_turned", 2 * self.chunks)
        self.ht_ready = core.count(f"{name}_ht_ready", 2 * self.chunks)
        self.mixed = core.count(f"{name}_mixed", self.pairs)

    def statistics(self, dve, at, x):
        b = at.b
        if at.has(2):
            dve.wait_ge(self.inv.sem, self.inv.at(at.back(2)))
            dve.wait_ge(self.std.sem, self.std.at(at.back(2)))
        for t in range(self.tiles):
            dve.bn_stats(self.st[b][:, t, :], x[:, t * D:(t + 1) * D]).then_inc(self.stats.sem, 1)

    def means_of(self, dve, at):
        for t in range(self.tiles):
            dve.wait_ge(self.stats.sem, self.stats.at(at, t + 1))
            apart(self.core, dve, at)
            dve.bn_aggr(self.mv[at.b][:, t, :], self.st[at.b][:, t, :]).then_inc(self.means.sem, 1)

    def root(self, act, at):
        act.wait_ge(self.means.sem, self.means.at(at))
        act.activation(self.sd[at.b][:, :], self.mv[at.b][:, :, 1], ACT.Sqrt, bias=self.eps[:, 0:1]
                       ).then_inc(self.std.sem, 1)

    def factors(self, dve, at):
        dve.wait_ge(self.std.sem, self.std.at(at))
        if at.has(2):
            dve.wait_ge(self.h_ready.sem, self.h_ready.at(at.back(2)))
        dve.reciprocal(self.rs[at.b][:, :], self.sd[at.b][:, :]).then_inc(self.inv.sem, 1)
        dve.wait_ge(self.inv.sem, self.inv.at(at, 1))
        dve.scalar_tensor_tensor(self.nm[at.b][:, :], self.mv[at.b][:, :, 0], -1.0, self.rs[at.b][:, :],
                                 ALU.mult, ALU.mult).then_inc(self.inv.sem, 1)

    def relu(self, act, at, x):
        act.wait_ge(self.inv.sem, self.inv.at(at))
        if at.has(2):
            act.wait_ge(self.turned.sem, self.turned.at(at.back(2)))
        for t in range(self.tiles):
            act.activation(self.H[at.b][:, t * D:(t + 1) * D], x[:, t * D:(t + 1) * D], ACT.Relu,
                           bias=self.nm[at.b][:, t:t + 1], scale=self.rs[at.b][:, t:t + 1]
                           ).then_inc(self.h_ready.sem, 1)

    def turn(self, pe, at):
        for c in range(self.chunks):
            for h in range(2):
                k = 2 * c + h
                if at.has(1):
                    pe.wait_ge(self.ht_ready.sem, self.ht_ready.at(at.back(1), k + 1))
                for t in range(4 * c, 4 * c + 4):
                    if h == 0:
                        pe.wait_ge(self.h_ready.sem, self.h_ready.at(at, t + 1))
                    ins = pe.transpose(self.TP[k][0:HALF, (t % 4) * P:(t % 4 + 1) * P],
                                       self.H[at.b][:, t * D + h * HALF:t * D + (h + 1) * HALF], self.core.eye)
                ins.then_inc(self.turned.sem, 1)

    def copies(self, act, at):
        if at.has(2):
            act.wait_ge(self.mixed.sem, self.mixed.at(at.back(2)))
        for c in range(self.chunks):
            for h in range(2):
                k = 2 * c + h
                act.wait_ge(self.turned.sem, self.turned.at(at, k + 1))
                act.activation(self.HT[at.b][0:HALF, c, h, :], self.TP[k][0:HALF, :], ACT.Copy
                               ).then_inc(self.ht_ready.sem, 1)

    def mix(self, pe, at, lin, added, per_pair):
        for q in range(self.pairs):
            if at.has(1):
                pe.wait_ge(added.sem, added.at(at.back(1), per_pair * (q + 1)))
            pe.wait_ge(self.ht_ready.sem, self.ht_ready.at(at, 2 * (q // 2) + 2))
            for t in (2 * q, 2 * q + 1):
                o = self.LP[q][:, (t % 2) * D:(t % 2 + 1) * D]
                x = self.HT[at.b][:, t // 4, :, (t % 4) * P:(t % 4 + 1) * P]
                pe.matmul(o, x[0:HALF, 0, :], lin[0:HALF, 0:D], start=True, stop=False)
                ins = pe.matmul(o, x[0:self.kb, 1, :], lin[0:self.kb, D:2 * D], start=False, stop=True)
            ins.then_inc(self.mixed.sem, 1)


def plain_node_pass(core, name, src, dst, with_agg):
    nc, d = core.nc, core.d
    kb = PACKS[name]["lin"][0]
    TN = 8
    n = core.nodes // (TN * P)
    with ExitStack() as ctx:
        W, w, _, _ = load_pack(core, ctx, name, feature_scales("lin", D) if name == "n3" else [], {})
        X = [sbuf(nc, ctx, f"{name}_x{b}", [P, TN * D]) for b in range(4)]
        Y = [sbuf(nc, ctx, f"{name}_y{b}", [P, TN * D]) for b in range(2)]
        eps = sbuf(nc, ctx, f"{name}_eps", [P, 1])
        zero = sbuf(nc, ctx, f"{name}_zero", [P, TN * AW])
        ln = Norm(core, ctx, name, TN, eps, kb)
        x_in = core.moves(f"{name}_x_in", buffers=4)
        h_out = core.moves(f"{name}_h_out")
        y_out = core.moves(f"{name}_y_out")
        zeroed = core.moves(f"{name}_zeroed")
        y_ready = core.count(f"{name}_y_ready", ln.pairs)
        const = core.sem(f"{name}_const")
        fold = core.sem(f"{name}_fold")
        rows = lambda a, at: a[bass.ds(at.g * (TN * P), TN * P), :].rearrange("(p t) c -> p (t c)", t=TN)
        n_const = 4 + 2 * (kb > HALF)
        with nc.Block() as block:
            @block.sync
            def _(sp):
                def body(at):
                    if at.within(0, n):
                        if at.has(4):
                            sp.wait_ge(y_ready.sem, y_ready.at(at.back(4)))
                        sp.dma_start(X[at.rest][:, :], rows(d[src], at)).then_inc(x_in.of(at), 16)
                    if at.within(3, n):
                        p = at.back(3)
                        sp.wait_ge(y_ready.sem, y_ready.at(p))
                        sp.dma_start(rows(d[dst], p), Y[p.b][:, :]).then_inc(y_out.of(p), 16)
                walk(sp, n, body, unroll=4, lag=3)
                for q in (n - 1, n - 2):
                    sp.wait_ge(y_out.of(At.of(q)), y_out.at(At.of(q)))

            @block.vector
            def _(dve):
                dve.memset(eps[:, :], EPS).then_inc(const, 1)
                dve.memset(zero[:, :], 0.0).then_inc(const, 1)
                for b in range(2):
                    if kb > HALF:
                        dve.memset(ln.HT[b][64:128, :, :, :], 0.0).then_inc(const, 1)
                    else:
                        dve.memset(ln.HT[b][64:HALF, :, :, :], 0.0).then_inc(const, 1)
                if kb > HALF:
                    dve.wait_ge(const, 4)
                    for b in range(2):
                        dve.memset(ln.HT[b][96:97, :, 1, :], 1.0).then_inc(const, 1)
                for h in range(2):
                    o = w["lin"][0:HALF, h * D + h * HALF:h * D + (h + 1) * HALF]
                    dve.tensor_tensor(o, o, core.eye[0:HALF, 0:HALF], ALU.add).then_inc(fold, 1)

                def body(at):
                    if at.within(0, n):
                        dve.wait_ge(x_in.of(at), x_in.at(at))
                        ln.statistics(dve, at, X[at.rest])
                    if at.within(1, n):
                        ln.factors(dve, at.back(1))
                    if at.within(0, n):
                        ln.means_of(dve, at)
                    if at.within(2, n):
                        p = at.back(2)
                        if p.has(2):
                            dve.wait_ge(y_out.of(p.back(2)), y_out.at(p.back(2)))
                        for q in range(ln.pairs):
                            c = slice(q * 2 * D, (q + 1) * 2 * D)
                            dve.wait_ge(ln.mixed.sem, ln.mixed.at(p, q + 1))
                            dve.tensor_tensor(Y[p.b][:, c], ln.LP[q][:, 0:2 * D], X[p.rest][:, c], ALU.add
                                              ).then_inc(y_ready.sem, 1)
                walk(dve, n, body, unroll=4, lag=2)

            @block.scalar
            def _(act):
                act.wait_ge(const, n_const)

                def body(at):
                    if at.within(2, n):
                        ln.copies(act, at.back(2))
                    if at.within(1, n):
                        p = at.back(1)
                        if p.has(2):
                            act.wait_ge(h_out.of(p.back(2)), h_out.at(p.back(2)))
                        ln.relu(act, p, X[p.rest])
                    if at.within(0, n):
                        ln.root(act, at)
                    if at.within(1, n):
                        p = at.back(1)
                        act.wait_ge(ln.h_ready.sem, ln.h_ready.at(p))
                        act.dma_start(rows(d["H"], p), ln.H[p.b][:, :]).then_inc(h_out.of(p), 16)
                        if with_agg:
                            act.dma_start(rows(d["AGG"], p), zero[:, :]).then_inc(zeroed.of(p), 16)
                walk(act, n, body, unroll=4, lag=2)
                for q in (n - 1, n - 2):
                    act.wait_ge(h_out.of(At.of(q)), h_out.at(At.of(q)))
                    if with_agg:
                        act.wait_ge(zeroed.of(At.of(q)), zeroed.at(At.of(q)))

            @block.tensor
            def _(pe):
                pe.wait_ge(fold, 2)
                pe.wait_ge(const, n_const)

                def body(at):
                    if at.within(2, n):
                        ln.mix(pe, at.back(2), w["lin"], y_ready, 1)
                    if at.within(1, n):
                        ln.turn(pe, at.back(1))
                walk(pe, n, body, unroll=4, lag=2)


class Gather:

    def __init__(self, core, ctx, name, table, end, width=D):
        self.core, self.table, self.end = core, table, end
        self.rows = [sbuf(core.nc, ctx, f"{name}_g{b}", [P, T, width]) for b in range(2)]
        self.index = [sbuf(core.nc, ctx, f"{name}_gi{b}", [P, T], I32) for b in range(2)]
        self.indexed = core.count(f"{name}_gather_index", 1)
        self.here = core.moves(f"{name}_gathered", T)

    def pool(self, pool, at):
        if at.has(2):
            pool.wait_ge(self.here.of(at.back(2)), self.here.at(at.back(2)))
        apart(self.core, pool, at)
        pool.tensor_copy(self.index[at.b][:, :], self.core.cols[self.end][:, bass.ds(at.g * T, T)]
                         ).then_inc(self.indexed.sem, 1)
        pool.wait_ge(self.indexed.sem, self.indexed.at(at))
        apart(self.core, pool, at)
        for t in range(T):
            pool.indirect_dma_start(self.rows[at.b][:, t, :], None, self.core.d[self.table],
                                    bass.IndirectOffsetOnAxis(ap=self.index[at.b][:, t:t + 1], axis=0)
                                    ).then_inc(self.here.of(at), 16)


class Scatter:

    def __init__(self, core, ctx, name, table, end, width, bank):
        nc = core.nc
        self.core, self.table, self.end, self.width, self.bank = core, table, end, width, bank
        self.U = [sbuf(nc, ctx, f"{name}_u{b}", [P, T, width]) for b in range(2)]
        self.out = [sbuf(nc, ctx, f"{name}_so{b}", [P, T, width]) for b in range(2)]
        self.same = [sbuf(nc, ctx, f"{name}_sm{b}", [P, T, P]) for b in range(2)]
        self.near = [sbuf(nc, ctx, f"{name}_sr{b}", [P, GR], I32) for b in range(2)]
        self.index = [sbuf(nc, ctx, f"{name}_si{b}", [P, T], I32) for b in range(2)]
        self.near_in = core.moves(f"{name}_targets_in")
        self.same_ready = core.count(f"{name}_same_ready", 1)
        self.u_ready = core.count(f"{name}_u_ready", 2)
        self.merged = core.count(f"{name}_merged", 2)
        self.out_ready = core.count(f"{name}_out_ready", 2)
        self.indexed = core.count(f"{name}_scatter_index", 1)
        self.added = core.moves(f"{name}_added", T)

    def sp(self, sp, at):
        if at.has(2):
            sp.wait_ge(self.same_ready.sem, self.same_ready.at(at.back(2)))
        sp.dma_start(self.near[at.b][:, :], self.core.d[f"{self.end}_rows"][:, bass.ds(at.g * GR, GR)]
                     .broadcast_to([P, GR])).then_inc(self.near_in.of(at), 16)

    def dve(self, dve, at):
        dve.wait_ge(self.near_in.of(at), self.near_in.at(at))
        if at.has(2):
            dve.wait_ge(self.merged.sem, self.merged.at(at.back(2)))
        dve.tensor_tensor(self.same[at.b][:, :, :], self.near[at.b][:, :].rearrange("p (t q) -> p t q", t=T),
                          over(self.core.cols[self.end][:, bass.ds(at.g * T, T)], P), ALU.is_equal
                          ).then_inc(self.same_ready.sem, 1)

    def pe(self, pe, at):
        pe.wait_ge(self.same_ready.sem, self.same_ready.at(at))
        pe.wait_ge(self.u_ready.sem, self.u_ready.at(at))
        for t in range(T):
            ins = pe.matmul(self.bank[t // 2][:, (t % 2) * self.width:(t % 2 + 1) * self.width],
                            self.same[at.b][:, t, :], self.U[at.b][:, t, :], start=True, stop=True)
            if t % 2:
                ins.then_inc(self.merged.sem, 1)

    def act(self, act, at):
        if at.has(2):
            act.wait_ge(self.added.of(at.back(2)), self.added.at(at.back(2)))
        for h in range(2):
            act.wait_ge(self.merged.sem, self.merged.at(at, h + 1))
            act.activation(self.out[at.b][:, 2 * h:2 * h + 2, :].rearrange("p t c -> p (t c)"),
                           self.bank[h][:, 0:2 * self.width], ACT.Copy).then_inc(self.out_ready.sem, 1)

    def pool(self, pool, at):
        if at.has(2):
            pool.wait_ge(self.added.of(at.back(2)), self.added.at(at.back(2)))
        apart(self.core, pool, at)
        pool.tensor_copy(self.index[at.b][:, :], self.core.target[self.end][:, bass.ds(at.g * T, T)]
                         ).then_inc(self.indexed.sem, 1)
        pool.wait_ge(self.indexed.sem, self.indexed.at(at))
        pool.wait_ge(self.out_ready.sem, self.out_ready.at(at))
        if at.has(1):
            pool.wait_ge(self.added.of(at.back(1)), self.added.at(at.back(1)))
        apart(self.core, pool, at)
        for t in range(T):
            if t:
                pool.wait_ge(self.added.of(at), self.added.at(at, t))
                apart(self.core, pool, at)
            pool.indirect_dma_start(self.core.d[self.table],
                                    bass.IndirectOffsetOnAxis(ap=self.index[at.b][:, t:t + 1], axis=0),
                                    self.out[at.b][:, t, :], None, compute_op=ALU.add
                                    ).then_inc(self.added.of(at), 16)


class Plan:

    def __init__(self, core, ctx, name, counts, ring, tiles, lag):
        self.counts, self.ring, self.lag = counts, ring, lag
        self.F = [sbuf(core.nc, ctx, f"{name}_f{i}", [P, GR]) for i in range(tiles)]
        self.first = [sum(counts[:s]) for s in range(len(counts))]
        self.ns, self.nm = len(counts), sum(counts)
        self.filled = core.count(f"{name}_filled", self.ns)
        self.multiplied = core.count(f"{name}_multiplied", self.nm)
        self.contracted = core.count(f"{name}_contracted", self.nm)

    def bank(self, s):
        return self.ring[s % len(self.ring)]

    def tile(self, m):
        return self.F[m % len(self.F)]

    def bank_read(self, s):
        last = s - len(self.ring)
        if last >= 0:
            return self.first[last] + self.counts[last]
        last = max(x for x in range(self.ns) if x % len(self.ring) == s)
        return self.first[last] + self.counts[last] - self.nm

    def tile_read(self, m):
        last = m - len(self.F)
        if last >= 0:
            return last + 1
        return max(x for x in range(self.nm) if x % len(self.F) == m) + 1 - self.nm


def edges0(core):
    nc, d, n, name = core.nc, core.d, core.edge_groups, "e0"
    r2 = 1 / np.sqrt(2.0)
    with ExitStack() as ctx:
        W, w, hi, lo = load_pack(core, ctx, name,
                                 [("w1", 0, P, 0, 4 * S, r2 / np.sqrt(512)),
                                  ("w2", 0, 96, 0, 8 * S, r2 / (np.sqrt(3.0) * 16)),
                                  ("w4", 0, 96, 0, 8 * 96, r2 / 16), ("w3", 0, P, 0, 2 * P, r2 / np.sqrt(512))],
                                 {"w3": True, "gather": False})
        EA = [sbuf(nc, ctx, f"e0_ea{b}", [64, GR]) for b in range(2)]
        EH = [sbuf(nc, ctx, f"e0_eh{b}", [P, GR], F32R) for b in range(2)]
        XX = [sbuf(nc, ctx, f"e0_xx{b}", [P, T, 224]) for b in range(2)]
        XS = [sbuf(nc, ctx, f"e0_xs{b}", [P, GR]) for b in range(2)]
        XH = [sbuf(nc, ctx, f"e0_xh{b}", [P, GR], F32R) for b in range(2)]
        XV = [sbuf(nc, ctx, f"e0_xv{b}", [96, GR]) for b in range(2)]
        T3 = [sbuf(nc, ctx, f"e0_t3{b}", [P, 2, GR]) for b in range(2)]
        US = [sbuf(nc, ctx, f"e0_us{b}", [P, GR]) for b in range(2)]
        UV = [sbuf(nc, ctx, f"e0_uv{b}", [97, GR]) for b in range(2)]
        fold_s = sbuf(nc, ctx, "e0_fold_s", [P, D])
        fold_v = sbuf(nc, ctx, "e0_fold_v", [97, D])
        front = banks(nc, ctx, "e0_front", 2)
        ring = banks(nc, ctx, "e0_ring", 4)
        AS, AV = banks(nc, ctx, "e0_acc", 2)

        ga = Gather(core, ctx, name, "H", "dst")
        sc = Scatter(core, ctx, name, "X1", "src", D, front)
        ea_in = core.moves("e0_ea_in", 2)
        spread = core.count("e0_spread", 2)
        turned = core.count("e0_turned", 2)
        x_ready = core.count("e0_x_ready", 3)
        ea_hi = core.count("e0_ea_hi", 1)
        rest = core.count("e0_rest", 2)
        t3_done = core.count("e0_t3_done", 2)
        t3_ready = core.count("e0_t3_ready", 2)
        sums = core.count("e0_sums", 2)
        mixed = core.count("e0_mixed", 2)
        folded, fold_ready, const = (core.sem(f"e0_{x}") for x in ("folded", "fold_ready", "const"))

        sources = []
        for c in range(4):
            sources.append((P, c, (XS,), w["w1"][:, c * S:(c + 1) * S], AS, 64 * (c % 2), c < 2))
        for c in range(8):
            sources.append((96, 4 + c, (XV,), w["w2"][:, c * S:(c + 1) * S], AS, 64 * (c % 2), False))
        for c in range(8):
            sources.append((96, 12 + c, (XV,), w["w4"][:, c * 96:(c + 1) * 96], AV, 0, c == 0))
        for i in range(3):
            for q in range(2):
                sources.append((P, 20 + 2 * i + q, (T3, q), w["sum"], AV, 32 * i, False))
        pr = Plan(core, ctx, name, [1] * len(sources), ring, 4, 3)

        with nc.Block() as block:
            @block.gpsimd
            def _(pool):
                def body(at):
                    if at.first():
                        ga.pool(pool, at)
                    if not at.last(n):
                        if at.has(1):
                            pool.wait_ge(spread.sem, spread.at(at.back(1)))
                        apart(core, pool, at)
                        ga.pool(pool, at.next())
                    if not at.first():
                        sc.pool(pool, at.back(1))
                    if at.last(n):
                        sc.pool(pool, at)
                        for q in (at, at.back(1)):
                            pool.wait_ge(sc.added.of(q), sc.added.at(q))
                            apart(core, pool, q)
                walk(pool, n, body)

            @block.sync
            def _(sp):
                def body(at):
                    if at.has(2):
                        sp.wait_ge(rest.sem, rest.at(at.back(2)))
                    for h in range(2):
                        sp.dma_start(EA[at.b][32 * h:32 * h + 32, :], d["ea32"][:, bass.ds(at.g * GR, GR)]
                                     ).then_inc(ea_in.of(at), 16)
                    sc.sp(sp, at)
                walk(sp, n, body)

            @block.scalar
            def _(act):
                act.wait_ge(folded, 2)
                act.activation(fold_s[:, :], front[0][:, 0:D], ACT.Copy).then_inc(fold_ready, 1)
                act.activation(fold_v[:, :], front[1][0:97, 0:D], ACT.Copy).then_inc(fold_ready, 1)
                act.wait_ge(const, 4)

                def start(at):
                    act.wait_ge(ga.here.of(at), ga.here.at(at))
                    act.activation(XX[at.b][:, :, 0:P].rearrange("p t (r a) -> p t r a", r=2),
                                   ga.rows[at.b][:, :, 0:S].unsqueeze(2).broadcast_to([P, T, 2, S]), ACT.Copy
                                   ).then_inc(spread.sem, 1)
                    act.activation(XX[at.b][:, :, P:224].rearrange("p t (i a) -> p t i a", i=3),
                                   ga.rows[at.b][:, :, S:D].rearrange("p t (a i) -> p t i a", i=3), ACT.Copy
                                   ).then_inc(spread.sem, 1)
                    act.wait_ge(ea_in.of(at), ea_in.at(at))
                    act.activation(EH[at.b][0:64, :], EA[at.b][:, :], ACT.Copy).then_inc(ea_hi.sem, 1)
                    act.wait_ge(turned.sem, turned.at(at, 1))
                    act.activation(XS[at.b][:, :], front[0][:, :], ACT.Copy).then_inc(x_ready.sem, 1)
                    act.activation(XH[at.b][:, :], front[0][:, :], ACT.Copy).then_inc(x_ready.sem, 1)
                    act.wait_ge(turned.sem, turned.at(at, 2))
                    act.activation(XV[at.b][:, :], front[1][0:96, :], ACT.Copy).then_inc(x_ready.sem, 1)
                    for q in range(2):
                        act.wait_ge(t3_done.sem, t3_done.at(at, q + 1))
                        act.activation(T3[at.b][:, q, :], front[q][:, :], ACT.Copy).then_inc(t3_ready.sem, 1)

                def finish(at):
                    act.wait_ge(pr.contracted.sem, pr.contracted.at(at))
                    act.activation(US[at.b][:, :], AS[:, :], ACT.Copy).then_inc(sums.sem, 1)
                    act.activation(UV[at.b][0:96, :], AV[0:96, :], ACT.Copy).then_inc(sums.sem, 1)
                    for h in range(2):
                        act.wait_ge(mixed.sem, mixed.at(at, h + 1))
                        act.activation(sc.U[at.b][:, 2 * h:2 * h + 2, :].rearrange("p t c -> p (t c)"),
                                       front[h][:, 0:2 * D], ACT.Copy).then_inc(sc.u_ready.sem, 1)
                    sc.act(act, at)

                def body(at):
                    if at.first():
                        start(at)
                    else:
                        finish(at.back(1))
                    if not at.last(n):
                        start(at.next())
                    else:
                        finish(at)
                walk(act, n, body)

            @block.vector
            def _(dve):
                for b in range(2):
                    dve.memset(EH[b][64:128, :].bitcast(F32), 0.0).then_inc(const, 1)
                    dve.memset(UV[b][96:97, :], 1.0).then_inc(const, 1)

                def split(at):
                    dve.wait_ge(ea_hi.sem, ea_hi.at(at))
                    dve.tensor_tensor(EH[at.b][32:64, :], EA[at.b][32:64, :], EH[at.b][32:64, :].bitcast(F32),
                                      ALU.subtract).then_inc(rest.sem, 1)
                    dve.wait_ge(x_ready.sem, x_ready.at(at, 2))
                    dve.tensor_tensor(XH[at.b][64:128, :], XS[at.b][64:128, :], XH[at.b][64:128, :].bitcast(F32),
                                      ALU.subtract).then_inc(rest.sem, 1)

                def body(at):
                    if at.first():
                        split(at)
                        dve.wait_ge(x_ready.sem, x_ready.at(at, 3))
                    dve.wait_ge(x_ready.sem, x_ready.at(at))
                    dve.wait_ge(t3_ready.sem, t3_ready.at(at))
                    for s, (r, _, other, _, _, _, _) in enumerate(sources):
                        dve.wait_ge(pr.filled.sem, pr.filled.at(at, s + 1))
                        k = pr.tile_read(s)
                        if k > 0 or at.has(1):
                            dve.wait_ge(pr.contracted.sem, pr.contracted.at(at, k))
                        x = other[0][at.b][0:r, :] if len(other) == 1 else other[0][at.b][0:r, other[1], :]
                        dve.tensor_tensor(pr.tile(s)[0:r, :], pr.bank(s)[0:r, :], x, ALU.mult
                                          ).then_inc(pr.multiplied.sem, 1)
                        if s == 0:
                            sc.dve(dve, at)
                        if s == 17 and not at.last(n):
                            split(at.next())
                walk(dve, n, body)

            @block.tensor
            def _(pe):
                for k, (part, m) in enumerate((("wm_s", P), ("wm_v", 97))):
                    for h in range(2):
                        ins = pe.matmul(front[k][0:m, 0:D], w[part][:, h * m:(h + 1) * m],
                                        w["wu"][:, h * D:(h + 1) * D], start=h == 0, stop=h == 1)
                    ins.then_inc(folded, 1)
                pe.wait_ge(fold_ready, 2)
                pe.wait_ge(const, 4)

                def turn(at):
                    pe.wait_ge(spread.sem, spread.at(at))
                    for k, (lo_, hi_) in enumerate(((0, P), (P, 224))):
                        for t in range(T):
                            ins = pe.transpose(front[k][0:hi_ - lo_, t * P:(t + 1) * P],
                                               XX[at.b][:, t, lo_:hi_], core.eye)
                        ins.then_inc(turned.sem, 1)

                def t3(at):
                    pe.wait_ge(x_ready.sem, x_ready.at(at))
                    pe.wait_ge(rest.sem, rest.at(at))
                    for q in range(2):
                        pe.matmul(front[q][:, :], hi["w3"][:, q * P:(q + 1) * P], XH[at.b][:, :],
                                  start=True, stop=False)
                        pe.matmul(front[q][:, :], lo["w3"][:, q * P:(q + 1) * P], XH[at.b][:, :],
                                  start=False, stop=True).then_inc(t3_done.sem, 1)

                def mix(at, after):
                    pe.wait_ge(t3_ready.sem, t3_ready.at(after))
                    pe.wait_ge(sums.sem, sums.at(at))
                    for t in range(T):
                        o = front[t // 2][:, (t % 2) * D:(t % 2 + 1) * D]
                        pe.matmul(o, US[at.b][:, t * P:(t + 1) * P], fold_s[:, :], start=True, stop=False)
                        ins = pe.matmul(o, UV[at.b][:, t * P:(t + 1) * P], fold_v[:, :], start=False, stop=True)
                        if t % 2:
                            ins.then_inc(mixed.sem, 1)

                def body(at):
                    if at.first():
                        turn(at)
                        t3(at)
                    for s in range(pr.ns + pr.lag):
                        if s < pr.ns:
                            _, sel, _, lhs, _, _, _ = sources[s]
                            k = pr.bank_read(s)
                            if k > 0 or at.has(1):
                                pe.wait_ge(pr.multiplied.sem, pr.multiplied.at(at, k))
                            m = lhs.shape[0]
                            pe.matmul(pr.bank(s)[0:m, :], hi["gather"][:, sel * P:sel * P + m], EH[at.b][:, :],
                                      start=True, stop=True).then_inc(pr.filled.sem, 1)
                        m = s - pr.lag
                        if m == 0 and at.has(1):
                            pe.wait_ge(sums.sem, sums.at(at.back(1)))
                        if m >= 0:
                            r, _, _, lhs, acc, r0, start = sources[m]
                            pe.wait_ge(pr.multiplied.sem, pr.multiplied.at(at, m + 1))
                            pe.matmul(acc[r0:r0 + lhs.shape[1], :], lhs, pr.tile(m)[0:r, :], start=start,
                                      stop=True, skip_group_check=True).then_inc(pr.contracted.sem, 1)
                        if s == 3 and not at.first():
                            mix(at.back(1), at)
                        if s == 9 and not at.first():
                            sc.pe(pe, at.back(1))
                        if s == 14 and not at.last(n):
                            if at.first():
                                pe.wait_ge(t3_ready.sem, t3_ready.at(at))
                            else:
                                pe.wait_ge(sc.out_ready.sem, sc.out_ready.at(at.back(1)))
                            turn(at.next())
                        if s == 20 and not at.last(n):
                            t3(at.next())
                    if at.last(n):
                        if at.has(1):
                            pe.wait_ge(sc.out_ready.sem, sc.out_ready.at(at.back(1)))
                        mix(at, at)
                        sc.pe(pe, at)
                walk(pe, n, body)
def edges_conv(core, name, table, hidden_in, c1, out_table, norm):
    nc, d, n = core.nc, core.d, core.edge_groups
    width = AW if norm else D
    n_out = D + 1 if norm else D
    k96, l2 = 1 / np.sqrt(96), PACKS[name]["l2"][1]
    c_l2 = 1.0 if norm else float(np.cos(np.pi / 8) / (np.sqrt(8.0) * np.sqrt(96.0)))
    with ExitStack() as ctx:
        W, w, hi, _ = load_pack(core, ctx, name,
                                feature_scales("l1", 288) + [
                                    ("fc2", 0, P, 0, 192, 1 / 8 if norm else 1 / 10),
                                    ("l2", 0, 64, 0, AW, c_l2), ("l2", 64, 96, 0, AW, c_l2 / np.sqrt(3.0)),
                                    ("l2", 0, 96, AW, 4 * AW, c_l2)],
                                {"gather": False})
        AT = [sbuf(nc, ctx, f"{name}_at{b}", [P, GR]) for b in range(2)]
        AH = [sbuf(nc, ctx, f"{name}_ah{b}", [P, GR], F32R) for b in range(2)]
        XT = [sbuf(nc, ctx, f"{name}_xt{b}", [HALF, 2, GR]) for b in range(2)]
        HN = [sbuf(nc, ctx, f"{name}_hn{b}", [P, T, D]) for b in range(2)] if norm else None
        HS = [sbuf(nc, ctx, f"{name}_hs{b}", [P, GR]) for b in range(2)]
        WW = [sbuf(nc, ctx, f"{name}_ww{b}", [96, 2, GR]) for b in range(2)]
        PQ = [sbuf(nc, ctx, f"{name}_pq{i}", [96, 2, GR]) for i in range(2)]
        SV = [sbuf(nc, ctx, f"{name}_sv{b}", [96, 6, GR]) for b in range(2)]
        front = banks(nc, ctx, f"{name}_front", 2)
        mlp, = banks(nc, ctx, f"{name}_mlp", 1)
        EB = banks(nc, ctx, f"{name}_eb", 2)
        GB = banks(nc, ctx, f"{name}_gb", 2)

        ga = Gather(core, ctx, name, table, "src")
        gz = Gather(core, ctx, name + "z", "Z", "src" if norm else "dst", 1)
        sc = Scatter(core, ctx, name, out_table, "dst", width, front)
        at_in = core.moves(f"{name}_at_in", 3)
        at_hi = core.count(f"{name}_at_hi", 1)
        at_lo = core.count(f"{name}_at_lo", 1)
        turned = core.count(f"{name}_turned", 2)
        x_ready = core.count(f"{name}_x_ready", 2)
        gated = core.count(f"{name}_gated", 3)
        gate_out = core.count(f"{name}_gate_out", 3)
        filled = core.count(f"{name}_filled", 9)
        made = core.count(f"{name}_made", 12)
        mixed = core.count(f"{name}_mixed", 2)
        const = core.sem(f"{name}_const")
        if norm:
            st = [sbuf(nc, ctx, f"{name}_st{b}", [P, T, 6]) for b in range(2)]
            mv = [sbuf(nc, ctx, f"{name}_mv{b}", [P, T, 2]) for b in range(2)]
            sd = [sbuf(nc, ctx, f"{name}_sd{b}", [P, T]) for b in range(2)]
            rs = [sbuf(nc, ctx, f"{name}_rs{b}", [P, T]) for b in range(2)]
            eps = sbuf(nc, ctx, f"{name}_eps", [P, 1])
            stats = core.count(f"{name}_stats", T)
            means = core.count(f"{name}_means", T)
            std = core.count(f"{name}_std", 1)
            inv = core.count(f"{name}_inv", 1)
            centred = core.count(f"{name}_centred", T)
            h_ready = core.count(f"{name}_h_ready", T)

        with nc.Block() as block:
            @block.gpsimd
            def _(pool):
                def body(at):
                    if at.first():
                        ga.pool(pool, at)
                        gz.pool(pool, at)
                    if not at.last(n):
                        if norm:
                            if at.has(1):
                                pool.wait_ge(h_ready.sem, h_ready.at(at.back(1)))
                            apart(core, pool, at)
                        else:
                            if at.has(1):
                                pool.wait_ge(turned.sem, turned.at(at.back(1)))
                            apart(core, pool, at)
                        ga.pool(pool, at.next())
                        if not norm:
                            if at.has(1):
                                pool.wait_ge(sc.u_ready.sem, sc.u_ready.at(at.back(1)))
                            apart(core, pool, at)
                        gz.pool(pool, at.next())
                    if not at.first():
                        sc.pool(pool, at.back(1))
                    if at.last(n):
                        sc.pool(pool, at)
                        for q in (at, at.back(1)):
                            pool.wait_ge(sc.added.of(q), sc.added.at(q))
                            apart(core, pool, q)
                walk(pool, n, body)

            @block.sync
            def _(sp):
                sp.wait_ge(const, 2)

                def body(at):
                    if at.has(2):
                        sp.wait_ge(at_lo.sem, at_lo.at(at.back(2)))
                    if at.has(2):
                        sp.wait_ge(gated.sem, gated.at(at.back(2), 1))
                    cols = bass.ds(at.g * GR, GR)
                    k = d[hidden_in].shape[0]
                    sp.dma_start(AT[at.b][0:k, :], d[hidden_in][:, cols]).then_inc(at_in.of(at), 16)
                    for r0 in (32, 64):
                        sp.dma_start(AT[at.b][r0:r0 + 4, :], d["ea4"][:, cols]).then_inc(at_in.of(at), 16)
                    sc.sp(sp, at)
                walk(sp, n, body)

            @block.scalar
            def _(act):
                act.wait_ge(const, 5 if norm else 2)

                def root(at):
                    if norm:
                        act.wait_ge(means.sem, means.at(at))
                        act.activation(sd[at.b][:, :], mv[at.b][:, :, 1], ACT.Sqrt, bias=eps[:, 0:1]
                                       ).then_inc(std.sem, 1)

                def start(at):
                    act.wait_ge(at_in.of(at), at_in.at(at))
                    act.activation(AH[at.b][:, :], AT[at.b][:, :], ACT.Copy).then_inc(at_hi.sem, 1)
                    act.wait_ge(gated.sem, gated.at(at, 1))
                    act.activation(HS[at.b][:, :], mlp[:, :], ACT.Silu, scale=float(c1)).then_inc(gate_out.sem, 1)
                    act.wait_ge(gated.sem, gated.at(at, 2))
                    act.activation(WW[at.b][:, 0, :], mlp[0:96, :], ACT.Copy).then_inc(gate_out.sem, 1)
                    for h in range(2):
                        act.wait_ge(turned.sem, turned.at(at, h + 1))
                        act.activation(XT[at.b][:, h, :], front[h][0:HALF, :], ACT.Copy).then_inc(x_ready.sem, 1)
                    act.wait_ge(gated.sem, gated.at(at, 3))
                    act.activation(WW[at.b][:, 1, :], mlp[0:96, :], ACT.Copy).then_inc(gate_out.sem, 1)

                def finish(at):
                    for h in range(2):
                        act.wait_ge(mixed.sem, mixed.at(at, h + 1))
                        if norm:
                            act.activation(sc.U[at.b][:, 2 * h:2 * h + 2, 0:n_out],
                                           front[h][:, 0:2 * n_out].rearrange("p (t c) -> p t c", t=2), ACT.Copy
                                           ).then_inc(sc.u_ready.sem, 1)
                        else:
                            for t in (2 * h, 2 * h + 1):
                                act.wait_ge(gz.here.of(at), gz.here.at(at))
                                ins = act.activation(sc.U[at.b][:, t, :], front[h][:, (t % 2) * D:(t % 2 + 1) * D],
                                                     ACT.Copy, scale=gz.rows[at.b][:, t, 0:1])
                            ins.then_inc(sc.u_ready.sem, 1)
                    sc.act(act, at)

                def body(at):
                    if at.first():
                        root(at)
                        start(at)
                    if not at.last(n):
                        root(at.next())
                    if not at.first():
                        finish(at.back(1))
                    if not at.last(n):
                        start(at.next())
                    else:
                        finish(at)
                walk(act, n, body)

            @block.vector
            def _(dve):
                for b in range(2):
                    dve.memset(AT[b][:, :], 0.0).then_inc(const, 1)
                if norm:
                    dve.memset(eps[:, :], EPS).then_inc(const, 1)
                    for b in range(2):
                        dve.memset(sc.U[b][:, :, D + 1:AW], 1.0).then_inc(const, 1)

                def statistics(at):
                    if norm:
                        dve.wait_ge(ga.here.of(at), ga.here.at(at))
                        if at.has(2):
                            dve.wait_ge(std.sem, std.at(at.back(2)))
                        for t in range(T):
                            dve.bn_stats(st[at.b][:, t, :], ga.rows[at.b][:, t, :]).then_inc(stats.sem, 1)
                        for t in range(T):
                            dve.wait_ge(stats.sem, stats.at(at, t + 1))
                            apart(core, dve, at)
                            dve.bn_aggr(mv[at.b][:, t, :], st[at.b][:, t, :]).then_inc(means.sem, 1)

                def prepare(at):
                    if norm:
                        dve.wait_ge(std.sem, std.at(at))
                        dve.reciprocal(rs[at.b][:, :], sd[at.b][:, :]).then_inc(inv.sem, 1)
                        dve.wait_ge(inv.sem, inv.at(at))
                        if at.has(2):
                            dve.wait_ge(turned.sem, turned.at(at.back(2)))
                        for t in range(T):
                            dve.tensor_scalar(HN[at.b][:, t, :], ga.rows[at.b][:, t, :], mv[at.b][:, t, 0:1],
                                              rs[at.b][:, t:t + 1], ALU.subtract, ALU.mult
                                              ).then_inc(centred.sem, 1)
                        dve.wait_ge(gz.here.of(at), gz.here.at(at))
                        for t in range(T):
                            dve.wait_ge(centred.sem, centred.at(at, t + 1))
                            dve.tensor_scalar(HN[at.b][:, t, :], HN[at.b][:, t, :], 0.0, gz.rows[at.b][:, t, :],
                                              ALU.max, ALU.mult).then_inc(h_ready.sem, 1)
                    dve.wait_ge(at_hi.sem, at_hi.at(at))
                    dve.tensor_tensor(AH[at.b][64:96, :], AT[at.b][64:96, :], AH[at.b][64:96, :].bitcast(F32),
                                      ALU.subtract).then_inc(at_lo.sem, 1)

                def products(at):
                    dve.wait_ge(gate_out.sem, gate_out.at(at))
                    if at.has(2):
                        dve.wait_ge(mixed.sem, mixed.at(at.back(2)))
                    for m in range(3):
                        t = PQ[m % 2]
                        for q in range(2):
                            dve.wait_ge(filled.sem, filled.at(at, 3 * m + 2 + q))
                            if m < 2 and at.has(1):
                                dve.wait_ge(made.sem, made.at(at.back(1), 12 - 4 * m))
                            if m == 2:
                                dve.wait_ge(made.sem, made.at(at, 4))
                            dve.tensor_tensor(t[:, q, :], WW[at.b][:, q, :], GB[q][0:96, :], ALU.mult
                                              ).then_inc(made.sem, 1)
                        for q in range(2):
                            dve.wait_ge(made.sem, made.at(at, 4 * m + 1 + q))
                            dve.wait_ge(filled.sem, filled.at(at, 3 * m + 1))
                            dve.tensor_tensor(SV[at.b][:, 3 * q + m, :], t[:, q, :], EB[m % 2][0:96, :], ALU.mult
                                              ).then_inc(made.sem, 1)

                def body(at):
                    if at.first():
                        statistics(at)
                        prepare(at)
                    sc.dve(dve, at)
                    if not at.last(n):
                        statistics(at.next())
                    products(at)
                    if not at.last(n):
                        prepare(at.next())
                walk(dve, n, body)

            @block.tensor
            def _(pe):
                pe.wait_ge(const, 2)

                def turn(at):
                    if norm:
                        pe.wait_ge(h_ready.sem, h_ready.at(at))
                    else:
                        pe.wait_ge(ga.here.of(at), ga.here.at(at))
                    src = HN[at.b] if norm else ga.rows[at.b]
                    for h in range(2):
                        for t in range(T):
                            ins = pe.transpose(front[h][0:HALF, t * P:(t + 1) * P],
                                               src[:, t, h * HALF:(h + 1) * HALF], core.eye)
                        ins.then_inc(turned.sem, 1)

                def gates(at, k):
                    if k == 0:
                        pe.wait_ge(at_in.of(at), at_in.at(at))
                        if at.has(1):
                            pe.wait_ge(gate_out.sem, gate_out.at(at.back(1)))
                        pe.matmul(mlp[:, :], w["fc1"], AT[at.b][:, :], start=True, stop=True
                                  ).then_inc(gated.sem, 1)
                    else:
                        pe.wait_ge(gate_out.sem, gate_out.at(at, k))
                        pe.matmul(mlp[0:96, :], w["fc2"][:, (k - 1) * 96:k * 96], HS[at.b][:, :],
                                  start=True, stop=True).then_inc(gated.sem, 1)

                def fill(at, m):
                    if m == 2:
                        pe.wait_ge(made.sem, made.at(at, 4))
                    elif at.has(1):
                        pe.wait_ge(made.sem, made.at(at.back(1), 12 - 4 * m))
                    for h in range(2):
                        ins = pe.matmul(EB[m % 2][0:96, :], w["l1"][:, h * 288 + m * 96:h * 288 + (m + 1) * 96],
                                        XT[at.b][:, h, :], start=h == 0, stop=h == 1)
                    ins.then_inc(filled.sem, 1)
                    for q in range(2):
                        k = 4 * (m - 1) + 1 + q
                        if k > 0 or at.has(1):
                            pe.wait_ge(made.sem, made.at(at, k))
                        k = 3 * q + m
                        pe.matmul(GB[q][0:96, :], hi["gather"][:, k * 96:(k + 1) * 96], AH[at.b][:, :],
                                  start=True, stop=True).then_inc(filled.sem, 1)

                def mix(at):
                    pe.wait_ge(made.sem, made.at(at))
                    for t in range(T):
                        for k in range(6):
                            part = 1 + k if k < 3 else 0
                            ins = pe.matmul(front[t // 2][:, (t % 2) * n_out:(t % 2 + 1) * n_out],
                                            SV[at.b][:, k, t * P:(t + 1) * P],
                                            w["l2"][:, part * AW:part * AW + n_out], start=k == 0, stop=k == 5)
                        if t % 2:
                            ins.then_inc(mixed.sem, 1)

                def body(at):
                    if at.first():
                        turn(at)
                        for k in range(3):
                            gates(at, k)
                    pe.wait_ge(at_lo.sem, at_lo.at(at))
                    pe.wait_ge(x_ready.sem, x_ready.at(at))
                    fill(at, 0)
                    if not at.last(n):
                        gates(at.next(), 0)
                    if not at.first():
                        mix(at.back(1))
                    fill(at, 1)
                    if not at.first():
                        sc.pe(pe, at.back(1))
                    fill(at, 2)
                    if not at.last(n):
                        gates(at.next(), 1)
                        if not at.first():
                            if at.has(1):
                                pe.wait_ge(sc.out_ready.sem, sc.out_ready.at(at.back(1)))
                        else:
                            pe.wait_ge(x_ready.sem, x_ready.at(at))
                        turn(at.next())
                        gates(at.next(), 2)
                    else:
                        if at.has(1):
                            pe.wait_ge(sc.out_ready.sem, sc.out_ready.at(at.back(1)))
                        mix(at)
                        sc.pe(pe, at)
                walk(pe, n, body)


def edges1(core):
    edges_conv(core, "e1", "X1", "ea16", 1 / 4, "AGG", True)


def edges2(core):
    edges_conv(core, "e2", "H", "ea12", 1 / np.sqrt(12.0), "X3", False)


def nodes1(core):
    nc, d, n = core.nc, core.d, core.node_groups
    with ExitStack() as ctx:
        sin8 = float(np.sin(np.pi / 8))
        W, w, _, _ = load_pack(core, ctx, "n1", feature_scales("sc", D) +
                               [(p, a, b, c, e, v * sin8) for p, a, b, c, e, v in feature_scales("sc2", D)], {})
        some = lambda count, tag, shape: [sbuf(nc, ctx, f"n1_{tag}{b}", shape) for b in range(count)]
        X, A, Z = some(4, "x", [P, T * D]), some(4, "a", [P, T * AW]), some(4, "z", [P, T])
        X2, ZB = some(4, "x2", [P, T * D]), some(4, "zb", [P, T])
        Y, ZH = some(2, "y", [P, T * D]), some(2, "zh", [P, T * D])
        cf, tmp = some(2, "cf", [P, 5, T]), some(2, "tmp", [P, T * D])
        eps = sbuf(nc, ctx, "n1_eps", [P, 1])
        a, b = Norm(core, ctx, "n1a", T, eps), Norm(core, ctx, "n1b", T, eps)
        x_in = core.moves("n1_x_in", 3, buffers=4)
        y_out, h_out = core.moves("n1_y_out"), core.moves("n1_h_out")
        const = core.sem("n1_const")
        coef = core.count("n1_coef", 5)
        scaled = core.count("n1_scaled", T)
        summed = core.count("n1_summed", T)
        zb_ready = core.count("n1_zb_ready", 1)
        y_ready = core.count("n1_y_ready", T)
        zh_ready = core.count("n1_zh_ready", T)
        rows = lambda x, at: x[bass.ds(at.g * GR, GR), :].rearrange("(p t) c -> p (t c)", t=T)

        with nc.Block() as block:
            @block.sync
            def _(sp):
                def body(at):
                    if at.within(0, n):
                        if at.has(4):
                            sp.wait_ge(zb_ready.sem, zb_ready.at(at.back(4)))
                        sp.dma_start(X[at.rest][:, :], rows(d["X1"], at)).then_inc(x_in.of(at), 16)
                        sp.dma_start(A[at.rest][:, :], rows(d["AGG"], at)).then_inc(x_in.of(at), 16)
                        sp.dma_start(Z[at.rest][:, :], rows(d["Z"], at)).then_inc(x_in.of(at), 16)
                    if at.within(5, n):
                        p = at.back(5)
                        sp.wait_ge(y_ready.sem, y_ready.at(p))
                        sp.dma_start(rows(d["X3"], p), Y[p.b][:, :]).then_inc(y_out.of(p), 16)
                walk(sp, n, body, unroll=4, lag=5)
                for q in (n - 1, n - 2):
                    sp.wait_ge(y_out.of(At.of(q)), y_out.at(At.of(q)))

            @block.gpsimd
            def _(pool):
                def body(at):
                    if at.within(3, n):
                        p = at.back(3)
                        pool.wait_ge(b.h_ready.sem, b.h_ready.at(p))
                        pool.wait_ge(zb_ready.sem, zb_ready.at(p))
                        if p.has(2):
                            pool.wait_ge(h_out.of(p.back(2)), h_out.at(p.back(2)))
                        apart(core, pool, p)
                        for t in range(T):
                            pool.tensor_scalar(ZH[p.b][:, t * D:(t + 1) * D], b.H[p.b][:, t * D:(t + 1) * D],
                                               ZB[p.rest][:, t:t + 1], None, ALU.mult).then_inc(zh_ready.sem, 1)
                        pool.wait_ge(zh_ready.sem, zh_ready.at(p))
                        apart(core, pool, p)
                        pool.dma_start(rows(d["H"], p), ZH[p.b][:, :]).then_inc(h_out.of(p), 16)
                walk(pool, n, body, unroll=4, lag=3)
                for q in (n - 1, n - 2):
                    pool.wait_ge(h_out.of(At.of(q)), h_out.at(At.of(q)))

            @block.scalar
            def _(act):
                act.wait_ge(const, 1)

                def body(at):
                    if at.within(2, n):
                        a.copies(act, at.back(2))
                    if at.within(4, n):
                        b.copies(act, at.back(4))
                    if at.within(1, n):
                        a.relu(act, at.back(1), X[at.back(1).rest])
                    if at.within(3, n):
                        p = at.back(3)
                        if p.has(2):
                            act.wait_ge(zh_ready.sem, zh_ready.at(p.back(2)))
                        b.relu(act, p, X2[p.rest])
                    if at.within(0, n):
                        a.root(act, at)
                    if at.within(2, n):
                        b.root(act, at.back(2))
                walk(act, n, body, unroll=4, lag=4)

            @block.vector
            def _(dve):
                dve.memset(eps[:, :], EPS).then_inc(const, 1)
                col = lambda x, c: x[:, :].rearrange("p (t c) -> p t c", t=T)[:, :, c]

                def coefficient(at, step):
                    f = cf[at.b]
                    if step:
                        dve.wait_ge(coef.sem, coef.at(at, step))
                    elif at.has(2):
                        dve.wait_ge(scaled.sem, scaled.at(at.back(2)))
                    if step == 0:
                        dve.tensor_scalar(f[:, 0, :], col(A[at.rest], D + 1), 1.0, None, ALU.max
                                          ).then_inc(coef.sem, 1)
                    if step == 1:
                        dve.reciprocal(f[:, 1, :], f[:, 0, :]).then_inc(coef.sem, 1)
                    if step == 2:
                        dve.tensor_tensor(f[:, 2, :], f[:, 1, :], Z[at.rest][:, :], ALU.mult).then_inc(coef.sem, 1)
                    if step == 3:
                        dve.scalar_tensor_tensor(f[:, 3, :], f[:, 2, :], 1 / 96, f[:, 2, :], ALU.mult, ALU.mult
                                                 ).then_inc(coef.sem, 1)
                    if step == 4:
                        dve.tensor_tensor(f[:, 4, :], f[:, 3, :], col(A[at.rest], D), ALU.mult
                                          ).then_inc(coef.sem, 1)

                def body(at):
                    if at.within(1, n):
                        a.factors(dve, at.back(1))
                    if at.within(3, n):
                        b.factors(dve, at.back(3))
                    if at.within(0, n):
                        dve.wait_ge(x_in.of(at), x_in.at(at))
                        a.statistics(dve, at, X[at.rest])
                        a.means_of(dve, at)
                    if at.within(2, n):
                        p = at.back(2)
                        coefficient(p, 0)
                        coefficient(p, 1)
                        coefficient(p, 2)
                        coefficient(p, 3)
                        coefficient(p, 4)
                        dve.wait_ge(coef.sem, coef.at(p))
                        for t in range(T):
                            c = slice(t * D, (t + 1) * D)
                            dve.scalar_tensor_tensor(tmp[p.b][:, c], A[p.rest][:, t * AW:t * AW + D],
                                                     cf[p.b][:, 4, t:t + 1], X[p.rest][:, c], ALU.mult, ALU.add
                                                     ).then_inc(scaled.sem, 1)
                        for t in range(T):
                            c = slice(t * D, (t + 1) * D)
                            dve.wait_ge(a.mixed.sem, a.mixed.at(p, t // 2 + 1))
                            dve.wait_ge(scaled.sem, scaled.at(p, t + 1))
                            dve.scalar_tensor_tensor(X2[p.rest][:, c], a.LP[t // 2][:, (t % 2) * D:(t % 2 + 1) * D],
                                                     Z[p.rest][:, t:t + 1], tmp[p.b][:, c], ALU.mult, ALU.add
                                                     ).then_inc(summed.sem, 1)
                        if p.has(4):
                            dve.wait_ge(zh_ready.sem, zh_ready.at(p.back(4)))
                        dve.tensor_copy(ZB[p.rest][:, :], Z[p.rest][:, :]).then_inc(zb_ready.sem, 1)
                        dve.wait_ge(summed.sem, summed.at(p))
                        b.statistics(dve, p, X2[p.rest])
                        b.means_of(dve, p)
                    if at.within(4, n):
                        p = at.back(4)
                        if p.has(2):
                            dve.wait_ge(y_out.of(p.back(2)), y_out.at(p.back(2)))
                        for t in range(T):
                            c = slice(t * D, (t + 1) * D)
                            dve.wait_ge(b.mixed.sem, b.mixed.at(p, t // 2 + 1))
                            dve.scalar_tensor_tensor(Y[p.b][:, c], b.LP[t // 2][:, (t % 2) * D:(t % 2 + 1) * D],
                                                     ZB[p.rest][:, t:t + 1], X2[p.rest][:, c], ALU.mult, ALU.add
                                                     ).then_inc(y_ready.sem, 1)
                walk(dve, n, body, unroll=4, lag=4)

            @block.tensor
            def _(pe):
                def body(at):
                    if at.within(2, n):
                        a.mix(pe, at.back(2), w["sc"], summed, 2)
                    if at.within(4, n):
                        b.mix(pe, at.back(4), w["sc2"], y_ready, 2)
                    if at.within(1, n):
                        a.turn(pe, at.back(1))
                    if at.within(3, n):
                        b.turn(pe, at.back(3))
                walk(pe, n, body, unroll=4, lag=4)


def edges3(core):
    nc, d, n, name = core.nc, core.d, core.edge_groups, "e3"
    YW = 2 * D + V
    with ExitStack() as ctx:
        yc = [("y", 0, 64, 0, YW, 1 / 8), ("y", 64, 96, 0, YW, 1 / np.sqrt(32.0)),
              ("y", 0, 64, YW, 2 * YW, 1 / np.sqrt(32.0)), ("y", 64, 96, YW, 2 * YW, 1 / np.sqrt(96.0))]
        W, w, hi, lo = load_pack(core, ctx, name, yc + [
            ("ss", 0, P, 0, 32 * S, 1 / 64), ("vv", 0, P, 0, 8 * S, 1 / (np.sqrt(3.0) * 32)),
            ("sv", 0, P, 0, 8 * P, 1 / np.sqrt(2048.0)), ("vs", 0, P, 0, 8 * P, 1 / np.sqrt(2048.0))],
            {"sv": True, "vs": True, "pick_s": False, "pick_v": False})
        two = lambda tag, shape, dt=F32: [sbuf(nc, ctx, f"e3_{tag}{b}", shape, dt) for b in range(2)]
        one = lambda tag, shape, dt=F32: sbuf(nc, ctx, f"e3_{tag}", shape, dt)
        ED = two("ed", [P, T * 4])
        RV = one("rv", [P, T, 96])
        GD = one("gd", [P, T, 96])
        XD = one("xd", [96, 2, GR])
        A = one("a", [P, T, D])
        AR = one("ar", [P, T, 96])
        XA = one("xa", [P, T, 4 * P])
        XX = one("xx", [P, T, 4 * P])
        A0, XS = two("a0", [P, GR]), one("xs", [P, GR])
        A1, XV = two("a1", [P, 3, GR]), two("xv", [P, 3, GR])
        A0H, XSH = two("a0h", [P, GR], F32R), two("xsh", [P, GR], F32R)
        XVH = two("xvh", [P, 3, GR], F32R)
        US, UV = one("us", [P, GR]), one("uv", [96, GR])
        front = banks(nc, ctx, "e3_front", 3)
        ring = banks(nc, ctx, "e3_ring", 3)
        AS, AV = banks(nc, ctx, "e3_acc", 2)

        gs, gd = Gather(core, ctx, "e3s", "H", "src"), Gather(core, ctx, "e3d", "H", "dst")
        sc = Scatter(core, ctx, name, "OUT", "src", D, [front[2], front[0]])
        ed_in = core.moves("e3_ed_in")
        vr = core.count("e3_vr", T)
        gd_ready = core.count("e3_gd_ready", 2)
        turned_d = core.count("e3_turned_d", 2)
        xd_ready = core.count("e3_xd_ready", 2)
        y_done = core.count("e3_y_done", T)
        a_scaled = core.count("e3_a_scaled", T)
        a_added = core.count("e3_a_added", 2 * T)
        a_ready = core.count("e3_a_ready", 1)
        spread = core.count("e3_spread", 8)
        turned = core.count("e3_turned", 8)
        out = core.count("e3_turned_out", 8)
        high = core.count("e3_high", 5)
        rest = core.count("e3_rest", 5)
        sums = core.count("e3_sums", 2)
        mixed = core.count("e3_mixed", 2)
        const = core.sem("e3_const")

        picked, applied = [], []
        for c in range(32):
            picked.append((("pick_s", c, XSH, None),
                           [(A0, None, w["ss"][:, c * S:(c + 1) * S], AS, 64 * (c % 2), c < 2)]))
        for c in range(8):
            for i in range(3):
                picked.append((("pick_v", c, XVH, i),
                               [(A1, i, w["vv"][:, c * S:(c + 1) * S], AS, 64 * ((c + i) % 2), False)]))
        for c in range(8):
            for part, rhs, other in (("sv", XSH, A1), ("vs", A0H, XV)):
                applied.append(((part, c, rhs, None),
                                [(other, i, w["sum"][:, c * V:(c + 1) * V], AV, 32 * i,
                                  c == 0 and part == "sv") for i in range(3)]))
        sources = []
        for c in range(8):
            sources += picked[7 * c:7 * c + 3] + [applied[2 * c]] + picked[7 * c + 3:7 * c + 7] + [applied[2 * c + 1]]
        part_of = lambda x, at, i: x[at.b][:, :] if i is None else x[at.b][:, i, :]
        pr = Plan(core, ctx, name, [len(x[1]) for x in sources], ring, 4, 2)

        with nc.Block() as block:
            @block.gpsimd
            def _(pool):
                def v_r(at):
                    pool.wait_ge(gd.here.of(at), gd.here.at(at))
                    pool.wait_ge(ed_in.of(at), ed_in.at(at))
                    if at.has(1):
                        pool.wait_ge(gd_ready.sem, gd_ready.at(at.back(1)))
                    apart(core, pool, at)
                    for t in range(T):
                        pool.tensor_tensor(RV[:, t, :].rearrange("p (u i) -> p u i", i=3),
                                           gd.rows[at.b][:, t, S:D].rearrange("p (u i) -> p u i", i=3),
                                           ED[at.b][:, 4 * t:4 * t + 3].unsqueeze(1).broadcast_to([P, V, 3]),
                                           ALU.mult).then_inc(vr.sem, 1)

                def body(at):
                    if at.first():
                        gd.pool(pool, at)
                        gs.pool(pool, at)
                        v_r(at)
                    if not at.last(n):
                        if at.has(1):
                            pool.wait_ge(turned_d.sem, turned_d.at(at.back(1)))
                        apart(core, pool, at)
                        gd.pool(pool, at.next())
                        if at.has(1):
                            pool.wait_ge(spread.sem, spread.at(at.back(1)))
                        apart(core, pool, at)
                        gs.pool(pool, at.next())
                        v_r(at.next())
                    if not at.first():
                        sc.pool(pool, at.back(1))
                    if at.last(n):
                        sc.pool(pool, at)
                        for q in (at, at.back(1)):
                            pool.wait_ge(sc.added.of(q), sc.added.at(q))
                            apart(core, pool, q)
                walk(pool, n, body)

            @block.sync
            def _(sp):
                def body(at):
                    if at.has(2):
                        sp.wait_ge(a_ready.sem, a_ready.at(at.back(2)))
                    sp.dma_start(ED[at.b][:, :], d["ea4_cols"][:, bass.ds(at.g * (4 * T), 4 * T)]
                                 ).then_inc(ed_in.of(at), 16)
                    sc.sp(sp, at)
                walk(sp, n, body)

            @block.scalar
            def _(act):
                act.wait_ge(const, 2)

                def spread_out(at, src, x, k0):
                    act.activation(x[:, :, 0:P].rearrange("p t (r a) -> p t r a", r=2),
                                   src[:, :, 0:S].unsqueeze(2).broadcast_to([P, T, 2, S]), ACT.Copy
                                   ).then_inc(spread.sem, 1)
                    for i in range(3):
                        v = src[:, :, S:D].rearrange("p t (u i) -> p t u i", i=3)[:, :, :, i]
                        act.activation(x[:, :, (1 + i) * P:(2 + i) * P].rearrange("p t (r u) -> p t r u", r=4),
                                       v.unsqueeze(2).broadcast_to([P, T, 4, V]), ACT.Copy
                                       ).then_inc(spread.sem, 1)

                def start(at):
                    act.wait_ge(gd.here.of(at), gd.here.at(at))
                    if at.has(1):
                        act.wait_ge(turned_d.sem, turned_d.at(at.back(1)))
                    act.activation(GD[:, :, 0:S], gd.rows[at.b][:, :, 96:D], ACT.Copy).then_inc(gd_ready.sem, 1)
                    act.wait_ge(gs.here.of(at), gs.here.at(at))
                    spread_out(at, gs.rows[at.b], XX, 0)
                    for h in range(2):
                        act.wait_ge(turned_d.sem, turned_d.at(at, h + 1))
                        act.activation(XD[:, h, :], front[(4 + h) % 3][0:96, :], ACT.Copy).then_inc(xd_ready.sem, 1)
                    for t in range(T):
                        act.wait_ge(y_done.sem, y_done.at(at, t + 1))
                        act.activation(A[:, t, :], front[t % 3][:, D:2 * D], ACT.Copy,
                                       scale=ED[at.b][:, 4 * t + 3:4 * t + 4]).then_inc(a_scaled.sem, 1)
                    targets = [XS[:, :]] + [XV[at.b][:, i, :] for i in range(3)] + \
                              [A0[at.b][:, :]] + [A1[at.b][:, i, :] for i in range(3)]
                    for k in range(8):
                        if k == 4:
                            act.wait_ge(a_ready.sem, a_ready.at(at))
                            spread_out(at, A, XA, 4)
                        act.wait_ge(turned.sem, turned.at(at, k + 1))
                        act.activation(targets[k], front[(10 + k) % 3][:, :], ACT.Copy).then_inc(out.sem, 1)
                        if k < 5:
                            h = (XSH[at.b][:, :], XVH[at.b][0:64, 0, :], XVH[at.b][0:64, 1, :],
                                 XVH[at.b][0:64, 2, :], A0H[at.b][:, :])[k]
                            act.wait_ge(out.sem, out.at(at, k + 1))
                            act.activation(h, targets[k][0:h.shape[0], :], ACT.Copy).then_inc(high.sem, 1)

                def finish(at):
                    act.wait_ge(pr.contracted.sem, pr.contracted.at(at))
                    act.activation(US[:, :], AS[:, :], ACT.Copy).then_inc(sums.sem, 1)
                    act.activation(UV[:, :], AV[0:96, :], ACT.Copy).then_inc(sums.sem, 1)
                    for h in range(2):
                        act.wait_ge(mixed.sem, mixed.at(at, h + 1))
                        act.activation(sc.U[at.b][:, 2 * h:2 * h + 2, :].rearrange("p t c -> p (t c)"),
                                       front[h][:, 0:2 * D], ACT.Copy).then_inc(sc.u_ready.sem, 1)
                    sc.act(act, at)

                def body(at):
                    if at.first():
                        start(at)
                    else:
                        finish(at.back(1))
                    if not at.last(n):
                        start(at.next())
                    else:
                        finish(at)
                walk(act, n, body)

            @block.vector
            def _(dve):
                for b in range(2):
                    dve.memset(XVH[b][64:128, :, :].bitcast(F32), 0.0).then_inc(const, 1)

                def dot(at):
                    dve.wait_ge(vr.sem, vr.at(at))
                    if at.has(1):
                        dve.wait_ge(turned_d.sem, turned_d.at(at.back(1)))
                    dve.tensor_reduce(GD[:, :, S:96], RV[:, :, :].rearrange("p t (u i) -> p t u i", i=3),
                                      AX.X, ALU.add).then_inc(gd_ready.sem, 1)

                def message(at, tiles):
                    for t in tiles:
                        dve.wait_ge(a_scaled.sem, a_scaled.at(at, t + 1))
                        dve.tensor_tensor(A[:, t, :], front[t % 3][:, 0:D], A[:, t, :], ALU.add
                                          ).then_inc(a_added.sem, 1)
                        dve.tensor_tensor(AR[:, t, :].rearrange("p (w i) -> p w i", i=3),
                                          over(front[t % 3][:, 2 * D:YW], 3),
                                          ED[at.b][:, 4 * t:4 * t + 3].unsqueeze(1).broadcast_to([P, V, 3]),
                                          ALU.mult).then_inc(a_added.sem, 1)
                    if T - 1 not in tiles:
                        return
                    dve.wait_ge(a_added.sem, a_added.at(at))
                    dve.tensor_tensor(A[:, :, S:D], A[:, :, S:D], AR[:, :, :], ALU.add).then_inc(a_ready.sem, 1)

                def remainders(at, ks):
                    pairs = [(XSH[at.b][64:128, :], XS[64:128, :])] + \
                            [(XVH[at.b][32:64, i, :], XV[at.b][32:64, i, :]) for i in range(3)] + \
                            [(A0H[at.b][64:128, :], A0[at.b][64:128, :])]
                    for k in ks:
                        dve.wait_ge(high.sem, high.at(at, k + 1))
                        dve.tensor_tensor(pairs[k][0], pairs[k][1], pairs[k][0].bitcast(F32), ALU.subtract
                                          ).then_inc(rest.sem, 1)

                def body(at):
                    if at.first():
                        dot(at)
                        message(at, range(T))
                        remainders(at, range(5))
                    dve.wait_ge(out.sem, out.at(at))
                    for s, (_, products) in enumerate(sources):
                        dve.wait_ge(pr.filled.sem, pr.filled.at(at, s + 1))
                        for j, (other, i, _, _, _, _) in enumerate(products):
                            m = pr.first[s] + j
                            k = pr.tile_read(m)
                            if k > 0 or at.has(1):
                                dve.wait_ge(pr.contracted.sem, pr.contracted.at(at, k))
                            dve.tensor_tensor(pr.tile(m)[:, :], pr.bank(s)[:, :], part_of(other, at, i), ALU.mult
                                              ).then_inc(pr.multiplied.sem, 1)
                        if s == 1:
                            sc.dve(dve, at)
                        if not at.last(n):
                            if s == 18:
                                dot(at.next())
                            if s == 30:
                                message(at.next(), (0, 1, 2))
                            if s == 34:
                                message(at.next(), (3,))
                            if s == 46:
                                remainders(at.next(), range(4))
                            if s == 64:
                                remainders(at.next(), range(4, 5))
                walk(dve, n, body)

            @block.tensor
            def _(pe):
                pe.wait_ge(const, 2)

                def turn_d(at):
                    if at.has(2):
                        pe.wait_ge(sc.out_ready.sem, sc.out_ready.at(at.back(2)))
                    if at.has(1):
                        pe.wait_ge(out.sem, out.at(at.back(1)))
                    pe.wait_ge(gd_ready.sem, gd_ready.at(at))
                    pe.wait_ge(gd.here.of(at), gd.here.at(at))
                    for h in range(2):
                        for t in range(T):
                            src = gd.rows[at.b][:, t, 0:96] if h == 0 else GD[:, t, :]
                            ins = pe.transpose(front[(4 + h) % 3][0:96, t * P:(t + 1) * P], src, core.eye)
                        ins.then_inc(turned_d.sem, 1)

                def message(at, tiles):
                    pe.wait_ge(xd_ready.sem, xd_ready.at(at))
                    for t in tiles:
                        if t == 3:
                            pe.wait_ge(a_added.sem, a_added.at(at, 2))
                        for h in range(2):
                            ins = pe.matmul(front[t % 3][:, 0:YW], XD[:, h, t * P:(t + 1) * P],
                                            w["y"][:, h * YW:(h + 1) * YW], start=h == 0, stop=h == 1)
                        ins.then_inc(y_done.sem, 1)

                def turn(at, ks):
                    for k in ks:
                        if k < 3:
                            pe.wait_ge(a_added.sem, a_added.at(at, 2 * (k + 2)))
                        else:
                            pe.wait_ge(out.sem, out.at(at, k - 2))
                        pe.wait_ge(spread.sem, spread.at(at, k + 1))
                        x = XX if k < 4 else XA
                        for t in range(T):
                            ins = pe.transpose(front[(10 + k) % 3][:, t * P:(t + 1) * P],
                                               x[:, t, (k % 4) * P:(k % 4 + 1) * P], core.eye)
                        ins.then_inc(turned.sem, 1)

                def mix(at, after):
                    pe.wait_ge(out.sem, out.at(after))
                    pe.wait_ge(sums.sem, sums.at(at))
                    for t in range(T):
                        o = front[t // 2][:, (t % 2) * D:(t % 2 + 1) * D]
                        pe.matmul(o, US[:, t * P:(t + 1) * P], w["out_s"], start=True, stop=False)
                        ins = pe.matmul(o, UV[:, t * P:(t + 1) * P], w["out_v"], start=False, stop=True)
                        if t % 2:
                            ins.then_inc(mixed.sem, 1)

                def body(at):
                    if at.first():
                        turn_d(at)
                        message(at, range(T))
                        turn(at, range(8))
                    pe.wait_ge(out.sem, out.at(at))
                    pe.wait_ge(rest.sem, rest.at(at))
                    for s in range(pr.ns + pr.lag):
                        if s < pr.ns:
                            part, c, rhs, i = sources[s][0]
                            k = pr.bank_read(s)
                            if k > 0 or at.has(1):
                                pe.wait_ge(pr.multiplied.sem, pr.multiplied.at(at, k))
                            x = part_of(rhs, at, i)
                            ins = pe.matmul(pr.bank(s)[:, :], hi[part][:, c * P:(c + 1) * P], x,
                                            start=True, stop=part not in lo)
                            if part in lo:
                                ins = pe.matmul(pr.bank(s)[:, :], lo[part][:, c * P:(c + 1) * P], x,
                                                start=False, stop=True)
                            ins.then_inc(pr.filled.sem, 1)
                        if s == pr.lag and at.has(1):
                            pe.wait_ge(sums.sem, sums.at(at.back(1)))
                        if s >= pr.lag:
                            for j, (_, _, lhs, acc, r0, start) in enumerate(sources[s - pr.lag][1]):
                                m = pr.first[s - pr.lag] + j
                                pe.wait_ge(pr.multiplied.sem, pr.multiplied.at(at, m + 1))
                                pe.matmul(acc[r0:r0 + lhs.shape[1], :], lhs, pr.tile(m)[:, :], start=start,
                                          stop=True, skip_group_check=True).then_inc(pr.contracted.sem, 1)
                        if s == 6 and not at.first():
                            mix(at.back(1), at)
                        if s == 12 and not at.first():
                            sc.pe(pe, at.back(1))
                        if not at.last(n):
                            if s == 20:
                                if at.has(1):
                                    pe.wait_ge(sc.out_ready.sem, sc.out_ready.at(at.back(1)))
                                turn_d(at.next())
                            if s == 30:
                                message(at.next(), (0, 1, 2))
                            if s == 33:
                                message(at.next(), (3,))
                            if s == 40:
                                turn(at.next(), range(4))
                            if s == 52:
                                turn(at.next(), range(4, 8))
                    if at.last(n):
                        if at.has(1):
                            pe.wait_ge(sc.out_ready.sem, sc.out_ready.at(at.back(1)))
                        mix(at, at)
                        sc.pe(pe, at)
                walk(pe, n, body)


def build_program(nc, d, n_nodes, n_edges, passes):
    with ExitStack() as ctx:
        core = Core(nc, ctx, d, n_nodes, n_edges)
        tiles = n_edges // P
        for name, dt, width in (("X1", F32, D), ("AGG", F32, AW), ("H", F32, D), ("X3", F32, D)):
            if name not in d:
                d[name] = nc.dram_tensor(f"table_{name}", [n_nodes, width], dt, kind="Internal").ap()
        core.cols = {e: sbuf(nc, ctx, f"cols_{e}", [P, tiles], I32) for e in ("src", "dst")}
        core.target = {e: sbuf(nc, ctx, f"target_{e}", [P, tiles], I32) for e in ("src", "dst")}
        off, width = offsets("ident")
        core.ident = sbuf(nc, ctx, "ident", [P, width])
        core.eye = core.ident[:, off["eye"]:off["eye"] + P]
        core.earlier = core.ident[:, off["earlier"]:off["earlier"] + P]
        core.spare = core.ident[:, off["spare"]:off["spare"] + 1]
        for one_pass in [index_pass] + passes:
            core.run(one_pass)


def pass_list():
    return [
        lambda c: plain_node_pass(c, "n0", "X", "X1", True),
        edges0,
        edges1,
        nodes1,
        edges2,
        lambda c: plain_node_pass(c, "n3", "X3", "OUT", False),
        edges3,
    ]


def halves(a):
    m = a.shape[1]
    return a.reshape(2, HALF, m).transpose(1, 0, 2).reshape(HALF, 2 * m)


def block_diagonal(ws, wv):
    out = np.zeros((D, D), np.float32)
    out[:S, :S] = ws
    for i in range(3):
        out[S + i::3, S + i::3] = wv
    return out


def pack_conv(name, fc1, fc2, l1_s, l1_v, l2_s, l2_v, alpha):
    first = np.zeros((P, P), np.float32)
    first[:fc1.shape[0], :fc1.shape[1]] = fc1
    w = fc2.reshape(fc2.shape[0], 192)
    second = np.zeros((P, 2, 96), np.float32)
    second[:w.shape[0], 0, :S], second[:w.shape[0], 0, S:] = w[:, 64:128], w[:, 128:160]
    second[:w.shape[0], 1, :S], second[:w.shape[0], 1, S:] = w[:, 0:64], w[:, 160:192]
    l1 = np.zeros((D, 3, 96), np.float32)
    for m in range(3):
        l1[:S, m, :S] = l1_s
        l1[S + m::3, m, S:] = l1_v
    l2 = np.zeros((96, 4, AW), np.float32)
    l2[:, 0, :S] = l2_s
    if alpha is not None:
        l2[:, 0, D] = alpha[:, 0]
    for m in range(3):
        l2[:, 1 + m, S + m:D:3] = l2_v
    g = np.zeros((P, 6, 96), np.float32)
    for r0 in (32, 64):
        for m in range(3):
            g[r0 + 1 + m, m, :S] = 1
            g[r0, m, S:] = 1
            g[r0 + 1 + m, 3 + m, S:] = 1
        g[r0, 3, :S] = 1
    return pack(name, fc1=first, fc2=second, l1=halves(l1.reshape(D, 288)), l2=l2, gather=g)


def host_arrays(i, n_nodes, n_edges):
    n, e = i["x"].shape[0], i["src"].shape[0]
    tiles = n_edges // P

    def rows(a, count):
        out = np.zeros((count,) + a.shape[1:], a.dtype)
        out[:a.shape[0]] = a
        return out

    d = {"X": rows(i["x"], n_nodes), "Z": rows(i["node_vec1"], n_nodes)}
    for end in ("src", "dst"):
        idx = np.full(n_edges, n_nodes - 1, np.int32)
        idx[:e] = i[end]
        d[f"{end}_rows"] = idx.reshape(1, -1)
        d[f"{end}_cols"] = np.ascontiguousarray(idx.reshape(tiles, P).T)
    across = lambda a: np.ascontiguousarray(rows(a, n_edges).T)
    d["ea32"] = across(i["edge_attr_32"])
    d["ea16"] = across(i["edge_attr_16"])
    d["ea12"] = across(i["edge_attr_12"])
    d["ea4"] = across(i["edge_attr_4"])
    d["ea4_cols"] = np.ascontiguousarray(rows(i["edge_attr_4"], n_edges).reshape(tiles, P, 4).transpose(1, 0, 2)
                                         .reshape(P, tiles * 4))

    q = np.arange(P)
    d["pack_ident"] = pack("ident", eye=np.eye(P), earlier=(q[None, :] < q[:, None]),
                           spare=(n + q)[:, None])

    g = lambda k: i["L0_gnn_" + k]
    W1, W2, W3, W4 = (g(f"W{k}") for k in (1, 2, 3, 4))
    w4 = np.zeros((3, V, 8, 3, V), np.float32)
    for k in range(3):
        w4[k, :, :, k, :] = W4
    wmT = g("Wm").T
    wm_v = np.concatenate([wmT[:, S:].reshape(D, V, 3).transpose(0, 2, 1).reshape(D, 96), g("bm")[:, None]], 1)
    sel = np.zeros((P, 26, P), np.float32)
    for r0 in (0, 32):
        for c in range(4):
            for j in range(2):
                sel[r0 + 2 * c + j, c, j * S:(j + 1) * S] = 1
        for b in range(8):
            for k in range(3):
                sel[r0 + 8 + 3 * b + k, 4 + b, k * V:(k + 1) * V] = 1
            sel[r0 + b, 12 + b, :96] = 1
        for k in range(3):
            for h in range(2):
                for b in range(4):
                    sel[r0 + 8 + 3 * (4 * h + b) + k, 20 + 2 * k + h, b * V:(b + 1) * V] = 1
    d["pack_e0"] = pack(
        "e0", w1=W1.reshape(S, 4, 2, S).transpose(2, 0, 1, 3), w2=np.tile(W2.reshape(V, 8 * S), (3, 1)),
        w4=w4, w3=np.tile(W3.reshape(S, 8 * V), (2, 1)), wm_s=halves(np.tile(wmT[:, :S], (1, 2))),
        wm_v=halves(wm_v), wu=halves(g("Wu")[D:]), gather=sel, sum=np.tile(np.eye(V), (4, 1)))
    lin = np.zeros((97, 2 * D), np.float32)
    lin[:HALF] = halves(g("Wu")[:D])
    lin[96, D:] = g("bu")
    d["pack_n0"] = pack("n0", lin=lin)

    g = lambda k: i["L1_gnn_" + k]
    d["pack_e1"] = pack_conv("e1", g("Wfc1"), g("Wfc2"), g("Wl1_0"), g("Wl1_1"), g("Wl2_s"), g("Wl2_v"), g("Wa"))
    h = lambda k: i["L2_gnn_" + k]
    d["pack_e2"] = pack_conv("e2", h("W_fc1"), h("W_fc2"), h("W_l1_0"), h("W_l1_1"), h("W_l2_0"), h("W_l2_1"), None)
    d["pack_n1"] = pack("n1", sc=halves(block_diagonal(g("Wsc0"), g("Wsc1"))),
                        sc2=halves(block_diagonal(h("W_sc0"), h("W_sc1"))))

    g = lambda k: i["L3_gnn_" + k]
    d["pack_n3"] = pack("n3", lin=halves(block_diagonal(g("Lu_s"), g("Lu_v"))))
    y = np.zeros((192, 2 * D + V), np.float32)
    y[:D, 0:D] = block_diagonal(g("Lm_s"), g("Lm_v"))
    y[:D, D:2 * D] = block_diagonal(g("Wm_ss"), g("Wm_vs"))
    y[:S, 2 * D:] = g("Wm_sv")
    y[D:, 0:S] = g("Wm_vv")
    pick_s = np.zeros((P, 32, 2, S), np.float32)
    for c in range(32):
        for j in range(2):
            for r0 in (0, 64):
                pick_s[r0 + 2 * c + j, c, j, :] = 1
    pick_v = np.zeros((P, 8, 4, V), np.float32)
    total = np.zeros((P, 8, V), np.float32)
    for c in range(8):
        for j in range(4):
            for r0 in (0, 32):
                pick_v[r0 + 4 * c + j, c, j, :] = 1
            total[j * V:(j + 1) * V, c, 4 * c + j] = 1
    out_v = np.zeros((3, V, D), np.float32)
    for k in range(3):
        out_v[k, np.arange(V), S + 3 * np.arange(V) + k] = 1
    d["pack_e3"] = pack(
        "e3", y=y.reshape(2, 96, 2 * D + V).transpose(1, 0, 2), ss=g("Wu_ss").reshape(32, 2, S, S).transpose(1, 2, 0, 3),
        vv=g("Wu_vv").reshape(8, 4, V, S).transpose(1, 2, 0, 3),
        sv=np.tile(g("Wu_sv").reshape(S, V, 8, 4).transpose(0, 2, 3, 1).reshape(S, 8 * P), (2, 1)),
        vs=np.tile(g("Wu_vs").reshape(V, S, 8, 4).transpose(1, 2, 3, 0).reshape(S, 8 * P), (2, 1)),
        pick_s=pick_s, pick_v=pick_v, sum=total,
        out_s=np.tile(np.eye(S, D), (2, 1)), out_v=out_v)
    return d


def kernel(**inputs):
    import concourse.bacc as bacc
    from concourse.bass_utils import run_bass_kernel_spmd

    inputs = {k: np.asarray(v) for k, v in inputs.items()}
    n, e = inputs["x"].shape[0], inputs["src"].shape[0]
    n_nodes, n_edges = -(-(n + P) // (2 * GR)) * 2 * GR, -(-e // GR) * GR
    arrays = host_arrays(inputs, n_nodes, n_edges)
    nc = bacc.Bacc("TRN2", target_bir_lowering=False, num_devices=1)
    d = {k: nc.dram_tensor(f"in_{k}", a.shape, mybir.dt.from_np(a.dtype), kind="ExternalInput").ap()
         for k, a in arrays.items()}
    d["OUT"] = nc.dram_tensor("out_x", [n_nodes, D], F32, kind="ExternalOutput").ap()
    build_program(nc, d, n_nodes, n_edges, pass_list())
    result = run_bass_kernel_spmd(nc, [{f"in_{k}": a for k, a in arrays.items()}], core_ids=[0])
    return result.results[0]["out_x"][:n]
```

```python
import numpy as np
import concourse.bass as bass
from concourse import mybir
from contextlib import ExitStack

F32, F32R, I32 = mybir.dt.float32, mybir.dt.float32r, mybir.dt.int32
ALU = mybir.AluOpType
ACT = mybir.ActivationFunctionType
AX = mybir.AxisListType
POOL, DVE = mybir.EngineType.Pool, mybir.EngineType.DVE

P = 128
T = 4
GR = T * P
S, V, D = 64, 32, 160
HALF = D // 2
AW = D + 2
EPS = 1e-5


class At:

    def __init__(self, g, rest, half, quarter):
        self.g, self.rest, self.half, self.quarter = g, rest, half, quarter
        self.b = rest % 2

    @staticmethod
    def of(g):
        return At(g, g % 4, g // 2, g // 4)

    def back(self, n):
        r = self.rest - n
        return At(self.g - n, r % 4, self.half + (r // 2 - self.rest // 2), 
                  None if self.quarter is None else self.quarter + r // 4)

    def next(self):
        return self.back(-1)

    def has(self, n):
        return not isinstance(self.g, int) or self.g >= n

    def within(self, n, count):
        return not isinstance(self.g, int) or n <= self.g < n + count

    def first(self):
        return isinstance(self.g, int) and self.g == 0

    def last(self, count):
        return isinstance(self.g, int) and self.g == count - 1


def walk(eng, count, body, unroll=2, lag=0, ahead=1):
    head = -(-(lag + 2) // unroll) * unroll
    turns = (count - ahead - head) // unroll
    for g in range(head):
        body(At.of(g))
    with eng.Fori(head // unroll, head // unroll + turns) as j:
        for r in range(unroll):
            if unroll == 2:
                body(At(j * 2 + r, r, j, None))
            else:
                body(At(j * 4 + r, r, j * 2 + r // 2, j))
    for g in range(head + turns * unroll, count + lag):
        body(At.of(g))


def apart(core, eng, at):
    if not isinstance(at.g, int):
        eng.sem_inc(core.passed[eng.engine], 1)


class Count:

    def __init__(self, sem, per):
        self.sem, self.per = sem, per

    def at(self, at, k=None):
        return at.g * self.per + (self.per if k is None else k)


class Moves:

    def __init__(self, sems, per=1):
        self.sems, self.per = sems, per

    def of(self, at):
        return self.sems[at.rest % len(self.sems)]

    def at(self, at, k=None):
        n = at.half if len(self.sems) == 2 else at.quarter
        return n * (16 * self.per) + 16 * (self.per if k is None else k)


class Core:

    def __init__(self, nc, ctx, d, n_nodes, n_edges):
        self.nc, self.ctx, self.d = nc, ctx, d
        self.nodes = n_nodes
        self.node_groups, self.edge_groups = n_nodes // GR, n_edges // GR

        self.passed = {e: nc.alloc_semaphore(name=f"passed_{e.name}") for e in (POOL, DVE)}
        self.pass_sems = []

    def sem(self, name):
        self.pass_sems.append(self.nc.alloc_semaphore(name=name))
        return self.pass_sems[-1]

    def run(self, one_pass):
        one_pass(self)
        self.nc.clear_and_free_semaphores(self.pass_sems)
        self.nc.all_engine_barrier()
        self.pass_sems = []

    def count(self, name, per):
        return Count(self.sem(name), per)

    def moves(self, name, per=1, buffers=2):
        return Moves([self.sem(f"{name}_{b}") for b in range(buffers)], per)


def sbuf(nc, ctx, name, shape, dt=F32):
    return ctx.enter_context(nc.sbuf_tensor(name, shape, dt))


def banks(nc, ctx, name, n):
    return [ctx.enter_context(nc.psum_tensor(f"{name}{i}", [P, 512], F32)) for i in range(n)]


def over(ap, n):
    p, m = ap.shape
    return ap.unsqueeze(2).broadcast_to([p, m, n])


PACKS = {
    "n0": {"lin": (97, 2 * D)},
    "e0": {"w1": (P, 4 * S), "w2": (96, 8 * S), "w4": (96, 8 * 96),
           "wm_s": (HALF, 2 * P), "wm_v": (HALF, 2 * 97), "wu": (HALF, 2 * D), "sum": (P, V),
           "w3": (P, 2 * P), "gather": (P, 26 * P)},
    "e1": {"fc1": (P, P), "fc2": (P, 192), "l1": (HALF, 2 * 3 * 96), "l2": (96, 4 * AW),
           "gather": (P, 6 * 96)},
    "n1": {"sc": (HALF, 2 * D), "sc2": (HALF, 2 * D)},
    "e2": {"fc1": (P, P), "fc2": (P, 192), "l1": (HALF, 2 * 3 * 96), "l2": (96, 4 * AW),
           "gather": (P, 6 * 96)},
    "n3": {"lin": (HALF, 2 * D)},
    "e3": {"y": (96, 2 * (2 * D + V)), "ss": (P, 32 * S), "vv": (P, 8 * S), "sum": (P, 8 * V),
           "out_s": (P, D), "out_v": (96, D), "sv": (P, 8 * P), "vs": (P, 8 * P),
           "pick_s": (P, 32 * P), "pick_v": (P, 8 * P)},
    "ident": {"eye": (P, P), "earlier": (P, P), "spare": (P, 1)},
}


def offsets(name):
    at, out = 0, {}
    for k, (_, w) in PACKS[name].items():
        out[k] = at
        at += w
    return out, at


def pack(name, **parts):
    off, width = offsets(name)
    out = np.zeros((P, width), np.float32)
    for k, (rows, w) in PACKS[name].items():
        out[:rows, off[k]:off[k] + w] = np.asarray(parts[k]).reshape(rows, w)
    return out


def feature_scales(part, width):
    return [(part, 0, S, 0, width, 1 / 8), (part, S, HALF, 0, width, 1 / np.sqrt(32.0)),
            (part, 0, HALF, width, 2 * width, 1 / np.sqrt(32.0))]


def load_pack(core, ctx, name, scales, halves):
    nc = core.nc
    off, width = offsets(name)
    kept = min([off[k] for k in halves], default=width)
    W = sbuf(nc, ctx, f"{name}_w", [P, kept])
    hi = {k: sbuf(nc, ctx, f"{name}_{k}_hi", list(PACKS[name][k]), F32R) for k in halves}
    lo = {k: sbuf(nc, ctx, f"{name}_{k}_lo", list(PACKS[name][k]), F32R) for k in halves if halves[k]}
    loaded, loaded_first, scaled, rounded = (core.sem(f"{name}_w_{x}") for x in
                                             ("loaded", "loaded_first", "scaled", "rounded"))
    with ExitStack() as while_loading:
        first = sbuf(nc, while_loading, f"{name}_w_first", [P, max(width - kept, 1)])

        def part(k, r0=0, r1=None, c0=0, c1=None):
            rows, columns = PACKS[name][k]
            tile, at = (first, off[k] - kept) if off[k] >= kept else (W, off[k])
            return tile[r0:rows if r1 is None else r1, at + c0:at + (columns if c1 is None else c1)]

        with nc.Block() as block:
            @block.sync
            def _(sp):
                sp.dma_start(W[:, :], core.d[f"pack_{name}"][:, 0:kept]).then_inc(loaded, 16)

            @block.scalar
            def _(act):
                if halves:
                    act.dma_start(first[:, :], core.d[f"pack_{name}"][:, kept:width]).then_inc(loaded_first, 16)
                    act.wait_ge(loaded_first, 16)
                for k in hi:
                    if k not in lo:
                        act.activation(hi[k][:, :], part(k), ACT.Copy).then_inc(rounded, 1)

            @block.vector
            def _(dve):
                dve.wait_ge(loaded, 16)
                if halves:
                    dve.wait_ge(loaded_first, 16)
                for k, r0, r1, c0, c1, c in scales:
                    o = part(k, r0, r1, c0, c1)
                    dve.tensor_scalar(o, o, float(c), None, ALU.mult).then_inc(scaled, 1)
                if scales:
                    dve.wait_ge(scaled, len(scales))
                for k in lo:
                    dve.tensor_copy(hi[k][:, :], part(k)).then_inc(rounded, 1)
                if lo:
                    dve.wait_ge(rounded, len(hi))
                for k in lo:
                    dve.tensor_tensor(lo[k][:, :], part(k), hi[k][:, :].bitcast(F32),
                                      ALU.subtract).then_inc(rounded, 1)
                if halves:
                    dve.wait_ge(rounded, len(hi) + len(lo))
    return W, {k: part(k) for k in PACKS[name] if off[k] < kept}, hi, lo


def load_tables(core):
    loaded = core.sem("tables_loaded")
    with core.nc.Block() as block:
        @block.sync
        def _(sp):
            for e in ("src", "dst"):
                sp.dma_start(core.cols[e][:, :], core.d[f"{e}_cols"]).then_inc(loaded, 16)
            sp.dma_start(core.ident[:, :], core.d["pack_ident"]).then_inc(loaded, 16)
            sp.wait_ge(loaded, 48)


class Norm:

    def __init__(self, core, ctx, name, tiles, eps, kb=HALF):
        nc = core.nc
        self.core, self.tiles, self.eps, self.kb = core, tiles, eps, kb
        self.pairs = tiles // 2
        self.chunks = tiles // 4
        two = lambda what, shape: [sbuf(nc, ctx, f"{name}_{what}{b}", shape) for b in range(2)]
        self.H = two("h", [P, tiles * D])
        self.HT = two("ht", [HALF if kb == HALF else P, self.chunks, 2, GR])
        self.st, self.mv = two("st", [P, tiles, 6]), two("mv", [P, tiles, 2])
        self.sd, self.rs, self.nm = two("sd", [P, tiles]), two("rs", [P, tiles]), two("nm", [P, tiles])
        self.TP = banks(nc, ctx, f"{name}_tp", 2 * self.chunks)
        self.LP = banks(nc, ctx, f"{name}_lp", self.pairs)
        self.stats = core.count(f"{name}_stats", tiles)
        self.means = core.count(f"{name}_means", tiles)
        self.std = core.count(f"{name}_std", 1)
        self.inv = core.count(f"{name}_inv", 2)
        self.h_ready = core.count(f"{name}_h_ready", tiles)
        self.turned = core.count(f"{name}_turned", 2 * self.chunks)
        self.ht_ready = core.count(f"{name}_ht_ready", 2 * self.chunks)
        self.mixed = core.count(f"{name}_mixed", self.pairs)

    def statistics(self, dve, at, x):
        b = at.b
        if at.has(2):
            dve.wait_ge(self.inv.sem, self.inv.at(at.back(2)))
            dve.wait_ge(self.std.sem, self.std.at(at.back(2)))
        for t in range(self.tiles):
            dve.bn_stats(self.st[b][:, t, :], x[:, t * D:(t + 1) * D]).then_inc(self.stats.sem, 1)

    def means_of(self, dve, at):
        for t in range(self.tiles):
            dve.wait_ge(self.stats.sem, self.stats.at(at, t + 1))
            apart(self.core, dve, at)
            dve.bn_aggr(self.mv[at.b][:, t, :], self.st[at.b][:, t, :]).then_inc(self.means.sem, 1)

    def root(self, act, at):
        act.wait_ge(self.means.sem, self.means.at(at))
        act.activation(self.sd[at.b][:, :], self.mv[at.b][:, :, 1], ACT.Sqrt, bias=self.eps[:, 0:1]
                       ).then_inc(self.std.sem, 1)

    def factors(self, dve, at):
        dve.wait_ge(self.std.sem, self.std.at(at))
        if at.has(2):
            dve.wait_ge(self.h_ready.sem, self.h_ready.at(at.back(2)))
        dve.reciprocal(self.rs[at.b][:, :], self.sd[at.b][:, :]).then_inc(self.inv.sem, 1)
        dve.wait_ge(self.inv.sem, self.inv.at(at, 1))
        dve.scalar_tensor_tensor(self.nm[at.b][:, :], self.mv[at.b][:, :, 0], -1.0, self.rs[at.b][:, :],
                                 ALU.mult, ALU.mult).then_inc(self.inv.sem, 1)

    def relu(self, act, at, x):
        act.wait_ge(self.inv.sem, self.inv.at(at))
        if at.has(2):
            act.wait_ge(self.turned.sem, self.turned.at(at.back(2)))
        for t in range(self.tiles):
            act.activation(self.H[at.b][:, t * D:(t + 1) * D], x[:, t * D:(t + 1) * D], ACT.Relu,
                           bias=self.nm[at.b][:, t:t + 1], scale=self.rs[at.b][:, t:t + 1]
                           ).then_inc(self.h_ready.sem, 1)

    def turn(self, pe, at):
        for c in range(self.chunks):
            for h in range(2):
                k = 2 * c + h
                if at.has(1):
                    pe.wait_ge(self.ht_ready.sem, self.ht_ready.at(at.back(1), k + 1))
                for t in range(4 * c, 4 * c + 4):
                    if h == 0:
                        pe.wait_ge(self.h_ready.sem, self.h_ready.at(at, t + 1))
                    ins = pe.transpose(self.TP[k][0:HALF, (t % 4) * P:(t % 4 + 1) * P],
                                       self.H[at.b][:, t * D + h * HALF:t * D + (h + 1) * HALF], self.core.eye)
                ins.then_inc(self.turned.sem, 1)

    def copies(self, act, at):
        if at.has(2):
            act.wait_ge(self.mixed.sem, self.mixed.at(at.back(2)))
        for c in range(self.chunks):
            for h in range(2):
                k = 2 * c + h
                act.wait_ge(self.turned.sem, self.turned.at(at, k + 1))
                act.activation(self.HT[at.b][0:HALF, c, h, :], self.TP[k][0:HALF, :], ACT.Copy
                               ).then_inc(self.ht_ready.sem, 1)

    def mix(self, pe, at, lin, added, per_pair):
        for q in range(self.pairs):
            if at.has(1):
                pe.wait_ge(added.sem, added.at(at.back(1), per_pair * (q + 1)))
            pe.wait_ge(self.ht_ready.sem, self.ht_ready.at(at, 2 * (q // 2) + 2))
            for t in (2 * q, 2 * q + 1):
                o = self.LP[q][:, (t % 2) * D:(t % 2 + 1) * D]
                x = self.HT[at.b][:, t // 4, :, (t % 4) * P:(t % 4 + 1) * P]
                pe.matmul(o, x[0:HALF, 0, :], lin[0:HALF, 0:D], start=True, stop=False)
                ins = pe.matmul(o, x[0:self.kb, 1, :], lin[0:self.kb, D:2 * D], start=False, stop=True)
            ins.then_inc(self.mixed.sem, 1)


def plain_node_pass(core, name, src, dst, with_agg):
    nc, d = core.nc, core.d
    kb = PACKS[name]["lin"][0]
    TN = 8
    n = core.nodes // (TN * P)
    with ExitStack() as ctx:
        W, w, _, _ = load_pack(core, ctx, name, feature_scales("lin", D) if name == "n3" else [], {})
        X = [sbuf(nc, ctx, f"{name}_x{b}", [P, TN * D]) for b in range(4)]
        Y = [sbuf(nc, ctx, f"{name}_y{b}", [P, TN * D]) for b in range(2)]
        eps = sbuf(nc, ctx, f"{name}_eps", [P, 1])
        zero = sbuf(nc, ctx, f"{name}_zero", [P, TN * AW])
        ln = Norm(core, ctx, name, TN, eps, kb)
        x_in = core.moves(f"{name}_x_in", buffers=4)
        h_out = core.moves(f"{name}_h_out")
        y_out = core.moves(f"{name}_y_out")
        zeroed = core.moves(f"{name}_zeroed")
        y_ready = core.count(f"{name}_y_ready", ln.pairs)
        const = core.sem(f"{name}_const")
        fold = core.sem(f"{name}_fold")
        rows = lambda a, at: a[bass.ds(at.g * (TN * P), TN * P), :].rearrange("(p t) c -> p (t c)", t=TN)
        n_const = 4 + 2 * (kb > HALF)
        with nc.Block() as block:
            @block.sync
            def _(sp):
                def body(at):
                    if at.within(0, n):
                        if at.has(4):
                            sp.wait_ge(y_ready.sem, y_ready.at(at.back(4)))
                        sp.dma_start(X[at.rest][:, :], rows(d[src], at)).then_inc(x_in.of(at), 16)
                    if at.within(3, n):
                        p = at.back(3)
                        sp.wait_ge(y_ready.sem, y_ready.at(p))
                        sp.dma_start(rows(d[dst], p), Y[p.b][:, :]).then_inc(y_out.of(p), 16)
                walk(sp, n, body, unroll=4, lag=3)
                for q in (n - 1, n - 2):
                    sp.wait_ge(y_out.of(At.of(q)), y_out.at(At.of(q)))

            @block.vector
            def _(dve):
                dve.memset(eps[:, :], EPS).then_inc(const, 1)
                dve.memset(zero[:, :], 0.0).then_inc(const, 1)
                for b in range(2):
                    if kb > HALF:
                        dve.memset(ln.HT[b][64:128, :, :, :], 0.0).then_inc(const, 1)
                    else:
                        dve.memset(ln.HT[b][64:HALF, :, :, :], 0.0).then_inc(const, 1)
                if kb > HALF:
                    dve.wait_ge(const, 4)
                    for b in range(2):
                        dve.memset(ln.HT[b][96:97, :, 1, :], 1.0).then_inc(const, 1)
                for h in range(2):
                    o = w["lin"][0:HALF, h * D + h * HALF:h * D + (h + 1) * HALF]
                    dve.tensor_tensor(o, o, core.eye[0:HALF, 0:HALF], ALU.add).then_inc(fold, 1)

                def body(at):
                    if at.within(0, n):
                        dve.wait_ge(x_in.of(at), x_in.at(at))
                        ln.statistics(dve, at, X[at.rest])
                    if at.within(1, n):
                        ln.factors(dve, at.back(1))
                    if at.within(0, n):
                        ln.means_of(dve, at)
                    if at.within(2, n):
                        p = at.back(2)
                        if p.has(2):
                            dve.wait_ge(y_out.of(p.back(2)), y_out.at(p.back(2)))
                        for q in range(ln.pairs):
                            c = slice(q * 2 * D, (q + 1) * 2 * D)
                            dve.wait_ge(ln.mixed.sem, ln.mixed.at(p, q + 1))
                            dve.tensor_tensor(Y[p.b][:, c], ln.LP[q][:, 0:2 * D], X[p.rest][:, c], ALU.add
                                              ).then_inc(y_ready.sem, 1)
                walk(dve, n, body, unroll=4, lag=2)

            @block.scalar
            def _(act):
                act.wait_ge(const, n_const)

                def body(at):
                    if at.within(2, n):
                        ln.copies(act, at.back(2))
                    if at.within(1, n):
                        p = at.back(1)
                        if p.has(2):
                            act.wait_ge(h_out.of(p.back(2)), h_out.at(p.back(2)))
                        ln.relu(act, p, X[p.rest])
                    if at.within(0, n):
                        ln.root(act, at)
                    if at.within(1, n):
                        p = at.back(1)
                        act.wait_ge(ln.h_ready.sem, ln.h_ready.at(p))
                        act.dma_start(rows(d["H"], p), ln.H[p.b][:, :]).then_inc(h_out.of(p), 16)
                        if with_agg:
                            act.dma_start(rows(d["AGG"], p), zero[:, :]).then_inc(zeroed.of(p), 16)
                walk(act, n, body, unroll=4, lag=2)
                for q in (n - 1, n - 2):
                    act.wait_ge(h_out.of(At.of(q)), h_out.at(At.of(q)))
                    if with_agg:
                        act.wait_ge(zeroed.of(At.of(q)), zeroed.at(At.of(q)))

            @block.tensor
            def _(pe):
                pe.wait_ge(fold, 2)
                pe.wait_ge(const, n_const)

                def body(at):
                    if at.within(2, n):
                        ln.mix(pe, at.back(2), w["lin"], y_ready, 1)
                    if at.within(1, n):
                        ln.turn(pe, at.back(1))
                walk(pe, n, body, unroll=4, lag=2)


class Gather:

    def __init__(self, core, ctx, name, table, end, width=D):
        self.core, self.table, self.end = core, table, end
        self.rows = [sbuf(core.nc, ctx, f"{name}_g{b}", [P, T, width]) for b in range(2)]
        self.index = [sbuf(core.nc, ctx, f"{name}_gi{b}", [P, T], I32) for b in range(2)]
        self.indexed = core.count(f"{name}_gather_index", 1)
        self.here = core.moves(f"{name}_gathered", T)

    def index_of(self, pool, at):
        if at.has(2):
            pool.wait_ge(self.here.of(at.back(2)), self.here.at(at.back(2)))
        apart(self.core, pool, at)
        pool.tensor_copy(self.index[at.b][:, :], self.core.cols[self.end][:, bass.ds(at.g * T, T)]
                         ).then_inc(self.indexed.sem, 1)
        pool.wait_ge(self.indexed.sem, self.indexed.at(at))
        apart(self.core, pool, at)

    def fetch(self, pool, at, t):
        pool.indirect_dma_start(self.rows[at.b][:, t, :], None, self.core.d[self.table],
                                bass.IndirectOffsetOnAxis(ap=self.index[at.b][:, t:t + 1], axis=0)
                                ).then_inc(self.here.of(at), 16)


class Scatter:

    def __init__(self, core, ctx, name, table, end, width, bank, placing=False):
        nc = core.nc
        self.core, self.table, self.end, self.width, self.bank = core, table, end, width, bank
        self.U = [sbuf(nc, ctx, f"{name}_u{b}", [P, T, width]) for b in range(2)]
        self.out = [sbuf(nc, ctx, f"{name}_so{b}", [P, T, width]) for b in range(2)]
        self.same = [sbuf(nc, ctx, f"{name}_sm{b}", [P, T, P]) for b in range(2)]
        self.near = [sbuf(nc, ctx, f"{name}_sr{b}", [P, GR], I32) for b in range(2)]
        self.index = [sbuf(nc, ctx, f"{name}_si{b}", [P, T], I32) for b in range(2)]
        self.near_in = core.moves(f"{name}_targets_in")
        self.same_ready = core.count(f"{name}_same_ready", 1)
        self.u_ready = core.count(f"{name}_u_ready", 2)
        self.merged = core.count(f"{name}_merged", 2)
        self.out_ready = core.count(f"{name}_out_ready", 2)
        self.indexed = core.count(f"{name}_scatter_index", 1)
        self.added = core.moves(f"{name}_added", T)
        self.placing = placing
        if placing:
            self.early = sbuf(nc, ctx, f"{name}_early", [P, T, P])
            self.rank, self.own = (sbuf(nc, ctx, f"{name}_{k}", [P, T]) for k in ("rank", "own"))
            self.off = sbuf(nc, ctx, f"{name}_off", [P, T])
            self.placed = core.count(f"{name}_placed", 7)

    def sp(self, sp, at):
        if at.has(2):
            sp.wait_ge(self.same_ready.sem, self.same_ready.at(at.back(2)))
        sp.dma_start(self.near[at.b][:, :], self.core.d[f"{self.end}_rows"][:, bass.ds(at.g * GR, GR)]
                     .broadcast_to([P, GR])).then_inc(self.near_in.of(at), 16)

    def dve(self, dve, at):
        dve.wait_ge(self.near_in.of(at), self.near_in.at(at))
        if at.has(2):
            dve.wait_ge(self.merged.sem, self.merged.at(at.back(2)))
        dve.tensor_tensor(self.same[at.b][:, :, :], self.near[at.b][:, :].rearrange("p (t q) -> p t q", t=T),
                          over(self.core.cols[self.end][:, bass.ds(at.g * T, T)], P), ALU.is_equal
                          ).then_inc(self.same_ready.sem, 1)

    def place(self, dve, at):
        core, placed = self.core, self.placed
        cols = core.cols[self.end][:, bass.ds(at.g * T, T)]
        dve.wait_ge(self.same_ready.sem, self.same_ready.at(at))
        dve.tensor_tensor(self.early[:, :, :], self.same[at.b][:, :, :],
                          core.earlier.unsqueeze(1).broadcast_to([P, T, P]), ALU.mult).then_inc(placed.sem, 1)
        dve.tensor_copy(self.own[:, :], cols).then_inc(placed.sem, 1)
        dve.wait_ge(placed.sem, placed.at(at, 1))
        dve.tensor_reduce(self.rank[:, :], self.early[:, :, :], AX.X, ALU.max).then_inc(placed.sem, 1)
        dve.wait_ge(placed.sem, placed.at(at, 2))
        dve.tensor_scalar(self.off[:, :], self.own[:, :], -1.0, core.spare, ALU.mult, ALU.add
                          ).then_inc(placed.sem, 1)
        dve.wait_ge(placed.sem, placed.at(at, 4))
        dve.tensor_tensor(self.off[:, :], self.rank[:, :], self.off[:, :], ALU.mult).then_inc(placed.sem, 1)
        dve.wait_ge(placed.sem, placed.at(at, 5))
        dve.tensor_tensor(self.own[:, :], self.own[:, :], self.off[:, :], ALU.add).then_inc(placed.sem, 1)
        dve.wait_ge(placed.sem, placed.at(at, 6))
        dve.tensor_copy(core.target[self.end][:, bass.ds(at.g * T, T)], self.own[:, :]).then_inc(placed.sem, 1)

    def pe(self, pe, at):
        pe.wait_ge(self.same_ready.sem, self.same_ready.at(at))
        pe.wait_ge(self.u_ready.sem, self.u_ready.at(at))
        for t in range(T):
            ins = pe.matmul(self.bank[t // 2][:, (t % 2) * self.width:(t % 2 + 1) * self.width],
                            self.same[at.b][:, t, :], self.U[at.b][:, t, :], start=True, stop=True)
            if t % 2:
                ins.then_inc(self.merged.sem, 1)

    def act(self, act, at):
        if at.has(2):
            act.wait_ge(self.added.of(at.back(2)), self.added.at(at.back(2)))
        for h in range(2):
            act.wait_ge(self.merged.sem, self.merged.at(at, h + 1))
            act.activation(self.out[at.b][:, 2 * h:2 * h + 2, :].rearrange("p t c -> p (t c)"),
                           self.bank[h][:, 0:2 * self.width], ACT.Copy).then_inc(self.out_ready.sem, 1)

    def index_of(self, pool, at):
        if at.has(2):
            pool.wait_ge(self.added.of(at.back(2)), self.added.at(at.back(2)))
        if self.placing:
            pool.wait_ge(self.placed.sem, self.placed.at(at))
        apart(self.core, pool, at)
        pool.tensor_copy(self.index[at.b][:, :], self.core.target[self.end][:, bass.ds(at.g * T, T)]
                         ).then_inc(self.indexed.sem, 1)
        pool.wait_ge(self.indexed.sem, self.indexed.at(at))
        apart(self.core, pool, at)

    def add(self, pool, at, t):
        if t:
            pool.wait_ge(self.added.of(at), self.added.at(at, t))
        else:
            pool.wait_ge(self.out_ready.sem, self.out_ready.at(at))
            if at.has(1):
                pool.wait_ge(self.added.of(at.back(1)), self.added.at(at.back(1)))
        apart(self.core, pool, at)
        pool.indirect_dma_start(self.core.d[self.table],
                                bass.IndirectOffsetOnAxis(ap=self.index[at.b][:, t:t + 1], axis=0),
                                self.out[at.b][:, t, :], None, compute_op=ALU.add
                                ).then_inc(self.added.of(at), 16)


class Plan:

    def __init__(self, core, ctx, name, counts, ring, tiles, lag):
        self.counts, self.ring, self.lag = counts, ring, lag
        self.F = [sbuf(core.nc, ctx, f"{name}_f{i}", [P, GR]) for i in range(tiles)]
        self.first = [sum(counts[:s]) for s in range(len(counts))]
        self.ns, self.nm = len(counts), sum(counts)
        self.filled = core.count(f"{name}_filled", self.ns)
        self.multiplied = core.count(f"{name}_multiplied", self.nm)
        self.contracted = core.count(f"{name}_contracted", self.nm)

    def bank(self, s):
        return self.ring[s % len(self.ring)]

    def tile(self, m):
        return self.F[m % len(self.F)]

    def bank_read(self, s):
        last = s - len(self.ring)
        if last >= 0:
            return self.first[last] + self.counts[last]
        last = max(x for x in range(self.ns) if x % len(self.ring) == s)
        return self.first[last] + self.counts[last] - self.nm

    def tile_read(self, m):
        last = m - len(self.F)
        if last >= 0:
            return last + 1
        return max(x for x in range(self.nm) if x % len(self.F) == m) + 1 - self.nm


def edges0(core):
    nc, d, n, name = core.nc, core.d, core.edge_groups, "e0"
    r2 = 1 / np.sqrt(2.0)
    with ExitStack() as ctx:
        W, w, hi, lo = load_pack(core, ctx, name,
                                 [("w1", 0, P, 0, 4 * S, r2 / np.sqrt(512)),
                                  ("w2", 0, 96, 0, 8 * S, r2 / (np.sqrt(3.0) * 16)),
                                  ("w4", 0, 96, 0, 8 * 96, r2 / 16), ("w3", 0, P, 0, 2 * P, r2 / np.sqrt(512))],
                                 {"w3": True, "gather": False})
        EA = [sbuf(nc, ctx, f"e0_ea{b}", [64, GR]) for b in range(2)]
        EH = [sbuf(nc, ctx, f"e0_eh{b}", [P, GR], F32R) for b in range(2)]
        XX = [sbuf(nc, ctx, f"e0_xx{b}", [P, T, 224]) for b in range(2)]
        XS = [sbuf(nc, ctx, f"e0_xs{b}", [P, GR]) for b in range(2)]
        XH = [sbuf(nc, ctx, f"e0_xh{b}", [P, GR], F32R) for b in range(2)]
        XV = [sbuf(nc, ctx, f"e0_xv{b}", [96, GR]) for b in range(2)]
        T3 = [sbuf(nc, ctx, f"e0_t3{b}", [P, 2, GR]) for b in range(2)]
        US = [sbuf(nc, ctx, f"e0_us{b}", [P, GR]) for b in range(2)]
        UV = [sbuf(nc, ctx, f"e0_uv{b}", [97, GR]) for b in range(2)]
        fold_s = sbuf(nc, ctx, "e0_fold_s", [P, D])
        fold_v = sbuf(nc, ctx, "e0_fold_v", [97, D])
        front = banks(nc, ctx, "e0_front", 2)
        ring = banks(nc, ctx, "e0_ring", 4)
        AS, AV = banks(nc, ctx, "e0_acc", 2)

        ga = Gather(core, ctx, name, "H", "dst")
        sc = Scatter(core, ctx, name, "X1", "src", D, front, placing=True)
        ea_in = core.moves("e0_ea_in", 2)
        spread = core.count("e0_spread", 2)
        turned = core.count("e0_turned", 2)
        x_ready = core.count("e0_x_ready", 3)
        ea_hi = core.count("e0_ea_hi", 1)
        rest = core.count("e0_rest", 2)
        t3_done = core.count("e0_t3_done", 2)
        t3_ready = core.count("e0_t3_ready", 2)
        sums = core.count("e0_sums", 2)
        mixed = core.count("e0_mixed", 2)
        folded, fold_ready, const = (core.sem(f"e0_{x}") for x in ("folded", "fold_ready", "const"))

        sources = []
        for c in range(4):
            sources.append((P, c, (XS,), w["w1"][:, c * S:(c + 1) * S], AS, 64 * (c % 2), c < 2))
        for c in range(8):
            sources.append((96, 4 + c, (XV,), w["w2"][:, c * S:(c + 1) * S], AS, 64 * (c % 2), False))
        for c in range(8):
            sources.append((96, 12 + c, (XV,), w["w4"][:, c * 96:(c + 1) * 96], AV, 0, c == 0))
        for i in range(3):
            for q in range(2):
                sources.append((P, 20 + 2 * i + q, (T3, q), w["sum"], AV, 32 * i, False))
        pr = Plan(core, ctx, name, [1] * len(sources), ring, 7, 4)

        with nc.Block() as block:
            @block.gpsimd
            def _(pool):
                for g in (0, 1):
                    ga.index_of(pool, At.of(g))
                    for t in range(T):
                        ga.fetch(pool, At.of(g), t)

                def body(at):
                    more = at.within(-2, n)
                    if more:
                        pool.wait_ge(spread.sem, spread.at(at))
                        ga.index_of(pool, at.back(-2))
                    if at.within(1, n):
                        sc.index_of(pool, at.back(1))
                    for t in range(T):
                        if more:
                            ga.fetch(pool, at.back(-2), t)
                        if at.within(1, n):
                            sc.add(pool, at.back(1), t)
                walk(pool, n, body, lag=1, ahead=2)
                for g in (n - 1, n - 2):
                    pool.wait_ge(sc.added.of(At.of(g)), sc.added.at(At.of(g)))

            @block.sync
            def _(sp):
                def body(at):
                    if at.has(2):
                        sp.wait_ge(rest.sem, rest.at(at.back(2)))
                    for h in range(2):
                        sp.dma_start(EA[at.b][32 * h:32 * h + 32, :], d["ea32"][:, bass.ds(at.g * GR, GR)]
                                     ).then_inc(ea_in.of(at), 16)
                    sc.sp(sp, at)
                walk(sp, n, body)

            @block.scalar
            def _(act):
                act.wait_ge(folded, 2)
                act.activation(fold_s[:, :], front[0][:, 0:D], ACT.Copy).then_inc(fold_ready, 1)
                act.activation(fold_v[:, :], front[1][0:97, 0:D], ACT.Copy).then_inc(fold_ready, 1)
                act.wait_ge(const, 4)

                def start(at):
                    act.wait_ge(ga.here.of(at), ga.here.at(at))
                    act.activation(XX[at.b][:, :, 0:P].rearrange("p t (r a) -> p t r a", r=2),
                                   ga.rows[at.b][:, :, 0:S].unsqueeze(2).broadcast_to([P, T, 2, S]), ACT.Copy
                                   ).then_inc(spread.sem, 1)
                    act.activation(XX[at.b][:, :, P:224].rearrange("p t (i a) -> p t i a", i=3),
                                   ga.rows[at.b][:, :, S:D].rearrange("p t (a i) -> p t i a", i=3), ACT.Copy
                                   ).then_inc(spread.sem, 1)
                    act.wait_ge(ea_in.of(at), ea_in.at(at))
                    act.activation(EH[at.b][0:64, :], EA[at.b][:, :], ACT.Copy).then_inc(ea_hi.sem, 1)
                    act.wait_ge(turned.sem, turned.at(at, 1))
                    act.activation(XS[at.b][:, :], front[0][:, :], ACT.Copy).then_inc(x_ready.sem, 1)
                    act.activation(XH[at.b][:, :], front[0][:, :], ACT.Copy).then_inc(x_ready.sem, 1)
                    act.wait_ge(turned.sem, turned.at(at, 2))
                    act.activation(XV[at.b][:, :], front[1][0:96, :], ACT.Copy).then_inc(x_ready.sem, 1)
                    for q in range(2):
                        act.wait_ge(t3_done.sem, t3_done.at(at, q + 1))
                        act.activation(T3[at.b][:, q, :], front[q][:, :], ACT.Copy).then_inc(t3_ready.sem, 1)

                def finish(at):
                    act.wait_ge(pr.contracted.sem, pr.contracted.at(at))
                    act.activation(US[at.b][:, :], AS[:, :], ACT.Copy).then_inc(sums.sem, 1)
                    act.activation(UV[at.b][0:96, :], AV[0:96, :], ACT.Copy).then_inc(sums.sem, 1)
                    for h in range(2):
                        act.wait_ge(mixed.sem, mixed.at(at, h + 1))
                        act.activation(sc.U[at.b][:, 2 * h:2 * h + 2, :].rearrange("p t c -> p (t c)"),
                                       front[h][:, 0:2 * D], ACT.Copy).then_inc(sc.u_ready.sem, 1)
                    sc.act(act, at)

                def body(at):
                    if at.first():
                        start(at)
                    else:
                        finish(at.back(1))
                    if not at.last(n):
                        start(at.next())
                    else:
                        finish(at)
                walk(act, n, body)

            @block.vector
            def _(dve):
                for b in range(2):
                    dve.memset(EH[b][64:128, :].bitcast(F32), 0.0).then_inc(const, 1)
                    dve.memset(UV[b][96:97, :], 1.0).then_inc(const, 1)

                def split(at):
                    dve.wait_ge(ea_hi.sem, ea_hi.at(at))
                    dve.tensor_tensor(EH[at.b][32:64, :], EA[at.b][32:64, :], EH[at.b][32:64, :].bitcast(F32),
                                      ALU.subtract).then_inc(rest.sem, 1)
                    dve.wait_ge(x_ready.sem, x_ready.at(at, 2))
                    dve.tensor_tensor(XH[at.b][64:128, :], XS[at.b][64:128, :], XH[at.b][64:128, :].bitcast(F32),
                                      ALU.subtract).then_inc(rest.sem, 1)

                def body(at):
                    if at.first():
                        split(at)
                        dve.wait_ge(x_ready.sem, x_ready.at(at, 3))
                    dve.wait_ge(x_ready.sem, x_ready.at(at))
                    dve.wait_ge(t3_ready.sem, t3_ready.at(at))
                    for s, (r, _, other, _, _, _, _) in enumerate(sources):
                        dve.wait_ge(pr.filled.sem, pr.filled.at(at, s + 1))
                        k = pr.tile_read(s)
                        if k > 0 or at.has(1):
                            dve.wait_ge(pr.contracted.sem, pr.contracted.at(at, k))
                        x = other[0][at.b][0:r, :] if len(other) == 1 else other[0][at.b][0:r, other[1], :]
                        dve.tensor_tensor(pr.tile(s)[0:r, :], pr.bank(s)[0:r, :], x, ALU.mult
                                          ).then_inc(pr.multiplied.sem, 1)
                        if s == 0:
                            sc.dve(dve, at)
                        if s == 8:
                            sc.place(dve, at)
                        if s == 17 and not at.last(n):
                            split(at.next())
                walk(dve, n, body)

            @block.tensor
            def _(pe):
                for k, (part, m) in enumerate((("wm_s", P), ("wm_v", 97))):
                    for h in range(2):
                        ins = pe.matmul(front[k][0:m, 0:D], w[part][:, h * m:(h + 1) * m],
                                        w["wu"][:, h * D:(h + 1) * D], start=h == 0, stop=h == 1)
                    ins.then_inc(folded, 1)
                pe.wait_ge(fold_ready, 2)
                pe.wait_ge(const, 4)

                def turn(at):
                    pe.wait_ge(spread.sem, spread.at(at))
                    for k, (lo_, hi_) in enumerate(((0, P), (P, 224))):
                        for t in range(T):
                            ins = pe.transpose(front[k][0:hi_ - lo_, t * P:(t + 1) * P],
                                               XX[at.b][:, t, lo_:hi_], core.eye)
                        ins.then_inc(turned.sem, 1)

                def t3(at):
                    pe.wait_ge(x_ready.sem, x_ready.at(at))
                    pe.wait_ge(rest.sem, rest.at(at))
                    for q in range(2):
                        pe.matmul(front[q][:, :], hi["w3"][:, q * P:(q + 1) * P], XH[at.b][:, :],
                                  start=True, stop=False)
                        pe.matmul(front[q][:, :], lo["w3"][:, q * P:(q + 1) * P], XH[at.b][:, :],
                                  start=False, stop=True).then_inc(t3_done.sem, 1)

                def mix(at, after):
                    pe.wait_ge(t3_ready.sem, t3_ready.at(after))
                    pe.wait_ge(sums.sem, sums.at(at))
                    for t in range(T):
                        o = front[t // 2][:, (t % 2) * D:(t % 2 + 1) * D]
                        pe.matmul(o, US[at.b][:, t * P:(t + 1) * P], fold_s[:, :], start=True, stop=False)
                        ins = pe.matmul(o, UV[at.b][:, t * P:(t + 1) * P], fold_v[:, :], start=False, stop=True)
                        if t % 2:
                            ins.then_inc(mixed.sem, 1)

                def body(at):
                    if at.first():
                        turn(at)
                        t3(at)
                    for s in range(pr.ns + pr.lag):
                        if s < pr.ns:
                            _, sel, _, lhs, _, _, _ = sources[s]
                            k = pr.bank_read(s)
                            if k > 0 or at.has(1):
                                pe.wait_ge(pr.multiplied.sem, pr.multiplied.at(at, k))
                            m = lhs.shape[0]
                            pe.matmul(pr.bank(s)[0:m, :], hi["gather"][:, sel * P:sel * P + m], EH[at.b][:, :],
                                      start=True, stop=True).then_inc(pr.filled.sem, 1)
                        m = s - pr.lag
                        if m == 0 and at.has(1):
                            pe.wait_ge(sums.sem, sums.at(at.back(1)))
                        if m >= 0:
                            r, _, _, lhs, acc, r0, start = sources[m]
                            pe.wait_ge(pr.multiplied.sem, pr.multiplied.at(at, m + 1))
                            pe.matmul(acc[r0:r0 + lhs.shape[1], :], lhs, pr.tile(m)[0:r, :], start=start,
                                      stop=True, skip_group_check=True).then_inc(pr.contracted.sem, 1)
                        if s == 3 and not at.first():
                            mix(at.back(1), at)
                        if s == 9 and not at.first():
                            sc.pe(pe, at.back(1))
                        if s == 14 and not at.last(n):
                            if at.first():
                                pe.wait_ge(t3_ready.sem, t3_ready.at(at))
                            else:
                                pe.wait_ge(sc.out_ready.sem, sc.out_ready.at(at.back(1)))
                            turn(at.next())
                        if s == 20 and not at.last(n):
                            t3(at.next())
                    if at.last(n):
                        if at.has(1):
                            pe.wait_ge(sc.out_ready.sem, sc.out_ready.at(at.back(1)))
                        mix(at, at)
                        sc.pe(pe, at)
                walk(pe, n, body)
def edges_conv(core, name, table, hidden_in, c1, out_table, norm):
    nc, d, n = core.nc, core.d, core.edge_groups
    width = AW if norm else D
    n_out = D + 1 if norm else D
    k96, l2 = 1 / np.sqrt(96), PACKS[name]["l2"][1]
    c_l2 = 1.0 if norm else float(np.cos(np.pi / 8) / (np.sqrt(8.0) * np.sqrt(96.0)))
    with ExitStack() as ctx:
        W, w, hi, _ = load_pack(core, ctx, name,
                                feature_scales("l1", 288) + [
                                    ("fc2", 0, P, 0, 192, 1 / 8 if norm else 1 / 10),
                                    ("l2", 0, 64, 0, AW, c_l2), ("l2", 64, 96, 0, AW, c_l2 / np.sqrt(3.0)),
                                    ("l2", 0, 96, AW, 4 * AW, c_l2)],
                                {"gather": False})
        AT = [sbuf(nc, ctx, f"{name}_at{b}", [P, GR]) for b in range(2)]
        AH = [sbuf(nc, ctx, f"{name}_ah{b}", [P, GR], F32R) for b in range(2)]
        XT = [sbuf(nc, ctx, f"{name}_xt{b}", [HALF, 2, GR]) for b in range(2)]
        HN = [sbuf(nc, ctx, f"{name}_hn{b}", [P, T, D]) for b in range(2)] if norm else None
        HS = [sbuf(nc, ctx, f"{name}_hs{b}", [P, GR]) for b in range(2)]
        WW = [sbuf(nc, ctx, f"{name}_ww{b}", [96, 2, GR]) for b in range(2)]
        PQ = [sbuf(nc, ctx, f"{name}_pq{i}", [96, 2, GR]) for i in range(2)]
        SV = [sbuf(nc, ctx, f"{name}_sv{b}", [96, 6, GR]) for b in range(2)]
        front = banks(nc, ctx, f"{name}_front", 2)
        mlp, = banks(nc, ctx, f"{name}_mlp", 1)
        EB = banks(nc, ctx, f"{name}_eb", 2)
        GB = banks(nc, ctx, f"{name}_gb", 2)

        ga = Gather(core, ctx, name, table, "src")
        gz = Gather(core, ctx, name + "z", "Z", "src" if norm else "dst", 1)
        sc = Scatter(core, ctx, name, out_table, "dst", width, front, placing=norm)
        at_in = core.moves(f"{name}_at_in", 3)
        at_hi = core.count(f"{name}_at_hi", 1)
        at_lo = core.count(f"{name}_at_lo", 1)
        turned = core.count(f"{name}_turned", 2)
        x_ready = core.count(f"{name}_x_ready", 2)
        gated = core.count(f"{name}_gated", 3)
        gate_out = core.count(f"{name}_gate_out", 3)
        filled = core.count(f"{name}_filled", 9)
        made = core.count(f"{name}_made", 14)
        mixed = core.count(f"{name}_mixed", 2)
        const = core.sem(f"{name}_const")
        if norm:
            st = [sbuf(nc, ctx, f"{name}_st{b}", [P, T, 6]) for b in range(2)]
            mv = [sbuf(nc, ctx, f"{name}_mv{b}", [P, T, 2]) for b in range(2)]
            sd = [sbuf(nc, ctx, f"{name}_sd{b}", [P, T]) for b in range(2)]
            rs = [sbuf(nc, ctx, f"{name}_rs{b}", [P, T]) for b in range(2)]
            eps = sbuf(nc, ctx, f"{name}_eps", [P, 1])
            stats = core.count(f"{name}_stats", T)
            means = core.count(f"{name}_means", T)
            std = core.count(f"{name}_std", 1)
            inv = core.count(f"{name}_inv", 1)
            centred = core.count(f"{name}_centred", T)
            h_ready = core.count(f"{name}_h_ready", T)

        with nc.Block() as block:
            @block.gpsimd
            def _(pool):
                z_ahead = 2 if norm else 1
                for g in (0, 1):
                    ga.index_of(pool, At.of(g))
                    if g < z_ahead:
                        gz.index_of(pool, At.of(g))
                    for t in range(T):
                        ga.fetch(pool, At.of(g), t)
                        if g < z_ahead:
                            gz.fetch(pool, At.of(g), t)

                def body(at):
                    rows_more, z_more = at.within(-2, n), at.within(-z_ahead, n)
                    if rows_more:
                        if norm:
                            pool.wait_ge(h_ready.sem, h_ready.at(at))
                        else:
                            pool.wait_ge(turned.sem, turned.at(at))
                        ga.index_of(pool, at.back(-2))
                    if z_more:
                        if not norm and at.has(1):
                            pool.wait_ge(sc.u_ready.sem, sc.u_ready.at(at.back(1)))
                        gz.index_of(pool, at.back(-z_ahead))
                    if at.within(1, n):
                        sc.index_of(pool, at.back(1))
                    for t in range(T):
                        if rows_more:
                            ga.fetch(pool, at.back(-2), t)
                        if z_more:
                            gz.fetch(pool, at.back(-z_ahead), t)
                        if at.within(1, n):
                            sc.add(pool, at.back(1), t)
                walk(pool, n, body, lag=1, ahead=2)
                for g in (n - 1, n - 2):
                    pool.wait_ge(sc.added.of(At.of(g)), sc.added.at(At.of(g)))

            @block.sync
            def _(sp):
                sp.wait_ge(const, 2)

                def body(at):
                    if at.has(2):
                        sp.wait_ge(at_lo.sem, at_lo.at(at.back(2)))
                    if at.has(2):
                        sp.wait_ge(gated.sem, gated.at(at.back(2), 1))
                    cols = bass.ds(at.g * GR, GR)
                    k = d[hidden_in].shape[0]
                    sp.dma_start(AT[at.b][0:k, :], d[hidden_in][:, cols]).then_inc(at_in.of(at), 16)
                    for r0 in (32, 64):
                        sp.dma_start(AT[at.b][r0:r0 + 4, :], d["ea4"][:, cols]).then_inc(at_in.of(at), 16)
                    sc.sp(sp, at)
                walk(sp, n, body)

            @block.scalar
            def _(act):
                act.wait_ge(const, 5 if norm else 2)

                def root(at):
                    if norm:
                        act.wait_ge(means.sem, means.at(at))
                        act.activation(sd[at.b][:, :], mv[at.b][:, :, 1], ACT.Sqrt, bias=eps[:, 0:1]
                                       ).then_inc(std.sem, 1)

                def start(at):
                    act.wait_ge(at_in.of(at), at_in.at(at))
                    act.activation(AH[at.b][:, :], AT[at.b][:, :], ACT.Copy).then_inc(at_hi.sem, 1)
                    act.wait_ge(gated.sem, gated.at(at, 1))
                    act.activation(HS[at.b][:, :], mlp[:, :], ACT.Silu, scale=float(c1)).then_inc(gate_out.sem, 1)
                    act.wait_ge(gated.sem, gated.at(at, 2))
                    act.activation(WW[at.b][:, 0, :], mlp[0:96, :], ACT.Copy).then_inc(gate_out.sem, 1)
                    for h in range(2):
                        act.wait_ge(turned.sem, turned.at(at, h + 1))
                        act.activation(XT[at.b][:, h, :], front[h][0:HALF, :], ACT.Copy).then_inc(x_ready.sem, 1)
                    act.wait_ge(gated.sem, gated.at(at, 3))
                    act.activation(WW[at.b][:, 1, :], mlp[0:96, :], ACT.Copy).then_inc(gate_out.sem, 1)

                def finish(at):
                    for h in range(2):
                        act.wait_ge(mixed.sem, mixed.at(at, h + 1))
                        if norm:
                            act.activation(sc.U[at.b][:, 2 * h:2 * h + 2, 0:n_out],
                                           front[h][:, 0:2 * n_out].rearrange("p (t c) -> p t c", t=2), ACT.Copy
                                           ).then_inc(sc.u_ready.sem, 1)
                        else:
                            for t in (2 * h, 2 * h + 1):
                                act.wait_ge(gz.here.of(at), gz.here.at(at))
                                ins = act.activation(sc.U[at.b][:, t, :], front[h][:, (t % 2) * D:(t % 2 + 1) * D],
                                                     ACT.Copy, scale=gz.rows[at.b][:, t, 0:1])
                            ins.then_inc(sc.u_ready.sem, 1)
                    sc.act(act, at)

                def body(at):
                    if at.first():
                        root(at)
                        start(at)
                    if not at.last(n):
                        root(at.next())
                    if not at.first():
                        finish(at.back(1))
                    if not at.last(n):
                        start(at.next())
                    else:
                        finish(at)
                walk(act, n, body)

            @block.vector
            def _(dve):
                for b in range(2):
                    dve.memset(AT[b][:, :], 0.0).then_inc(const, 1)
                if norm:
                    dve.memset(eps[:, :], EPS).then_inc(const, 1)
                    for b in range(2):
                        dve.memset(sc.U[b][:, :, D + 1:AW], 1.0).then_inc(const, 1)

                def statistics(at):
                    if norm:
                        dve.wait_ge(ga.here.of(at), ga.here.at(at))
                        if at.has(2):
                            dve.wait_ge(std.sem, std.at(at.back(2)))
                        for t in range(T):
                            dve.bn_stats(st[at.b][:, t, :], ga.rows[at.b][:, t, :]).then_inc(stats.sem, 1)
                        for t in range(T):
                            dve.wait_ge(stats.sem, stats.at(at, t + 1))
                            apart(core, dve, at)
                            dve.bn_aggr(mv[at.b][:, t, :], st[at.b][:, t, :]).then_inc(means.sem, 1)

                def prepare(at):
                    if norm:
                        dve.wait_ge(std.sem, std.at(at))
                        dve.reciprocal(rs[at.b][:, :], sd[at.b][:, :]).then_inc(inv.sem, 1)
                        dve.wait_ge(inv.sem, inv.at(at))
                        if at.has(2):
                            dve.wait_ge(turned.sem, turned.at(at.back(2)))
                        for t in range(T):
                            dve.tensor_scalar(HN[at.b][:, t, :], ga.rows[at.b][:, t, :], mv[at.b][:, t, 0:1],
                                              rs[at.b][:, t:t + 1], ALU.subtract, ALU.mult
                                              ).then_inc(centred.sem, 1)
                        dve.wait_ge(gz.here.of(at), gz.here.at(at))
                        for t in range(T):
                            dve.wait_ge(centred.sem, centred.at(at, t + 1))
                            dve.tensor_scalar(HN[at.b][:, t, :], HN[at.b][:, t, :], 0.0, gz.rows[at.b][:, t, :],
                                              ALU.max, ALU.mult).then_inc(h_ready.sem, 1)
                    dve.wait_ge(at_hi.sem, at_hi.at(at))
                    dve.tensor_tensor(AH[at.b][64:96, :], AT[at.b][64:96, :], AH[at.b][64:96, :].bitcast(F32),
                                      ALU.subtract).then_inc(at_lo.sem, 1)

                def products(at, m):
                    t = PQ[m % 2]
                    for q in range(2):
                        dve.wait_ge(filled.sem, filled.at(at, 3 * m + 2 + q))
                        if m < 2 and at.has(1):
                            dve.wait_ge(made.sem, made.at(at.back(1), 12 - 4 * m))
                        if m == 2:
                            dve.wait_ge(made.sem, made.at(at, 4))
                        dve.tensor_tensor(t[:, q, :], WW[at.b][:, q, :], GB[q][0:96, :], ALU.mult
                                          ).then_inc(made.sem, 1)
                    for q in range(2):
                        dve.wait_ge(made.sem, made.at(at, 4 * m + 1 + q))
                        dve.wait_ge(filled.sem, filled.at(at, 3 * m + 1))
                        dve.tensor_tensor(SV[at.b][:, 3 * q + m, :], t[:, q, :], EB[m % 2][0:96, :], ALU.mult
                                          ).then_inc(made.sem, 1)

                def total(at):
                    o = SV[at.b][:, 3, :]
                    for m in (1, 2):
                        dve.wait_ge(made.sem, made.at(at, 12 if m == 1 else 13))
                        dve.tensor_tensor(o, o, SV[at.b][:, 3 + m, :], ALU.add).then_inc(made.sem, 1)

                def body(at):
                    if at.first():
                        statistics(at)
                        prepare(at)
                    sc.dve(dve, at)
                    dve.wait_ge(gate_out.sem, gate_out.at(at))
                    if at.has(2):
                        dve.wait_ge(mixed.sem, mixed.at(at.back(2)))
                    products(at, 0)
                    if not at.last(n):
                        statistics(at.next())
                    products(at, 1)
                    if not at.last(n):
                        prepare(at.next())
                    products(at, 2)
                    total(at)
                    if norm:
                        sc.place(dve, at)
                walk(dve, n, body)

            @block.tensor
            def _(pe):
                pe.wait_ge(const, 2)

                def turn(at):
                    if norm:
                        pe.wait_ge(h_ready.sem, h_ready.at(at))
                    else:
                        pe.wait_ge(ga.here.of(at), ga.here.at(at))
                    src = HN[at.b] if norm else ga.rows[at.b]
                    for h in range(2):
                        for t in range(T):
                            ins = pe.transpose(front[h][0:HALF, t * P:(t + 1) * P],
                                               src[:, t, h * HALF:(h + 1) * HALF], core.eye)
                        ins.then_inc(turned.sem, 1)

                def gates(at, k):
                    if k == 0:
                        pe.wait_ge(at_in.of(at), at_in.at(at))
                        if at.has(1):
                            pe.wait_ge(gate_out.sem, gate_out.at(at.back(1)))
                        pe.matmul(mlp[:, :], w["fc1"], AT[at.b][:, :], start=True, stop=True
                                  ).then_inc(gated.sem, 1)
                    else:
                        pe.wait_ge(gate_out.sem, gate_out.at(at, k))
                        pe.matmul(mlp[0:96, :], w["fc2"][:, (k - 1) * 96:k * 96], HS[at.b][:, :],
                                  start=True, stop=True).then_inc(gated.sem, 1)

                def fill(at, m):
                    if m == 2:
                        pe.wait_ge(made.sem, made.at(at, 4))
                    elif at.has(1):
                        pe.wait_ge(made.sem, made.at(at.back(1), 12 - 4 * m))
                    r0 = 64 if m == 2 else 0
                    for h in range(2):
                        ins = pe.matmul(EB[m % 2][r0:96, :], w["l1"][:, h * 288 + m * 96 + r0:h * 288 + (m + 1) * 96],
                                        XT[at.b][:, h, :], start=h == 0, stop=h == 1)
                    ins.then_inc(filled.sem, 1)
                    for q in range(2):
                        k = 4 * (m - 1) + 1 + q if m else 8 + 1 + q - made.per
                        if k > 0 or at.has(1):
                            pe.wait_ge(made.sem, made.at(at, k))
                        k = 3 * q + m
                        pe.matmul(GB[q][0:96, :], hi["gather"][:, k * 96:(k + 1) * 96], AH[at.b][:, :],
                                  start=True, stop=True).then_inc(filled.sem, 1)

                def mix(at):
                    pe.wait_ge(made.sem, made.at(at))
                    for t in range(T):
                        for k in range(4):
                            part = 1 + k if k < 3 else 0
                            ins = pe.matmul(front[t // 2][:, (t % 2) * n_out:(t % 2 + 1) * n_out],
                                            SV[at.b][:, k, t * P:(t + 1) * P],
                                            w["l2"][:, part * AW:part * AW + n_out], start=k == 0, stop=k == 3)
                        if t % 2:
                            ins.then_inc(mixed.sem, 1)

                def body(at):
                    if at.first():
                        turn(at)
                        for k in range(3):
                            gates(at, k)
                    pe.wait_ge(at_lo.sem, at_lo.at(at))
                    pe.wait_ge(x_ready.sem, x_ready.at(at))
                    fill(at, 0)
                    if not at.last(n):
                        gates(at.next(), 0)
                    if not at.first():
                        mix(at.back(1))
                    fill(at, 1)
                    if not at.first():
                        sc.pe(pe, at.back(1))
                    fill(at, 2)
                    if not at.last(n):
                        gates(at.next(), 1)
                        if not at.first():
                            if at.has(1):
                                pe.wait_ge(sc.out_ready.sem, sc.out_ready.at(at.back(1)))
                        else:
                            pe.wait_ge(x_ready.sem, x_ready.at(at))
                        turn(at.next())
                        gates(at.next(), 2)
                    else:
                        if at.has(1):
                            pe.wait_ge(sc.out_ready.sem, sc.out_ready.at(at.back(1)))
                        mix(at)
                        sc.pe(pe, at)
                walk(pe, n, body)


def edges1(core):
    edges_conv(core, "e1", "X1", "ea16", 1 / 4, "AGG", True)


def edges2(core):
    edges_conv(core, "e2", "H", "ea12", 1 / np.sqrt(12.0), "X3", False)


def nodes1(core):
    nc, d, n = core.nc, core.d, core.node_groups
    with ExitStack() as ctx:
        sin8 = float(np.sin(np.pi / 8))
        W, w, _, _ = load_pack(core, ctx, "n1", feature_scales("sc", D) +
                               [(p, a, b, c, e, v * sin8) for p, a, b, c, e, v in feature_scales("sc2", D)], {})
        some = lambda count, tag, shape: [sbuf(nc, ctx, f"n1_{tag}{b}", shape) for b in range(count)]
        X, A, Z = some(4, "x", [P, T * D]), some(4, "a", [P, T * AW]), some(4, "z", [P, T])
        X2, ZB = some(4, "x2", [P, T * D]), some(4, "zb", [P, T])
        Y, ZH = some(2, "y", [P, T * D]), some(2, "zh", [P, T * D])
        cf, tmp = some(2, "cf", [P, 5, T]), some(2, "tmp", [P, T * D])
        eps = sbuf(nc, ctx, "n1_eps", [P, 1])
        a, b = Norm(core, ctx, "n1a", T, eps), Norm(core, ctx, "n1b", T, eps)
        x_in = core.moves("n1_x_in", 3, buffers=4)
        y_out, h_out = core.moves("n1_y_out"), core.moves("n1_h_out")
        const = core.sem("n1_const")
        coef = core.count("n1_coef", 5)
        scaled = core.count("n1_scaled", T)
        summed = core.count("n1_summed", T)
        zb_ready = core.count("n1_zb_ready", 1)
        y_ready = core.count("n1_y_ready", T)
        zh_ready = core.count("n1_zh_ready", T)
        rows = lambda x, at: x[bass.ds(at.g * GR, GR), :].rearrange("(p t) c -> p (t c)", t=T)

        with nc.Block() as block:
            @block.sync
            def _(sp):
                def body(at):
                    if at.within(0, n):
                        if at.has(4):
                            sp.wait_ge(zb_ready.sem, zb_ready.at(at.back(4)))
                        sp.dma_start(X[at.rest][:, :], rows(d["X1"], at)).then_inc(x_in.of(at), 16)
                        sp.dma_start(A[at.rest][:, :], rows(d["AGG"], at)).then_inc(x_in.of(at), 16)
                        sp.dma_start(Z[at.rest][:, :], rows(d["Z"], at)).then_inc(x_in.of(at), 16)
                    if at.within(5, n):
                        p = at.back(5)
                        sp.wait_ge(y_ready.sem, y_ready.at(p))
                        sp.dma_start(rows(d["X3"], p), Y[p.b][:, :]).then_inc(y_out.of(p), 16)
                walk(sp, n, body, unroll=4, lag=5)
                for q in (n - 1, n - 2):
                    sp.wait_ge(y_out.of(At.of(q)), y_out.at(At.of(q)))

            @block.gpsimd
            def _(pool):
                def body(at):
                    if at.within(3, n):
                        p = at.back(3)
                        pool.wait_ge(b.h_ready.sem, b.h_ready.at(p))
                        pool.wait_ge(zb_ready.sem, zb_ready.at(p))
                        if p.has(2):
                            pool.wait_ge(h_out.of(p.back(2)), h_out.at(p.back(2)))
                        apart(core, pool, p)
                        for t in range(T):
                            pool.tensor_scalar(ZH[p.b][:, t * D:(t + 1) * D], b.H[p.b][:, t * D:(t + 1) * D],
                                               ZB[p.rest][:, t:t + 1], None, ALU.mult).then_inc(zh_ready.sem, 1)
                        pool.wait_ge(zh_ready.sem, zh_ready.at(p))
                        apart(core, pool, p)
                        pool.dma_start(rows(d["H"], p), ZH[p.b][:, :]).then_inc(h_out.of(p), 16)
                walk(pool, n, body, unroll=4, lag=3)
                for q in (n - 1, n - 2):
                    pool.wait_ge(h_out.of(At.of(q)), h_out.at(At.of(q)))

            @block.scalar
            def _(act):
                act.wait_ge(const, 1)

                def body(at):
                    if at.within(2, n):
                        a.copies(act, at.back(2))
                    if at.within(4, n):
                        b.copies(act, at.back(4))
                    if at.within(1, n):
                        a.relu(act, at.back(1), X[at.back(1).rest])
                    if at.within(3, n):
                        p = at.back(3)
                        if p.has(2):
                            act.wait_ge(zh_ready.sem, zh_ready.at(p.back(2)))
                        b.relu(act, p, X2[p.rest])
                    if at.within(0, n):
                        a.root(act, at)
                    if at.within(2, n):
                        b.root(act, at.back(2))
                walk(act, n, body, unroll=4, lag=4)

            @block.vector
            def _(dve):
                dve.memset(eps[:, :], EPS).then_inc(const, 1)
                col = lambda x, c: x[:, :].rearrange("p (t c) -> p t c", t=T)[:, :, c]

                def coefficient(at, step):
                    f = cf[at.b]
                    if step:
                        dve.wait_ge(coef.sem, coef.at(at, step))
                    elif at.has(2):
                        dve.wait_ge(scaled.sem, scaled.at(at.back(2)))
                    if step == 0:
                        dve.tensor_scalar(f[:, 0, :], col(A[at.rest], D + 1), 1.0, None, ALU.max
                                          ).then_inc(coef.sem, 1)
                    if step == 1:
                        dve.reciprocal(f[:, 1, :], f[:, 0, :]).then_inc(coef.sem, 1)
                    if step == 2:
                        dve.tensor_tensor(f[:, 2, :], f[:, 1, :], Z[at.rest][:, :], ALU.mult).then_inc(coef.sem, 1)
                    if step == 3:
                        dve.scalar_tensor_tensor(f[:, 3, :], f[:, 2, :], 1 / 96, f[:, 2, :], ALU.mult, ALU.mult
                                                 ).then_inc(coef.sem, 1)
                    if step == 4:
                        dve.tensor_tensor(f[:, 4, :], f[:, 3, :], col(A[at.rest], D), ALU.mult
                                          ).then_inc(coef.sem, 1)

                def body(at):
                    if at.within(1, n):
                        a.factors(dve, at.back(1))
                    if at.within(3, n):
                        b.factors(dve, at.back(3))
                    if at.within(0, n):
                        dve.wait_ge(x_in.of(at), x_in.at(at))
                        a.statistics(dve, at, X[at.rest])
                        a.means_of(dve, at)
                    if at.within(2, n):
                        p = at.back(2)
                        coefficient(p, 0)
                        coefficient(p, 1)
                        coefficient(p, 2)
                        coefficient(p, 3)
                        coefficient(p, 4)
                        dve.wait_ge(coef.sem, coef.at(p))
                        for t in range(T):
                            c = slice(t * D, (t + 1) * D)
                            dve.scalar_tensor_tensor(tmp[p.b][:, c], A[p.rest][:, t * AW:t * AW + D],
                                                     cf[p.b][:, 4, t:t + 1], X[p.rest][:, c], ALU.mult, ALU.add
                                                     ).then_inc(scaled.sem, 1)
                        for t in range(T):
                            c = slice(t * D, (t + 1) * D)
                            dve.wait_ge(a.mixed.sem, a.mixed.at(p, t // 2 + 1))
                            dve.wait_ge(scaled.sem, scaled.at(p, t + 1))
                            dve.scalar_tensor_tensor(X2[p.rest][:, c], a.LP[t // 2][:, (t % 2) * D:(t % 2 + 1) * D],
                                                     Z[p.rest][:, t:t + 1], tmp[p.b][:, c], ALU.mult, ALU.add
                                                     ).then_inc(summed.sem, 1)
                        if p.has(4):
                            dve.wait_ge(zh_ready.sem, zh_ready.at(p.back(4)))
                        dve.tensor_copy(ZB[p.rest][:, :], Z[p.rest][:, :]).then_inc(zb_ready.sem, 1)
                        dve.wait_ge(summed.sem, summed.at(p))
                        b.statistics(dve, p, X2[p.rest])
                        b.means_of(dve, p)
                    if at.within(4, n):
                        p = at.back(4)
                        if p.has(2):
                            dve.wait_ge(y_out.of(p.back(2)), y_out.at(p.back(2)))
                        for t in range(T):
                            c = slice(t * D, (t + 1) * D)
                            dve.wait_ge(b.mixed.sem, b.mixed.at(p, t // 2 + 1))
                            dve.scalar_tensor_tensor(Y[p.b][:, c], b.LP[t // 2][:, (t % 2) * D:(t % 2 + 1) * D],
                                                     ZB[p.rest][:, t:t + 1], X2[p.rest][:, c], ALU.mult, ALU.add
                                                     ).then_inc(y_ready.sem, 1)
                walk(dve, n, body, unroll=4, lag=4)

            @block.tensor
            def _(pe):
                def body(at):
                    if at.within(2, n):
                        a.mix(pe, at.back(2), w["sc"], summed, 2)
                    if at.within(4, n):
                        b.mix(pe, at.back(4), w["sc2"], y_ready, 2)
                    if at.within(1, n):
                        a.turn(pe, at.back(1))
                    if at.within(3, n):
                        b.turn(pe, at.back(3))
                walk(pe, n, body, unroll=4, lag=4)


def edges3(core):
    nc, d, n, name = core.nc, core.d, core.edge_groups, "e3"
    YW = 2 * D + V
    CH = 8
    with ExitStack() as ctx:
        yc = [("y", 0, 64, 0, YW, 1 / 8), ("y", 64, 96, 0, YW, 1 / np.sqrt(32.0)),
              ("y", 0, 64, YW, 2 * YW, 1 / np.sqrt(32.0)), ("y", 64, 96, YW, 2 * YW, 1 / np.sqrt(96.0))]
        W, w, hi, lo = load_pack(core, ctx, name, yc + [
            ("ss", 0, P, 0, 32 * S, 1 / 64), ("vv", 0, P, 0, 8 * S, 1 / (np.sqrt(3.0) * 32)),
            ("sv", 0, P, 0, 8 * P, 1 / np.sqrt(2048.0)), ("vs", 0, P, 0, 8 * P, 1 / np.sqrt(2048.0))],
            {"sv": True, "vs": True, "pick_s": False, "pick_v": False})
        two = lambda tag, shape, dt=F32: [sbuf(nc, ctx, f"e3_{tag}{b}", shape, dt) for b in range(2)]
        one = lambda tag, shape, dt=F32: sbuf(nc, ctx, f"e3_{tag}", shape, dt)
        ED = two("ed", [P, T * 4])
        RV = one("rv", [P, T, 96])
        GD = one("gd", [P, T, 96])
        XD = one("xd", [96, 2, GR])
        A = one("a", [P, T, D])
        AR = one("ar", [P, T, 96])
        XA = one("xa", [P, T, 4 * P])
        XX = one("xx", [P, T, 4 * P])
        A0, XS = two("a0", [P, GR]), one("xs", [P, GR])
        A1, XV = two("a1", [P, 3, GR]), two("xv", [P, 3, GR])
        A0H, XSH = two("a0h", [P, GR], F32R), two("xsh", [P, GR], F32R)
        XVH = two("xvh", [P, 3, GR], F32R)
        US, UV = one("us", [P, GR]), one("uv", [96, GR])
        front = banks(nc, ctx, "e3_front", 3)
        ring = banks(nc, ctx, "e3_ring", 3)
        AS, AV = banks(nc, ctx, "e3_acc", 2)

        gs, gd = Gather(core, ctx, "e3s", "H", "src"), Gather(core, ctx, "e3d", "H", "dst")
        sc = Scatter(core, ctx, name, "OUT", "src", D, [front[2], front[0]])
        ed_in = core.moves("e3_ed_in")
        vr = core.count("e3_vr", T)
        gd_ready = core.count("e3_gd_ready", 2)
        turned_d = core.count("e3_turned_d", 2)
        xd_ready = core.count("e3_xd_ready", 2)
        y_done = core.count("e3_y_done", T)
        a_scaled = core.count("e3_a_scaled", T)
        a_added = core.count("e3_a_added", 2 * T)
        a_ready = core.count("e3_a_ready", 1)
        spread = core.count("e3_spread", 8)
        turned = core.count("e3_turned", 8)
        out = core.count("e3_turned_out", 8)
        high = core.count("e3_high", 5)
        rest = core.count("e3_rest", 5)
        sums = core.count("e3_sums", 2)
        mixed = core.count("e3_mixed", 2)
        const = core.sem("e3_const")

        picked, through_sv, through_vs = [], [], []
        for c in range(32):
            picked.append((("pick_s", c, XSH, None),
                           [(A0, None, w["ss"][:, c * S:(c + 1) * S], AS, 64 * (c % 2), c < 2)]))
        for c in range(CH):
            for i in range(3):
                picked.append((("pick_v", c, XVH, i),
                               [(A1, i, w["vv"][:, c * S:(c + 1) * S], AS, 64 * ((c + i) % 2), False)]))
        for c in range(CH):
            for part, rhs, other, to in (("sv", XSH, A1, through_sv), ("vs", A0H, XV, through_vs)):
                to.append(((part, c, rhs, None),
                           [(other, i, w["sum"][:, c * V:(c + 1) * V], AV, 32 * i, c == 0)
                             for i in range(3)]))
        sources = []
        for c in range(CH):
            sources += [through_vs[c], through_sv[c]] + picked[6 * c:6 * c + 6]
        BLOCK = len(sources) // CH
        sources += picked[6 * CH:]
        part_of = lambda x, at, i: x[at.b][:, :] if i is None else x[at.b][:, i, :]
        through_v = lambda s: s < BLOCK * CH and s % BLOCK == 0
        through_s = lambda s: s < BLOCK * CH and s % BLOCK == 1
        pr = Plan(core, ctx, name, [0 if through_v(s) or through_s(s) else 1 for s in range(len(sources))],
                  ring, 6, 3)
        FS = [one(f"fs{k}", [P, GR]) for k in range(6)]
        sv_made = core.count("e3_sv_made", 3 * CH)
        third_added = core.count("e3_third_added", CH)
        E = two("e", [P, GR])
        FP = [one(f"fp{k}", [P, GR]) for k in range(6)]
        moved = core.count("e3_moved", CH)
        pool_made = core.count("e3_pool_made", 5 * CH)
        pool_contracted = core.count("e3_pool_contracted", 3 * CH)

        with nc.Block() as block:
            @block.gpsimd
            def _(pool):
                def v_r(at):
                    pool.wait_ge(gd.here.of(at), gd.here.at(at))
                    pool.wait_ge(ed_in.of(at), ed_in.at(at))
                    if at.has(1):
                        pool.wait_ge(gd_ready.sem, gd_ready.at(at.back(1)))
                    apart(core, pool, at)
                    for t in range(T):
                        pool.tensor_tensor(RV[:, t, :].rearrange("p (u i) -> p u i", i=3),
                                           gd.rows[at.b][:, t, S:D].rearrange("p (u i) -> p u i", i=3),
                                           ED[at.b][:, 4 * t:4 * t + 3].unsqueeze(1).broadcast_to([P, V, 3]),
                                           ALU.mult).then_inc(vr.sem, 1)

                for g in (0, 1):
                    gd.index_of(pool, At.of(g))
                    gs.index_of(pool, At.of(g))
                    for t in range(T):
                        gd.fetch(pool, At.of(g), t)
                        gs.fetch(pool, At.of(g), t)
                v_r(At.of(0))

                def products(at, c):
                    pool.wait_ge(moved.sem, moved.at(at, c + 1))
                    if c >= 2:
                        pool.wait_ge(pool_contracted.sem, pool_contracted.at(at, 3 * (c - 1)))
                    elif at.has(1):
                        pool.wait_ge(pool_contracted.sem, pool_contracted.at(at.back(1), 3 * (CH + c - 1)))
                    for i in (2, 0, 1):
                        pool.tensor_tensor(FP[3 * (c % 2) + i][:, :], E[c % 2][:, :], XV[at.b][:, i, :], ALU.mult
                                           ).then_inc(pool_made.sem, 1)

                def total(at, c):
                    pool.wait_ge(sv_made.sem, sv_made.at(at, 3 * c + 2))
                    for i in range(2):
                        o = FP[3 * (c % 2) + i][:, :]
                        pool.wait_ge(pool_made.sem, pool_made.at(at, 5 * c + 2 + i))
                        pool.tensor_tensor(o, o, FS[3 * (c % 2) + i][:, :], ALU.add).then_inc(pool_made.sem, 1)

                def body(at):
                    more = at.within(-2, n)
                    if more:
                        pool.wait_ge(turned_d.sem, turned_d.at(at))
                        gd.index_of(pool, at.back(-2))
                        pool.wait_ge(spread.sem, spread.at(at))
                        gs.index_of(pool, at.back(-2))
                    if at.within(1, n):
                        sc.index_of(pool, at.back(1))
                    if at.within(0, n):
                        pool.wait_ge(out.sem, out.at(at))
                    for c in range(CH):
                        if at.within(0, n):
                            products(at, c)
                            total(at, c)
                        if c == 1 and at.within(-1, n):
                            v_r(at.next())
                        if c < T and more:
                            gd.fetch(pool, at.back(-2), c)
                            gs.fetch(pool, at.back(-2), c)
                        if c >= T and at.within(1, n):
                            sc.add(pool, at.back(1), c - T)
                walk(pool, n, body, lag=1, ahead=2)
                for g in (n - 1, n - 2):
                    pool.wait_ge(sc.added.of(At.of(g)), sc.added.at(At.of(g)))

            @block.sync
            def _(sp):
                def body(at):
                    if at.has(2):
                        sp.wait_ge(a_ready.sem, a_ready.at(at.back(2)))
                    sp.dma_start(ED[at.b][:, :], d["ea4_cols"][:, bass.ds(at.g * (4 * T), 4 * T)]
                                 ).then_inc(ed_in.of(at), 16)
                    sc.sp(sp, at)
                walk(sp, n, body)

            @block.scalar
            def _(act):
                act.wait_ge(const, 2)

                def spread_out(at, src, x):
                    act.activation(x[:, :, 0:P].rearrange("p t (r a) -> p t r a", r=2),
                                   src[:, :, 0:S].unsqueeze(2).broadcast_to([P, T, 2, S]), ACT.Copy
                                   ).then_inc(spread.sem, 1)
                    for i in range(3):
                        v = src[:, :, S:D].rearrange("p t (u i) -> p t u i", i=3)[:, :, :, i]
                        act.activation(x[:, :, (1 + i) * P:(2 + i) * P].rearrange("p t (r u) -> p t r u", r=4),
                                       v.unsqueeze(2).broadcast_to([P, T, 4, V]), ACT.Copy
                                       ).then_inc(spread.sem, 1)

                def centre(at):
                    act.wait_ge(gd.here.of(at), gd.here.at(at))
                    if at.has(1):
                        act.wait_ge(turned_d.sem, turned_d.at(at.back(1)))
                    act.activation(GD[:, :, 0:S], gd.rows[at.b][:, :, 96:D], ACT.Copy).then_inc(gd_ready.sem, 1)

                def source_rows(at):
                    act.wait_ge(gs.here.of(at), gs.here.at(at))
                    spread_out(at, gs.rows[at.b], XX)

                def target_rows(at):
                    for h in range(2):
                        act.wait_ge(turned_d.sem, turned_d.at(at, h + 1))
                        act.activation(XD[:, h, :], front[(4 + h) % 3][0:96, :], ACT.Copy).then_inc(xd_ready.sem, 1)

                def scale(at):
                    for t in range(T):
                        act.wait_ge(y_done.sem, y_done.at(at, t + 1))
                        act.activation(A[:, t, :], front[t % 3][:, D:2 * D], ACT.Copy,
                                       scale=ED[at.b][:, 4 * t + 3:4 * t + 4]).then_inc(a_scaled.sem, 1)

                def message_rows(at):
                    act.wait_ge(a_ready.sem, a_ready.at(at))
                    spread_out(at, A, XA)

                def transposes(at, ks):
                    targets = [XS[:, :]] + [XV[at.b][:, i, :] for i in range(3)] + \
                              [A0[at.b][:, :]] + [A1[at.b][:, i, :] for i in range(3)]
                    for k in ks:
                        act.wait_ge(turned.sem, turned.at(at, k + 1))
                        act.activation(targets[k], front[(10 + k) % 3][:, :], ACT.Copy).then_inc(out.sem, 1)
                        if k < 5:
                            h = (XSH[at.b][:, :], XVH[at.b][0:64, 0, :], XVH[at.b][0:64, 1, :],
                                 XVH[at.b][0:64, 2, :], A0H[at.b][:, :])[k]
                            act.wait_ge(out.sem, out.at(at, k + 1))
                            act.activation(h, targets[k][0:h.shape[0], :], ACT.Copy).then_inc(high.sem, 1)

                def results(at):
                    act.wait_ge(pr.contracted.sem, pr.contracted.at(at))
                    act.wait_ge(pool_contracted.sem, pool_contracted.at(at))
                    act.activation(US[:, :], AS[:, :], ACT.Copy).then_inc(sums.sem, 1)
                    act.activation(UV[:, :], AV[0:96, :], ACT.Copy).then_inc(sums.sem, 1)

                def rows_out(at):
                    for h in range(2):
                        act.wait_ge(mixed.sem, mixed.at(at, h + 1))
                        act.activation(sc.U[at.b][:, 2 * h:2 * h + 2, :].rearrange("p t c -> p (t c)"),
                                       front[h][:, 0:2 * D], ACT.Copy).then_inc(sc.u_ready.sem, 1)

                def move(at, c):
                    s = c * BLOCK
                    act.wait_ge(pr.filled.sem, pr.filled.at(at, s + 1))
                    if c >= 2:
                        act.wait_ge(pool_made.sem, pool_made.at(at, 5 * (c - 2) + 3))
                    elif at.has(1):
                        act.wait_ge(pool_made.sem, pool_made.at(at.back(1), 5 * (CH + c - 2) + 3))
                    act.activation(E[c % 2][:, :], pr.bank(s)[:, :], ACT.Copy).then_inc(moved.sem, 1)

                def body(at):
                    if at.first():
                        centre(at)
                        source_rows(at)
                        target_rows(at)
                        scale(at)
                        transposes(at, range(4))
                        message_rows(at)
                        transposes(at, range(4, 8))
                    else:
                        results(at.back(1))
                    move(at, 0)
                    if at.has(1):
                        rows_out(at.back(1))
                    move(at, 1)
                    if at.has(1):
                        sc.act(act, at.back(1))
                    if not at.last(n):
                        centre(at.next())
                    move(at, 2)
                    if not at.last(n):
                        source_rows(at.next())
                        target_rows(at.next())
                    move(at, 3)
                    if not at.last(n):
                        scale(at.next())
                    move(at, 4)
                    if not at.last(n):
                        transposes(at.next(), range(4))
                    move(at, 5)
                    if not at.last(n):
                        message_rows(at.next())
                        transposes(at.next(), (4, 5))
                    move(at, 6)
                    if not at.last(n):
                        transposes(at.next(), (6, 7))
                    move(at, 7)
                    if at.last(n):
                        results(at)
                        rows_out(at)
                        sc.act(act, at)
                walk(act, n, body)

            @block.vector
            def _(dve):
                for b in range(2):
                    dve.memset(XVH[b][64:128, :, :].bitcast(F32), 0.0).then_inc(const, 1)

                def dot(at):
                    dve.wait_ge(vr.sem, vr.at(at))
                    if at.has(1):
                        dve.wait_ge(turned_d.sem, turned_d.at(at.back(1)))
                    dve.tensor_reduce(GD[:, :, S:96], RV[:, :, :].rearrange("p t (u i) -> p t u i", i=3),
                                      AX.X, ALU.add).then_inc(gd_ready.sem, 1)

                def message(at, tiles):
                    for t in tiles:
                        dve.wait_ge(a_scaled.sem, a_scaled.at(at, t + 1))
                        dve.tensor_tensor(A[:, t, :], front[t % 3][:, 0:D], A[:, t, :], ALU.add
                                          ).then_inc(a_added.sem, 1)
                        dve.tensor_tensor(AR[:, t, :].rearrange("p (w i) -> p w i", i=3),
                                          over(front[t % 3][:, 2 * D:YW], 3),
                                          ED[at.b][:, 4 * t:4 * t + 3].unsqueeze(1).broadcast_to([P, V, 3]),
                                          ALU.mult).then_inc(a_added.sem, 1)
                    if T - 1 not in tiles:
                        return
                    dve.wait_ge(a_added.sem, a_added.at(at))
                    dve.tensor_tensor(A[:, :, S:D], A[:, :, S:D], AR[:, :, :], ALU.add).then_inc(a_ready.sem, 1)

                def remainders(at, ks):
                    pairs = [(XSH[at.b][64:128, :], XS[64:128, :])] + \
                            [(XVH[at.b][32:64, i, :], XV[at.b][32:64, i, :]) for i in range(3)] + \
                            [(A0H[at.b][64:128, :], A0[at.b][64:128, :])]
                    for k in ks:
                        dve.wait_ge(high.sem, high.at(at, k + 1))
                        dve.tensor_tensor(pairs[k][0], pairs[k][1], pairs[k][0].bitcast(F32), ALU.subtract
                                          ).then_inc(rest.sem, 1)

                def body(at):
                    if at.first():
                        dot(at)
                        message(at, range(T))
                        remainders(at, range(5))
                    dve.wait_ge(out.sem, out.at(at))
                    for s, (_, products) in enumerate(sources):
                        if s >= BLOCK and s % BLOCK == 0:
                            c = s // BLOCK - 1
                            o = FP[3 * (c % 2) + 2][:, :]
                            dve.wait_ge(pool_made.sem, pool_made.at(at, 5 * c + 1))
                            dve.wait_ge(sv_made.sem, sv_made.at(at, 3 * c + 3))
                            dve.tensor_tensor(o, o, FS[3 * (c % 2) + 2][:, :], ALU.add).then_inc(third_added.sem, 1)
                        if through_v(s):
                            continue
                        dve.wait_ge(pr.filled.sem, pr.filled.at(at, s + 1))
                        c = s // BLOCK
                        if through_s(s):
                            if c >= 2:
                                dve.wait_ge(pool_made.sem, pool_made.at(at, 5 * (c - 1)))
                                dve.wait_ge(third_added.sem, third_added.at(at, c - 1))
                            elif at.has(1):
                                dve.wait_ge(pool_made.sem, pool_made.at(at.back(1), 5 * (CH + c - 1)))
                                dve.wait_ge(third_added.sem, third_added.at(at.back(1), CH + c - 1))
                            for other, i, _, _, _, _ in products:
                                dve.tensor_tensor(FS[3 * (c % 2) + i][:, :], pr.bank(s)[:, :],
                                                  part_of(other, at, i), ALU.mult).then_inc(sv_made.sem, 1)
                        else:
                            other, i, _, _, _, _ = products[0]
                            m = pr.first[s]
                            k = pr.tile_read(m)
                            if k > 0 or at.has(1):
                                dve.wait_ge(pr.contracted.sem, pr.contracted.at(at, k))
                            dve.tensor_tensor(pr.tile(m)[:, :], pr.bank(s)[:, :], part_of(other, at, i), ALU.mult
                                              ).then_inc(pr.multiplied.sem, 1)
                        if s == 1:
                            sc.dve(dve, at)
                        if not at.last(n):
                            if s == 17:
                                dot(at.next())
                            if s == 28:
                                message(at.next(), (0, 1, 2))
                            if s == 31:
                                message(at.next(), (3,))
                            if s == 44:
                                remainders(at.next(), range(4))
                            if s == 57:
                                remainders(at.next(), range(4, 5))
                walk(dve, n, body)

            @block.tensor
            def _(pe):
                pe.wait_ge(const, 2)

                def turn_d(at):
                    if at.has(2):
                        pe.wait_ge(sc.out_ready.sem, sc.out_ready.at(at.back(2)))
                    if at.has(1):
                        pe.wait_ge(out.sem, out.at(at.back(1)))
                    pe.wait_ge(gd_ready.sem, gd_ready.at(at))
                    pe.wait_ge(gd.here.of(at), gd.here.at(at))
                    for h in range(2):
                        for t in range(T):
                            src = gd.rows[at.b][:, t, 0:96] if h == 0 else GD[:, t, :]
                            ins = pe.transpose(front[(4 + h) % 3][0:96, t * P:(t + 1) * P], src, core.eye)
                        ins.then_inc(turned_d.sem, 1)

                def message(at, tiles):
                    pe.wait_ge(xd_ready.sem, xd_ready.at(at))
                    for t in tiles:
                        if t == 3:
                            pe.wait_ge(a_added.sem, a_added.at(at, 2))
                        for h in range(2):
                            ins = pe.matmul(front[t % 3][:, 0:YW], XD[:, h, t * P:(t + 1) * P],
                                            w["y"][:, h * YW:(h + 1) * YW], start=h == 0, stop=h == 1)
                        ins.then_inc(y_done.sem, 1)

                def turn(at, ks):
                    for k in ks:
                        if k < 3:
                            pe.wait_ge(a_added.sem, a_added.at(at, 2 * (k + 2)))
                        else:
                            pe.wait_ge(out.sem, out.at(at, k - 2))
                        pe.wait_ge(spread.sem, spread.at(at, k + 1))
                        x = XX if k < 4 else XA
                        for t in range(T):
                            ins = pe.transpose(front[(10 + k) % 3][:, t * P:(t + 1) * P],
                                               x[:, t, (k % 4) * P:(k % 4 + 1) * P], core.eye)
                        ins.then_inc(turned.sem, 1)

                def mix(at, after):
                    pe.wait_ge(out.sem, out.at(after))
                    pe.wait_ge(sums.sem, sums.at(at))
                    for t in range(T):
                        o = front[t // 2][:, (t % 2) * D:(t % 2 + 1) * D]
                        pe.matmul(o, US[:, t * P:(t + 1) * P], w["out_s"], start=True, stop=False)
                        ins = pe.matmul(o, UV[:, t * P:(t + 1) * P], w["out_v"], start=False, stop=True)
                        if t % 2:
                            ins.then_inc(mixed.sem, 1)

                def body(at):
                    if at.first():
                        turn_d(at)
                        message(at, range(T))
                        turn(at, range(8))
                    pe.wait_ge(out.sem, out.at(at))
                    pe.wait_ge(rest.sem, rest.at(at))
                    for s in range(pr.ns + pr.lag):
                        if s < pr.ns:
                            part, c, rhs, i = sources[s][0]
                            last = s - len(ring)
                            if last >= 0 and through_v(last):
                                pe.wait_ge(moved.sem, moved.at(at, last // BLOCK + 1))
                            elif last >= 0 and through_s(last):
                                pe.wait_ge(sv_made.sem, sv_made.at(at, 3 * (last // BLOCK + 1)))
                            else:
                                k = pr.bank_read(s)
                                if k > 0 or at.has(1):
                                    pe.wait_ge(pr.multiplied.sem, pr.multiplied.at(at, k))
                            x = part_of(rhs, at, i)
                            ins = pe.matmul(pr.bank(s)[:, :], hi[part][:, c * P:(c + 1) * P], x,
                                            start=True, stop=part not in lo)
                            if part in lo:
                                ins = pe.matmul(pr.bank(s)[:, :], lo[part][:, c * P:(c + 1) * P], x,
                                                start=False, stop=True)
                            ins.then_inc(pr.filled.sem, 1)
                        if s == pr.lag + 2 and at.has(1):
                            pe.wait_ge(sums.sem, sums.at(at.back(1), 1))
                        if s == BLOCK + 3 and at.has(1):
                            pe.wait_ge(sums.sem, sums.at(at.back(1)))
                        if s >= pr.lag and not (through_v(s - pr.lag) or through_s(s - pr.lag)):
                            _, _, lhs, acc, r0, start = sources[s - pr.lag][1][0]
                            m = pr.first[s - pr.lag]
                            pe.wait_ge(pr.multiplied.sem, pr.multiplied.at(at, m + 1))
                            pe.matmul(acc[r0:r0 + lhs.shape[1], :], lhs, pr.tile(m)[:, :], start=start,
                                      stop=True, skip_group_check=True).then_inc(pr.contracted.sem, 1)
                        if s >= BLOCK and s % BLOCK == 3:
                            c = s // BLOCK - 1
                            for i, (_, _, lhs, acc, r0, start) in enumerate(through_sv[c][1]):
                                if i < 2:
                                    pe.wait_ge(pool_made.sem, pool_made.at(at, 5 * c + 4 + i))
                                else:
                                    pe.wait_ge(third_added.sem, third_added.at(at, c + 1))
                                pe.matmul(acc[r0:r0 + lhs.shape[1], :], lhs, FP[3 * (c % 2) + i][:, :], start=start,
                                          stop=True, skip_group_check=True).then_inc(pool_contracted.sem, 1)
                        if s == 7 and not at.first():
                            mix(at.back(1), at)
                        if s == 12 and not at.first():
                            sc.pe(pe, at.back(1))
                        if not at.last(n):
                            if s == 20:
                                if at.has(1):
                                    pe.wait_ge(sc.out_ready.sem, sc.out_ready.at(at.back(1)))
                                turn_d(at.next())
                            if s == 28:
                                message(at.next(), (0, 1, 2))
                            if s == 31:
                                message(at.next(), (3,))
                            if s == 36:
                                turn(at.next(), (0, 1))
                            if s == 39:
                                turn(at.next(), (2, 3))
                            if s == 46:
                                turn(at.next(), (4, 5))
                            if s == 53:
                                turn(at.next(), (6, 7))
                    if at.last(n):
                        if at.has(1):
                            pe.wait_ge(sc.out_ready.sem, sc.out_ready.at(at.back(1)))
                        mix(at, at)
                        sc.pe(pe, at)
                walk(pe, n, body)


def build_program(nc, d, n_nodes, n_edges, passes):
    with ExitStack() as ctx:
        core = Core(nc, ctx, d, n_nodes, n_edges)
        tiles = n_edges // P
        for name, dt, width in (("X1", F32, D), ("AGG", F32, AW), ("H", F32, D), ("X3", F32, D)):
            if name not in d:
                d[name] = nc.dram_tensor(f"table_{name}", [n_nodes, width], dt, kind="Internal").ap()
        core.cols = {e: sbuf(nc, ctx, f"cols_{e}", [P, tiles], I32) for e in ("src", "dst")}
        core.target = {e: sbuf(nc, ctx, f"target_{e}", [P, tiles], I32) for e in ("src", "dst")}
        off, width = offsets("ident")
        core.ident = sbuf(nc, ctx, "ident", [P, width])
        core.eye = core.ident[:, off["eye"]:off["eye"] + P]
        core.earlier = core.ident[:, off["earlier"]:off["earlier"] + P]
        core.spare = core.ident[:, off["spare"]:off["spare"] + 1]
        for one_pass in [load_tables] + passes:
            core.run(one_pass)


def pass_list():
    return [
        lambda c: plain_node_pass(c, "n0", "X", "X1", True),
        edges0,
        edges1,
        nodes1,
        edges2,
        lambda c: plain_node_pass(c, "n3", "X3", "OUT", False),
        edges3,
    ]


def halves(a):
    m = a.shape[1]
    return a.reshape(2, HALF, m).transpose(1, 0, 2).reshape(HALF, 2 * m)


def block_diagonal(ws, wv):
    out = np.zeros((D, D), np.float32)
    out[:S, :S] = ws
    for i in range(3):
        out[S + i::3, S + i::3] = wv
    return out


def pack_conv(name, fc1, fc2, l1_s, l1_v, l2_s, l2_v, alpha):
    first = np.zeros((P, P), np.float32)
    first[:fc1.shape[0], :fc1.shape[1]] = fc1
    w = fc2.reshape(fc2.shape[0], 192)
    second = np.zeros((P, 2, 96), np.float32)
    second[:w.shape[0], 0, :S], second[:w.shape[0], 0, S:] = w[:, 64:128], w[:, 128:160]
    second[:w.shape[0], 1, :S], second[:w.shape[0], 1, S:] = w[:, 0:64], w[:, 160:192]
    l1 = np.zeros((D, 3, 96), np.float32)
    for m in range(3):
        l1[:S, m, :S] = l1_s
        l1[S + m::3, m, S:] = l1_v
    l2 = np.zeros((96, 4, AW), np.float32)
    l2[:, 0, :S] = l2_s
    if alpha is not None:
        l2[:, 0, D] = alpha[:, 0]
    for m in range(3):
        l2[:, 1 + m, S + m:D:3] = l2_v
    g = np.zeros((P, 6, 96), np.float32)
    for r0 in (32, 64):
        for m in range(3):
            g[r0 + 1 + m, m, :S] = 1
            g[r0, m, S:] = 1
            g[r0 + 1 + m, 3 + m, S:] = 1
        g[r0, 3, :S] = 1
    return pack(name, fc1=first, fc2=second, l1=halves(l1.reshape(D, 288)), l2=l2, gather=g)


def host_arrays(i, n_nodes, n_edges):
    n, e = i["x"].shape[0], i["src"].shape[0]
    tiles = n_edges // P

    def rows(a, count):
        out = np.zeros((count,) + a.shape[1:], a.dtype)
        out[:a.shape[0]] = a
        return out

    d = {"X": rows(i["x"], n_nodes), "Z": rows(i["node_vec1"], n_nodes)}
    for end in ("src", "dst"):
        idx = np.full(n_edges, n_nodes - 1, np.int32)
        idx[:e] = i[end]
        d[f"{end}_rows"] = idx.reshape(1, -1)
        d[f"{end}_cols"] = np.ascontiguousarray(idx.reshape(tiles, P).T)
    across = lambda a: np.ascontiguousarray(rows(a, n_edges).T)
    d["ea32"] = across(i["edge_attr_32"])
    d["ea16"] = across(i["edge_attr_16"])
    d["ea12"] = across(i["edge_attr_12"])
    d["ea4"] = across(i["edge_attr_4"])
    d["ea4_cols"] = np.ascontiguousarray(rows(i["edge_attr_4"], n_edges).reshape(tiles, P, 4).transpose(1, 0, 2)
                                         .reshape(P, tiles * 4))

    q = np.arange(P)
    d["pack_ident"] = pack("ident", eye=np.eye(P), earlier=(q[None, :] < q[:, None]),
                           spare=(n + q)[:, None])

    g = lambda k: i["L0_gnn_" + k]
    W1, W2, W3, W4 = (g(f"W{k}") for k in (1, 2, 3, 4))
    w4 = np.zeros((3, V, 8, 3, V), np.float32)
    for k in range(3):
        w4[k, :, :, k, :] = W4
    wmT = g("Wm").T
    wm_v = np.concatenate([wmT[:, S:].reshape(D, V, 3).transpose(0, 2, 1).reshape(D, 96), g("bm")[:, None]], 1)
    sel = np.zeros((P, 26, P), np.float32)
    for r0 in (0, 32):
        for c in range(4):
            for j in range(2):
                sel[r0 + 2 * c + j, c, j * S:(j + 1) * S] = 1
        for b in range(8):
            for k in range(3):
                sel[r0 + 8 + 3 * b + k, 4 + b, k * V:(k + 1) * V] = 1
            sel[r0 + b, 12 + b, :96] = 1
        for k in range(3):
            for h in range(2):
                for b in range(4):
                    sel[r0 + 8 + 3 * (4 * h + b) + k, 20 + 2 * k + h, b * V:(b + 1) * V] = 1
    d["pack_e0"] = pack(
        "e0", w1=W1.reshape(S, 4, 2, S).transpose(2, 0, 1, 3), w2=np.tile(W2.reshape(V, 8 * S), (3, 1)),
        w4=w4, w3=np.tile(W3.reshape(S, 8 * V), (2, 1)), wm_s=halves(np.tile(wmT[:, :S], (1, 2))),
        wm_v=halves(wm_v), wu=halves(g("Wu")[D:]), gather=sel, sum=np.tile(np.eye(V), (4, 1)))
    lin = np.zeros((97, 2 * D), np.float32)
    lin[:HALF] = halves(g("Wu")[:D])
    lin[96, D:] = g("bu")
    d["pack_n0"] = pack("n0", lin=lin)

    g = lambda k: i["L1_gnn_" + k]
    d["pack_e1"] = pack_conv("e1", g("Wfc1"), g("Wfc2"), g("Wl1_0"), g("Wl1_1"), g("Wl2_s"), g("Wl2_v"), g("Wa"))
    h = lambda k: i["L2_gnn_" + k]
    d["pack_e2"] = pack_conv("e2", h("W_fc1"), h("W_fc2"), h("W_l1_0"), h("W_l1_1"), h("W_l2_0"), h("W_l2_1"), None)
    d["pack_n1"] = pack("n1", sc=halves(block_diagonal(g("Wsc0"), g("Wsc1"))),
                        sc2=halves(block_diagonal(h("W_sc0"), h("W_sc1"))))

    g = lambda k: i["L3_gnn_" + k]
    d["pack_n3"] = pack("n3", lin=halves(block_diagonal(g("Lu_s"), g("Lu_v"))))
    y = np.zeros((192, 2 * D + V), np.float32)
    y[:D, 0:D] = block_diagonal(g("Lm_s"), g("Lm_v"))
    y[:D, D:2 * D] = block_diagonal(g("Wm_ss"), g("Wm_vs"))
    y[:S, 2 * D:] = g("Wm_sv")
    y[D:, 0:S] = g("Wm_vv")
    pick_s = np.zeros((P, 32, 2, S), np.float32)
    for c in range(32):
        for j in range(2):
            for r0 in (0, 64):
                pick_s[r0 + 2 * c + j, c, j, :] = 1
    pick_v = np.zeros((P, 8, 4, V), np.float32)
    total = np.zeros((P, 8, V), np.float32)
    for c in range(8):
        for j in range(4):
            for r0 in (0, 32):
                pick_v[r0 + 4 * c + j, c, j, :] = 1
            total[j * V:(j + 1) * V, c, 4 * c + j] = 1
    out_v = np.zeros((3, V, D), np.float32)
    for k in range(3):
        out_v[k, np.arange(V), S + 3 * np.arange(V) + k] = 1
    d["pack_e3"] = pack(
        "e3", y=y.reshape(2, 96, 2 * D + V).transpose(1, 0, 2), ss=g("Wu_ss").reshape(32, 2, S, S).transpose(1, 2, 0, 3),
        vv=g("Wu_vv").reshape(8, 4, V, S).transpose(1, 2, 0, 3),
        sv=np.tile(g("Wu_sv").reshape(S, V, 8, 4).transpose(0, 2, 3, 1).reshape(S, 8 * P), (2, 1)),
        vs=np.tile(g("Wu_vs").reshape(V, S, 8, 4).transpose(1, 2, 3, 0).reshape(S, 8 * P), (2, 1)),
        pick_s=pick_s, pick_v=pick_v, sum=total,
        out_s=np.tile(np.eye(S, D), (2, 1)), out_v=out_v)
    return d


def kernel(**inputs):
    import concourse.bacc as bacc
    from concourse.bass_utils import run_bass_kernel_spmd

    inputs = {k: np.asarray(v) for k, v in inputs.items()}
    n, e = inputs["x"].shape[0], inputs["src"].shape[0]
    n_nodes, n_edges = -(-(n + P) // (2 * GR)) * 2 * GR, -(-e // GR) * GR
    arrays = host_arrays(inputs, n_nodes, n_edges)
    nc = bacc.Bacc("TRN2", target_bir_lowering=False, num_devices=1)
    d = {k: nc.dram_tensor(f"in_{k}", a.shape, mybir.dt.from_np(a.dtype), kind="ExternalInput").ap()
         for k, a in arrays.items()}
    d["OUT"] = nc.dram_tensor("out_x", [n_nodes, D], F32, kind="ExternalOutput").ap()
    build_program(nc, d, n_nodes, n_edges, pass_list())
    result = run_bass_kernel_spmd(nc, [{f"in_{k}": a for k, a in arrays.items()}], core_ids=[0])
    return result.results[0]["out_x"][:n]
```
